# Optimizing a Trainium2 kernel written in Bass

```python
import numpy as np
import jax
import jax.numpy as jnp

def _softmax(x, axis=-1):
    return jax.nn.softmax(x, axis=axis)

def _gelu(x):
    return jax.nn.gelu(x, approximate=True)

def _silu(x):
    return jax.nn.silu(x)

def _sigmoid(x):
    return jax.nn.sigmoid(x)

def _layernorm(x, axis=-1, eps=1e-05):
    m = jnp.mean(x, axis=axis, keepdims=True)
    v = jnp.var(x, axis=axis, keepdims=True)
    return (x - m) / jnp.sqrt(v + eps)

def _scatter_add(tgt, idx, src, axis=0):
    return tgt.at[idx].add(src)

def _segment_sum(src, seg, n):
    return jax.ops.segment_sum(src, seg, n)
kernel_name = 'mk_flamingo_gated_d2_seqx_r8_8c9579'

def setup_inputs(seed: int=0):
    np.random.seed(seed)
    _w = jnp.asarray

    def _rec_inputs():
        import jax
        import jax.numpy as jnp
        _rk = jax.random.key(seed)
        x = -0.000125 + 0.9999 * jax.random.normal(jax.random.fold_in(_rk, 1), (32, 100, 256), jnp.float32)
        _lenS = 100 - jax.random.randint(jax.random.fold_in(_rk, 7), (32,), 0, max(1, 100 // 4) + 1, jnp.int32)
        _lenS2 = 1444 - jax.random.randint(jax.random.fold_in(_rk, 8), (32,), 0, max(1, 1444 // 4) + 1, jnp.int32)
        _ctx_2048P = jax.random.normal(jax.random.fold_in(_rk, 11), (32, 16, 256), jnp.float32)
        _ctx_2048c = jax.random.dirichlet(jax.random.fold_in(_rk, 511), 0.3 * jnp.ones((16,), jnp.float32), (32, 1444))
        _ctx_2048t = jnp.einsum('bsk,bkd->bsd', _ctx_2048c, _ctx_2048P)
        _ctx_2048t = _ctx_2048t * jax.lax.rsqrt(jnp.mean(jnp.square(_ctx_2048t)) + 1e-12) * 0.953939
        ctx_2048 = -0.000514642 + 1.00011 * (_ctx_2048t + 0.3 * jax.random.normal(jax.random.fold_in(_rk, 611), (32, 1444, 256), jnp.float32))
        _validS = jnp.arange(100)[None, :] < _lenS[:, None]
        _validS2 = jnp.arange(1444)[None, :] < _lenS2[:, None]
        _causal = jnp.tril(jnp.ones((100, 100), dtype=bool))
        mask_BxS2_bk0 = jnp.logical_not(jnp.broadcast_to(_validS2[:, :], (32, 1444)))
        _g = jax.random.normal(jax.random.fold_in(_rk, 9001), (2, 2), jnp.float32)
        _g = jnp.sign(_g) * jnp.maximum(jnp.abs(_g), 1.0) + (_g == 0) * 1.0
        g_xattn = _g[0]
        g_ffn = _g[1]
        return (x, ctx_2048, mask_BxS2_bk0, g_xattn, g_ffn)
    x, ctx_2048, mask_BxS2_bk0, g_xattn, g_ffn = _rec_inputs()

    def _L0_xattn_setup():
        import jax, jax.numpy as jnp
        import numpy as np
        key = jax.random.key(seed)
        k1, k2, k3 = jax.random.split(key, 3)
        B, S, D, M = (8, 256, 256, 128)
        hidden_states = jax.random.normal(k1, (B, S, D), dtype=jnp.float32)
        memory_tokens = jax.random.normal(k2, (B, M, D), dtype=jnp.float32)
        memory_mask = jax.random.randint(k3, (B, M), 0, 2).astype(jnp.bool_)
        return {'hidden_states': hidden_states, 'memory_tokens': memory_tokens, 'memory_mask': memory_mask}
    _L0_xattn_all = _L0_xattn_setup()
    _L0_xattn_in = {k: v for k, v in _L0_xattn_all.items() if k in ()}
    del _L0_xattn_all

    def _L0_ffn_setup():
        import jax, jax.numpy as jnp
        import numpy as np
        B, S, H = (4, 128, 256)
        E, K, I, SI = (16, 4, 176, 704)

        def _silu_mul(gu, inter):
            return jax.nn.silu(gu[:, :inter]) * gu[:, inter:]
        key = jax.random.key(seed)
        ks = jax.random.split(key, 7)
        s = 0.02
        return {'hidden_states': jax.random.normal(ks[0], (B, S, H), jnp.float32), 'gate_w': jax.random.normal(ks[1], (E, H), jnp.float32) * s, 'expert_gate_up': jax.random.normal(ks[2], (E, 2 * I, H), jnp.float32) * s, 'expert_down': jax.random.normal(ks[3], (E, H, I), jnp.float32) * s, 'shared_gate_up': jax.random.normal(ks[4], (2 * SI, H), jnp.float32) * s, 'shared_down': jax.random.normal(ks[5], (H, SI), jnp.float32) * s, 'shared_gate_vec': jax.random.normal(ks[6], (1, H), jnp.float32) * s}
    _L0_ffn_all = _L0_ffn_setup()
    _L0_ffn_in = {k: v for k, v in _L0_ffn_all.items() if k in ('gate_w', 'expert_gate_up', 'expert_down', 'shared_gate_up', 'shared_down', 'shared_gate_vec')}
    del _L0_ffn_all

    def _L1_xattn_setup():
        import jax, jax.numpy as jnp
        import numpy as np
        key = jax.random.key(seed)
        k = jax.random.split(key, 6)
        B, S, D, NKV = (4, 512, 256, 64)
        inv = D ** (-0.5)
        return {'x': jax.random.normal(k[0], (B, S, D), jnp.float32), 'W_qkv': jax.random.normal(k[1], (3 * D, D), jnp.float32) * inv, 'W_o': jax.random.normal(k[2], (D, D), jnp.float32) * inv, 'beta_q': jnp.array(1.0, jnp.float32), 'beta_k': jnp.array(1.0, jnp.float32), 'gate': jnp.array(0.0, jnp.float32), 'log_tau': jnp.array(0.0, jnp.float32), 'K_mem': jax.random.normal(k[3], (B, NKV, D), jnp.float32), 'V_mem': jax.random.normal(k[4], (B, NKV, D), jnp.float32), 'clip_k': 54}
    _L1_xattn_all = _L1_xattn_setup()
    _L1_xattn_in = {k: v for k, v in _L1_xattn_all.items() if k in ('W_qkv', 'W_o', 'beta_q', 'beta_k', 'gate', 'log_tau')}
    del _L1_xattn_all

    def _L1_ffn_setup():
        import jax, jax.numpy as jnp
        import numpy as np
        D_MODEL = 256
        D_EXPERT = 1024
        EPS = 1e-08

        def ternary_quant(w):
            scale = jnp.mean(jnp.abs(w)) + EPS
            q = jnp.clip(jnp.round(w / scale), -1.0, 1.0) * scale
            return w + jax.lax.stop_gradient(q - w)
        key = jax.random.key(seed)
        k_x, k_up, k_gate, k_down = jax.random.split(key, 4)
        std_in = 1.0 / np.sqrt(D_MODEL)
        std_exp = 1.0 / np.sqrt(D_EXPERT)
        return {'x': jax.random.normal(k_x, (4, 256, D_MODEL), dtype=jnp.float32), 'W_up': jax.random.normal(k_up, (D_EXPERT, D_MODEL), dtype=jnp.float32) * std_in, 'W_gate': jax.random.normal(k_gate, (D_EXPERT, D_MODEL), dtype=jnp.float32) * std_in, 'W_down': jax.random.normal(k_down, (D_MODEL, D_EXPERT), dtype=jnp.float32) * std_exp}
    _L1_ffn_all = _L1_ffn_setup()
    _L1_ffn_in = {k: v for k, v in _L1_ffn_all.items() if k in ('W_up', 'W_gate', 'W_down')}
    del _L1_ffn_all
    return {'x': x, 'ctx_2048': ctx_2048, 'mask_BxS2_bk0': mask_BxS2_bk0, 'g_xattn': g_xattn, 'g_ffn': g_ffn, 'L0_ffn_gate_w': _L0_ffn_in['gate_w'], 'L0_ffn_expert_gate_up': _L0_ffn_in['expert_gate_up'], 'L0_ffn_expert_down': _L0_ffn_in['expert_down'], 'L0_ffn_shared_gate_up': _L0_ffn_in['shared_gate_up'], 'L0_ffn_shared_down': _L0_ffn_in['shared_down'], 'L0_ffn_shared_gate_vec': _L0_ffn_in['shared_gate_vec'], 'L1_xattn_W_qkv': _L1_xattn_in['W_qkv'], 'L1_xattn_W_o': _L1_xattn_in['W_o'], 'L1_xattn_beta_q': _L1_xattn_in['beta_q'], 'L1_xattn_beta_k': _L1_xattn_in['beta_k'], 'L1_xattn_gate': _L1_xattn_in['gate'], 'L1_xattn_log_tau': _L1_xattn_in['log_tau'], 'L1_ffn_W_up': _L1_ffn_in['W_up'], 'L1_ffn_W_gate': _L1_ffn_in['W_gate'], 'L1_ffn_W_down': _L1_ffn_in['W_down']}

def reference(x, ctx_2048, mask_BxS2_bk0, g_xattn, g_ffn, L0_ffn_gate_w, L0_ffn_expert_gate_up, L0_ffn_expert_down, L0_ffn_shared_gate_up, L0_ffn_shared_down, L0_ffn_shared_gate_vec, L1_xattn_W_qkv, L1_xattn_W_o, L1_xattn_beta_q, L1_xattn_beta_k, L1_xattn_gate, L1_xattn_log_tau, L1_ffn_W_up, L1_ffn_W_gate, L1_ffn_W_down):
    import jax
    import jax.numpy as jnp

    def _L0_xattn_ref(hidden_states, memory_tokens, memory_mask):
        import jax, jax.numpy as jnp
        import numpy as np
        B, S, D = hidden_states.shape
        scale = 1.0 / jnp.sqrt(jnp.asarray(D, hidden_states.dtype))
        scores = jnp.einsum('bsd,bmd->bsm', hidden_states, memory_tokens) * scale
        neg_inf = jnp.asarray(-1e+30, scores.dtype)
        scores = jnp.where(memory_mask[:, None, :], scores, neg_inf)
        attn = jax.nn.softmax(scores, axis=-1)
        readout = jnp.einsum('bsm,bmd->bsd', attn, memory_tokens)
        valid_b = jnp.any(memory_mask, axis=-1)
        out = jnp.where(valid_b[:, None, None], readout, jnp.zeros_like(readout))
        return out

    def _L0_ffn_ref(hidden_states, gate_w, expert_gate_up, expert_down, shared_gate_up, shared_down, shared_gate_vec):
        import jax, jax.numpy as jnp
        import numpy as np
        B, S, H = (4, 128, 256)
        E, K, I, SI = (16, 4, 176, 704)

        def _silu_mul(gu, inter):
            return jax.nn.silu(gu[:, :inter]) * gu[:, inter:]
        orig_shape = hidden_states.shape
        x = hidden_states.reshape(-1, H)
        router_logits = x @ gate_w.T
        routing_probs = jax.nn.softmax(router_logits.astype(jnp.float32), axis=-1)
        topk_w, topk_idx = jax.lax.top_k(routing_probs, K)
        topk_w = topk_w / topk_w.sum(axis=-1, keepdims=True)
        topk_w = topk_w.astype(x.dtype)
        combine = (jax.nn.one_hot(topk_idx, E, dtype=x.dtype) * topk_w[..., None]).sum(1)
        shared = _silu_mul(x @ shared_gate_up.T, SI) @ shared_down.T
        shared = shared * jax.nn.sigmoid(x @ shared_gate_vec.T)

        def step(acc, ew):
            w_gu, w_d, cw = ew
            h = _silu_mul(x @ w_gu.T, I)
            return (acc + h @ w_d.T * cw[:, None], None)
        acc0 = jnp.zeros_like(x)
        sparse, _ = jax.lax.scan(step, acc0, (expert_gate_up, expert_down, combine.T))
        return (shared + sparse).reshape(orig_shape)

    def _L1_xattn_ref(x, W_qkv, W_o, beta_q, beta_k, gate, log_tau, K_mem, V_mem, clip_k):
        import jax, jax.numpy as jnp
        import numpy as np
        D = x.shape[-1]
        scale = D ** (-0.5)
        qkv = x @ W_qkv.T
        Q = qkv[..., :D]
        alpha = jax.nn.sigmoid(gate)
        tau = jnp.exp(log_tau)
        coef = (alpha * beta_q + (1.0 - alpha) * beta_k) * scale * tau
        scores = coef * jnp.einsum('bsd,bnd->bsn', Q, K_mem)
        scores = scores - jnp.max(scores, axis=-1, keepdims=True)
        thr = jax.lax.top_k(scores, clip_k)[0][..., -1:]
        scores = jnp.where(scores < thr, -jnp.inf, scores)
        att = jax.nn.softmax(scores, axis=-1)
        out = jnp.einsum('bsn,bnd->bsd', att, V_mem)
        return out @ W_o.T

    def _L1_ffn_ref(x, W_up, W_gate, W_down):
        import jax, jax.numpy as jnp
        import numpy as np
        D_MODEL = 256
        D_EXPERT = 1024
        EPS = 1e-08

        def ternary_quant(w):
            scale = jnp.mean(jnp.abs(w)) + EPS
            q = jnp.clip(jnp.round(w / scale), -1.0, 1.0) * scale
            return w + jax.lax.stop_gradient(q - w)
        wu = ternary_quant(W_up)
        wg = ternary_quant(W_gate)
        wd = ternary_quant(W_down)
        up = jnp.einsum('bsd,ed->bse', x, wu)
        gate = jnp.einsum('bsd,ed->bse', x, wg)
        hidden = jax.nn.silu(up) * gate
        return jnp.einsum('bse,de->bsd', hidden, wd)
    x = x + jnp.tanh(g_xattn[0]) * _L0_xattn_ref(_layernorm(x, axis=-1), ctx_2048, mask_BxS2_bk0)
    x = x + jnp.tanh(g_ffn[0]) * _L0_ffn_ref(_layernorm(x, axis=-1), L0_ffn_gate_w, L0_ffn_expert_gate_up, L0_ffn_expert_down, L0_ffn_shared_gate_up, L0_ffn_shared_down, L0_ffn_shared_gate_vec)
    x = x + jnp.tanh(g_xattn[1]) * _L1_xattn_ref(_layernorm(x, axis=-1), L1_xattn_W_qkv, L1_xattn_W_o, L1_xattn_beta_q, L1_xattn_beta_k, L1_xattn_gate, L1_xattn_log_tau, ctx_2048, ctx_2048, 54)
    x = x + jnp.tanh(g_ffn[1]) * _L1_ffn_ref(_layernorm(x, axis=-1), L1_ffn_W_up, L1_ffn_W_gate, L1_ffn_W_down)
    return x

_drawn_inputs = setup_inputs


def setup_inputs(seed=0):
    import zlib

    import numpy as np

    out = dict(_drawn_inputs(seed))
    spreads = {'g_ffn': (-1.0, 0.6)}
    factors = {'L0_ffn_gate_w': 8.0,
     'L0_ffn_expert_gate_up': 8.0,
     'L0_ffn_expert_down': 8.0,
     'L0_ffn_shared_gate_up': 4.911,
     'L0_ffn_shared_down': 4.887,
     'L0_ffn_shared_gate_vec': 8.0}
    for name, (base, spread) in spreads.items():
        noise = np.random.default_rng([zlib.crc32(name.encode()), seed]).standard_normal(out[name].shape)
        drawn = base * np.exp(spread * noise) if base else spread * noise
        out[name] = jnp.asarray(drawn.astype(out[name].dtype))
    for name, factor in factors.items():
        out[name] = (out[name] * factor).astype(out[name].dtype)
    return out
```

```python
from contextlib import ExitStack

import concourse.bass as bass
from concourse import mybir

ALU = mybir.AluOpType
ACT = mybir.ActivationFunctionType
AX = mybir.AxisListType
F32 = mybir.dt.float32
F32R = mybir.dt.float32r
BF16 = mybir.dt.bfloat16
U8 = mybir.dt.uint8
U32 = mybir.dt.uint32

P = 128
NEG = -1.0e30
LOWEST = -3.0e38
LN_EPS = 1e-5
TERNARY_EPS = 1e-8
CLIP_K = 54
TOP_EXPERTS = 4
RING_PREP = 7


def flamingo_kernel(nc, x, ctx_mem, mask, g_xattn, g_ffn, gate_w, expert_gate_up, expert_down,
                    shared_gate_up, shared_down, shared_gate_vec, W_qkv, W_o, beta_q, beta_k, gate,
                    log_tau, W_up, W_gate, W_down, out):
    B, S, D = x.shape
    M = ctx_mem.shape[1]
    KD = D // P
    MC = -(-M // P)
    MT = M - (MC - 1) * P
    MPAD = MC * P
    SB = -(-M // 3)
    SB += SB % 2
    SCOLS = [(0, SB), (SB, SB), (2 * SB, M - 2 * SB)]
    E = gate_w.shape[0]
    EI = expert_down.shape[2]
    SI = shared_down.shape[1]
    FI = W_up.shape[0]
    GB = 4
    NG = B // GB
    GT = GB * S

    mask_bias_dram = nc.dram_tensor("mask_bias", (B, M), BF16, kind="Internal").ap()

    with ExitStack() as whole:
        def sem(name):
            return whole.enter_context(nc.semaphore(name))

        def keep(name, shape, dt=F32):
            return whole.enter_context(nc.sbuf_tensor(name, shape, dt))

        XN = keep("XN", [P, B, D])
        MV = keep("MV", [P, B, 2])
        RSTD = keep("RSTD", [P, B])
        VEPS = keep("VEPS", [P, B])
        MHALF = keep("MHALF", [P, B])
        ident = keep("ident", [P, P])
        ones = keep("ones", [P, P])
        gains = keep("gains", [P, 4])
        valid_gain = keep("valid_gain", [P, B])
        coef = keep("coef", [P, 1])
        CWN = keep("CWN", [P, B, E])
        SIGN = keep("SIGN", [P, B])

        def setup():
            with ExitStack() as ctx:
                def sb(name, shape, dt=F32):
                    return ctx.enter_context(nc.sbuf_tensor(name, shape, dt))
                mask_u8 = sb("mask_u8", [B, M], U8)
                mask_bias = sb("mask_bias_sb", [B, M], BF16)
                any_valid = sb("any_valid", [B, 1])
                any_wide = sb("any_wide", [B, P])
                g_raw = sb("g_raw", [P, 4])
                sc = sb("sc", [P, 16])
                stats = sb("stats", [P, B, 6])
                pv = ctx.enter_context(nc.psum_tensor("pv_valid", [P, B], F32))
                x_in, small_in, mask_in = sem("x_in"), sem("small_in"), sem("mask_in")
                consts, v_step, a_step = sem("consts"), sem("setup_v"), sem("setup_a")
                wide_t, bias_out, stat_done = sem("wide_t"), sem("bias_out"), sem("stat_done")
                blk = ctx.enter_context(nc.Block())

                @blk.sync
                def _(sp):
                    sp.dma_start(mask_u8[:], mask).then_inc(mask_in, 16)
                    sp.dma_start(g_raw[:, 0:2], g_xattn.rearrange("(a n) -> a n", a=1).partition_broadcast(P)
                                 if False else bass_bcast(g_xattn, 2)).then_inc(small_in, 16)
                    sp.dma_start(g_raw[:, 2:4], bass_bcast(g_ffn, 2)).then_inc(small_in, 16)
                    for n, t in enumerate((gate, beta_q, beta_k, log_tau)):
                        sp.dma_start(sc[:, n:n + 1], bass_bcast(t, 1)).then_inc(small_in, 16)
                    for n in range(4):
                        q = B // 4
                        sp.dma_start(XN[0:S, n * q:(n + 1) * q, :],
                                     x[n * q:(n + 1) * q].rearrange("b s d -> s b d")).then_inc(x_in, 16)
                    sp.wait_ge(v_step, 1)
                    sp.dma_start(mask_bias_dram, mask_bias[:]).then_inc(bias_out, 16)
                    sp.wait_ge(bias_out, 16)

                @blk.gpsimd
                def _(pool):
                    pool.memset(ident[:], 0.0).then_inc(consts, 1)
                    pool.memset(ones[:], 1.0).then_inc(consts, 1)
                    pool.memset(MHALF[:], -0.5).then_inc(consts, 1)
                    pool.wait_ge(consts, 3)
                    pool.affine_select(out=ident[:], in_=ident[:], compare_op=ALU.not_equal, fill=1.0, base=0,
                                       pattern=[[-1, P]], channel_multiplier=1).then_inc(consts, 1)

                @blk.scalar
                def _(act):
                    act.wait_ge(small_in, 96)
                    act.activation(gains[:], g_raw[:], ACT.Tanh).then_inc(a_step, 1)
                    act.activation(sc[:, 4:5], sc[:, 0:1], ACT.Exp, scale=-1.0).then_inc(a_step, 1)
                    act.activation(sc[:, 5:6], sc[:, 3:4], ACT.Exp).then_inc(a_step, 1)

                @blk.tensor
                def _(pe):
                    pe.wait_ge(consts, 4)
                    pe.wait_ge(v_step, 3)
                    pe.transpose(pv[:, :], any_wide[:], ident[0:B, 0:B]).then_inc(wide_t, 1)

                @blk.vector
                def _(dve):
                    n = 0

                    def chain(ins):
                        nonlocal n
                        n += 1
                        ins.then_inc(v_step, 1)
                        dve.wait_ge(v_step, n)
                    dve.wait_ge(mask_in, 16)
                    chain(dve.tensor_scalar(mask_bias[:], mask_u8[:], 1.0, -NEG, ALU.subtract, ALU.mult))
                    chain(dve.tensor_reduce(any_valid[:], mask_u8[:], AX.X, ALU.max))
                    dve.wait_ge(consts, 4)
                    chain(dve.tensor_scalar(any_wide[:], ones[0:B, :], any_valid[:, 0:1], None, ALU.mult))
                    dve.wait_ge(a_step, 3)
                    chain(dve.tensor_scalar(sc[:, 6:7], sc[:, 4:5], 1.0, None, ALU.add))
                    chain(dve.reciprocal(sc[:, 7:8], sc[:, 6:7]))
                    chain(dve.tensor_tensor(sc[:, 8:9], sc[:, 7:8], sc[:, 1:2], ALU.mult))
                    chain(dve.tensor_scalar(sc[:, 9:10], sc[:, 7:8], -1.0, 1.0, ALU.mult, ALU.add))
                    chain(dve.tensor_tensor(sc[:, 10:11], sc[:, 9:10], sc[:, 2:3], ALU.mult))
                    chain(dve.tensor_tensor(sc[:, 11:12], sc[:, 8:9], sc[:, 10:11], ALU.add))
                    chain(dve.tensor_scalar(coef[:], sc[:, 11:12], float(D) ** -0.5, sc[:, 5:6], ALU.mult, ALU.mult))
                    dve.wait_ge(wide_t, 1)
                    chain(dve.tensor_scalar(valid_gain[:], pv[:], gains[:, 0:1], None, ALU.mult))
                    for q in range(4):
                        dve.wait_ge(x_in, 64)
                        for b in range(q * B // 4, (q + 1) * B // 4):
                            last = dve.bn_stats(stats[0:S, b, :], XN[0:S, b, :])
                    last.then_inc(stat_done, 1)
                    dve.wait_ge(stat_done, 1)
                    for b in range(B):
                        dve.bn_aggr(MV[0:S, b, :], stats[0:S, b, :])

        def bass_bcast(t, n):
            return t.partition_broadcast(P)

        def attention(layer):
            L = f"a{layer}_"
            clipped = layer == 1
            R = RING_PREP + 3 + clipped
            with ExitStack() as ctx:
                def sb(name, shape, dt=F32):
                    return ctx.enter_context(nc.sbuf_tensor(L + name, shape, dt))

                def bank(name):
                    return ctx.enter_context(nc.psum_tensor(L + name, [P, 512], F32))
                CR = [sb(f"CR{p}", [P, MC, D]) for p in range(2)]
                NH = [sb(f"NH{p}", [P, MC, D], F32R) for p in range(2)]
                NL = [sb(f"NL{p}", [P, MC, D], F32R) for p in range(2)]
                TH, TL = sb("TH", [P, KD, MPAD], F32R), sb("TL", [P, KD, MPAD], F32R)
                QH, QL = sb("QH", [P, KD, S], F32R), sb("QL", [P, KD, S], F32R)
                XHAT = sb("XHAT", [P, D])
                SC = [sb(f"SC{p}", [P, M]) for p in range(2)]
                PR = sb("PR", [P, MPAD])
                PTH, PTL = sb("PTH", [P, MC, S], F32R), sb("PTL", [P, MC, S], F32R)
                small = [sb(f"small{p}", [P, 8]) for p in range(2)]
                bn = sb("bn", [P, 8])
                XNEW = sb("XNEW", [P, D])
                if clipped:
                    top = sb("top", [P, 56])
                    WORK = sb("WORK", [P, M])
                    EXPS = sb("EXPS", [P, M])
                    XTH, XTL = sb("XTH", [P, KD, S], F32R), sb("XTL", [P, KD, S], F32R)
                    ATT = sb("ATT", [P, D])
                    ATH, ATL = sb("ATH", [P, KD, S], F32R), sb("ATL", [P, KD, S], F32R)
                    wraw = sb("wraw", [P, 2, KD, D])
                    WH, WL = sb("WH", [P, 2, KD, D], F32R), sb("WL", [P, 2, KD, D], F32R)
                else:
                    BIAS = [sb(f"BIAS{p}", [P, M], BF16) for p in range(2)]
                    row0 = sb("row0", [P, S], BF16)
                ring = [bank("ring0"), bank("ring1")]
                SP = [bank(f"S{n}") for n in range(3)]
                OB, QB, PB = bank("O"), bank("Q"), bank("proj")

                ctx_in = [sem(L + "ctx_in0"), sem(L + "ctx_in1")]
                names = ("init", "rstd", "xhat", "ring_full", "ring_high", "ring_low", "scores_full", "scores_copied",
                         "neg_max", "exps", "probs", "softmax_read", "nat_high", "nat_low", "pv_done", "out_read",
                         "chain", "q_full", "q_high", "q_low", "proj_full", "updated", "w_in", "w_full",
                         "w_high", "w_low", "eps_done", "sink")
                unused = () if clipped else ("probs", "q_full", "q_high", "q_low", "proj_full", "updated", "w_in",
                                             "w_full", "w_high", "w_low")
                (init, rstd_done, xhat, ring_full, ring_high, ring_low, scores_full, scores_copied, neg_max, exps,
                 probs, softmax_read, nat_high, nat_low, pv_done, out_read, chain, q_full, q_high, q_low,
                 proj_full, updated, w_in, w_full, w_high, w_low, eps_done, sink) = (
                    None if n in unused else sem(L + n) for n in names)
                blk = ctx.enter_context(nc.Block())
                LOADS = 32 if clipped else 48

                def at_step(t, n):
                    return n if isinstance(t, int) and t < 0 else RING_PREP + R * t + n

                def steps(eng, step):
                    step(0, 0)
                    step(1, 1)
                    with eng.Fori(1, B // 2 - 1) as j:
                        for u in range(2):
                            step(2 * j + u, u)
                    step(B - 2, 0)
                    step(B - 1, 1)

                def is_last(t):
                    return isinstance(t, int) and t == B - 1

                @blk.sync
                def _(sp):
                    if clipped:
                        sp.dma_start(wraw[:, 0, :, :], W_qkv[0:D, :].rearrange("(c p) d -> p c d", p=P)).then_inc(w_in, 16)
                        sp.dma_start(wraw[:, 1, :, :], W_o.rearrange("(c p) d -> p c d", p=P)).then_inc(w_in, 16)
                    sp.wait_ge(init, 2 if clipped else 5)

                    def load(b, p, reused):
                        if reused:
                            sp.wait_ge(nat_low, b - 1)
                            sp.sem_inc(sink, 1)
                        sp.dma_start(CR[p][:, 0:MC - 1, :],
                                     dyn(ctx_mem, b)[0:(MC - 1) * P, :].rearrange("(c p) d -> p c d", p=P)).then_inc(ctx_in[p], 16)
                        sp.dma_start(CR[p][0:MT, MC - 1, :], dyn(ctx_mem, b)[(MC - 1) * P:M, :]).then_inc(ctx_in[p], 16)
                        if not clipped:
                            sp.dma_start(BIAS[p][0:1, :], dynrow(mask_bias_dram, b)).then_inc(ctx_in[p], 16)
                    load(0, 0, False)
                    load(1, 1, False)
                    load(2, 0, True)
                    with sp.Fori(0, (B - 4) // 2) as j:
                        for u in range(2):
                            load(2 * j + 3 + u, (u + 1) % 2, True)
                    load(B - 1, 1, True)

                @blk.gpsimd
                def _(pool):
                    pool.memset(CR[0][:, MC - 1, :], 0.0).then_inc(init, 1)
                    pool.memset(CR[1][:, MC - 1, :], 0.0).then_inc(init, 1)
                    if not clipped:
                        pool.memset(BIAS[0][:], 0.0).then_inc(init, 1)
                        pool.memset(BIAS[1][:], 0.0).then_inc(init, 1)
                        pool.memset(row0[:], 0.0).then_inc(init, 1)
                        pool.wait_ge(init, 5)
                        pool.memset(row0[0:1, :], 1.0).then_inc(init, 1)
                    pool.memset(PR[:], 0.0).then_inc(init, 1)
                    pool.wait_ge(eps_done, 1)
                    pool.tensor_tensor(RSTD[0:S, :], VEPS[0:S, :], MHALF[0:S, :], ALU.pow).then_inc(rstd_done, 1)

                    def split(b, p, count):
                        pool.wait_ge(ctx_in[p], count)
                        pool.wait_ge(scores_full, b + 1)
                        pool.wait_ge(nat_high, b + 1)
                        pool.tensor_tensor(NL[p][:], CR[p][:], NH[p][:].bitcast(F32), ALU.subtract).then_inc(nat_low, 1)
                    split(0, 0, LOADS)
                    split(1, 1, LOADS)
                    with pool.Fori(1, B // 2) as j:
                        for u in range(2):
                            split(2 * j + u, u, LOADS * j + LOADS)

                @blk.tensor
                def _(pe):
                    def group(r, n, put):
                        if not (isinstance(r, int) and r < 2):
                            pe.wait_ge(ring_low, r - 1 if n >= 2 else r)
                        put(ring[n % 2]).then_inc(ring_full, 1)

                    def prep(b, p, t):
                        pe.wait_ge(xhat, b + 1)

                        def queries(out):
                            for k in range(KD):
                                last = pe.transpose(out[:, k * S:(k + 1) * S], XHAT[0:S, k * P:(k + 1) * P], ident[0:S, 0:S])
                            return last
                        group(at_step(t, 0), 0, queries)
                        pe.wait_ge(ctx_in[p], LOADS * half(b, p) + LOADS)
                        for n in range(6):
                            k, c0 = n // 3, 4 * (n % 3)

                            def context(out, k=k, c0=c0):
                                for c in range(4):
                                    last = pe.transpose(out[:, c * P:(c + 1) * P], CR[p][:, c0 + c, k * P:(k + 1) * P], ident[:])
                                return last
                            group(at_step(t, 1 + n), 1 + n, context)
                            if n == 1 and clipped:
                                pe.wait_ge(ring_low, at_step(t, 1))
                                for m in range(KD):
                                    first = True
                                    for k2 in range(KD):
                                        for w, xx in ((WH, XTH), (WH, XTL), (WL, XTH)):
                                            last = pe.matmul(QB[:, m * S:(m + 1) * S], w[:, 0, k2, m * P:(m + 1) * P], xx[:, k2, :],
                                                             start=first, stop=k2 == KD - 1 and w is WL)
                                            first = False
                                last.then_inc(q_full, 1)

                    def scores(b, p, t):
                        pe.wait_ge(ring_low, at_step(t, RING_PREP))
                        if clipped:
                            pe.wait_ge(q_low, b + 1)
                        pe.wait_ge(scores_copied, b)
                        for n, (c0, w) in enumerate(SCOLS):
                            first = True
                            for k in range(KD):
                                for q, m in ((QH, TH), (QH, TL), (QL, TH)):
                                    last = pe.matmul(SP[n][0:S, 0:w], q[:, k, :], m[:, k, c0:c0 + w], start=first,
                                                     stop=clipped and k == KD - 1 and q is QL)
                                    first = False
                            if not clipped:
                                last = pe.matmul(SP[n][0:S, 0:w], row0[:], BIAS[p][:, c0:c0 + w], start=False, stop=True)
                        last.then_inc(scores_full, 1)

                    def step(t, u):
                        n0 = 0
                        if not is_last(t):
                            prep(t + 1, 1 - u, t)
                            scores(t + 1, 1 - u, t)
                            n0 = RING_PREP
                        pe.wait_ge(probs if clipped else exps, t + 1)
                        for n in range(3):
                            def turned(out, n=n):
                                for c in range(4):
                                    last = pe.transpose(out[:, c * S:(c + 1) * S], PR[0:S, (4 * n + c) * P:(4 * n + c + 1) * P], ident[0:S, 0:S])
                                return last
                            group(at_step(t, n0 + n), n0 + n, turned)
                        pe.wait_ge(ring_low, at_step(t, n0 + 3))
                        pe.wait_ge(nat_low, t + 1)
                        pe.wait_ge(out_read, t)
                        for c in range(MC):
                            for a, m in ((PTH, NH), (PTH, NL), (PTL, NH)):
                                last = pe.matmul(OB[0:S, 0:D], a[:, c, :], m[u][:, c, :], start=c == 0 and m is NH and a is PTH,
                                                 stop=c == MC - 1 and a is PTL)
                        last.then_inc(pv_done, 1)
                        if clipped:
                            pe.wait_ge(out_read, t + 1)

                            def attended(out):
                                for k in range(KD):
                                    last = pe.transpose(out[:, k * S:(k + 1) * S], ATT[0:S, k * P:(k + 1) * P], ident[0:S, 0:S])
                                return last
                            group(at_step(t, n0 + 3), n0 + 3, attended)
                            pe.wait_ge(ring_low, at_step(t, n0 + 4))
                            pe.wait_ge(updated, t)
                            for k in range(KD):
                                for a, w in ((ATH, WH), (ATH, WL), (ATL, WH)):
                                    last = pe.matmul(PB[0:S, 0:D], a[:, k, :], w[:, 1, k, :], start=k == 0 and a is ATH and w is WH,
                                                     stop=k == KD - 1 and a is ATL)
                            last.then_inc(proj_full, 1)

                    pe.wait_ge(init, 3 if clipped else 7)
                    if clipped:
                        pe.wait_ge(w_in, 32)
                        for w in range(2):
                            for k in range(KD):
                                n = 2 * w + k
                                if n >= 1:
                                    pe.wait_ge(w_low, n)
                                for c in range(KD):
                                    last = pe.transpose(QB[:, c * P:(c + 1) * P], wraw[:, w, c, k * P:(k + 1) * P], ident[:])
                                last.then_inc(w_full, 1)
                        pe.wait_ge(w_low, 4)
                    prep(0, 0, -1)
                    scores(0, 0, -1)
                    steps(pe, step)

                @blk.scalar
                def _(act):
                    if clipped:
                        for n in range(4):
                            act.wait_ge(w_full, n + 1)
                            act.copy(WH[:, n // 2, n % 2, :], QB[:, 0:D]).then_inc(w_high, 1)

                    def high(r, n, put):
                        act.wait_ge(ring_full, r + 1)
                        put(ring[n % 2]).then_inc(ring_high, 1)

                    def prep(b, p, t):
                        if not (isinstance(b, int) and b == 0):
                            act.wait_ge(scores_full, b)
                            if clipped:
                                act.wait_ge(q_full, b)
                        qd, scale = (XTH, 1.0) if clipped else (QH, float(D) ** -0.5)
                        high(at_step(t, 0), 0, lambda r: act.activation(qd[:], r[:, 0:KD * S].rearrange("p (k s) -> p k s", k=KD), ACT.Copy, scale=scale))
                        for n in range(6):
                            k, c0 = n // 3, 512 * (n % 3)
                            high(at_step(t, 1 + n), 1 + n, lambda r, k=k, c0=c0: act.copy(TH[:, k, c0:c0 + 512], r[:, :]))
                            if n == 2 and clipped:
                                act.wait_ge(q_full, b + 1)
                                act.activation(QH[:], QB[:, 0:KD * S].rearrange("p (k s) -> p k s", k=KD), ACT.Copy, scale=coef[:, 0:1]).then_inc(q_high, 1)

                    def split_high(b, p):
                        act.wait_ge(ctx_in[p], LOADS * half(b, p) + LOADS)
                        if not (isinstance(b, int) and b < 2):
                            act.wait_ge(pv_done, b - 1)
                        act.copy(NH[p][:], CR[p][:]).then_inc(nat_high, 1)

                    def copy_scores(b, p):
                        act.wait_ge(scores_full, b + 1)
                        if not (isinstance(b, int) and b < 2):
                            act.wait_ge(softmax_read, b - 1)
                            act.wait_ge(exps, b - 1)
                        for n, (c0, w) in enumerate(SCOLS):
                            last = act.copy(SC[p][0:S, c0:c0 + w], SP[n][0:S, 0:w])
                        last.then_inc(scores_copied, 1)

                    def step(t, u):
                        n0 = 0
                        if not is_last(t):
                            prep(t + 1, 1 - u, t)
                            n0 = RING_PREP
                        act.wait_ge(neg_max, t + 1)
                        act.wait_ge(probs_used[0], t)
                        act.activation((EXPS if clipped else PR)[0:S, 0:M], SC[u][0:S, :], ACT.Exp, bias=small[u][0:S, 0:1],
                                       **({} if clipped else {"accum_out": small[u][0:S, 1:2]})).then_inc(exps, 1)
                        if not is_last(t):
                            act.wait_ge(pv_done, t)
                            act.copy(NH[1 - u][:], CR[1 - u][:]).then_inc(nat_high, 1)
                            copy_scores_loop(t + 1, 1 - u)
                        act.wait_ge(pv_done, t)
                        for n in range(3):
                            high(at_step(t, n0 + n), n0 + n, lambda r, n=n: act.copy(
                                PTH[:, 4 * n:4 * n + 4, :], r[:, 0:4 * S].rearrange("p (c s) -> p c s", c=4)))
                        if clipped:
                            act.wait_ge(proj_full, t)
                            high(at_step(t, n0 + 3), n0 + 3, lambda r: act.copy(ATH[:], r[:, 0:KD * S].rearrange("p (k s) -> p k s", k=KD)))

                    probs_used = (probs if clipped else pv_done,)

                    def copy_scores_loop(b, p):
                        act.wait_ge(scores_full, b + 1)
                        act.wait_ge(softmax_read, b - 1)
                        act.wait_ge(exps, b - 1)
                        for n, (c0, w) in enumerate(SCOLS):
                            last = act.copy(SC[p][0:S, c0:c0 + w], SP[n][0:S, 0:w])
                        last.then_inc(scores_copied, 1)

                    prep(0, 0, -1)
                    split_high(0, 0)
                    copy_scores(0, 0)
                    steps(act, step)

                CH = 16 if clipped else 3

                @blk.vector
                def _(dve):
                    if clipped:
                        for n in range(4):
                            dve.wait_ge(w_high, n + 1)
                            dve.tensor_tensor(WL[:, n // 2, n % 2, :], QB[:, 0:D], WH[:, n // 2, n % 2, :].bitcast(F32),
                                              ALU.subtract).then_inc(w_low, 1)
                    dve.tensor_scalar(VEPS[0:S, :], MV[0:S, :, 1], LN_EPS, None, ALU.add).then_inc(eps_done, 1)
                    dve.wait_ge(rstd_done, 1)

                    def held(s, value):
                        dve.wait_ge(s, value)
                        if clipped:
                            dve.sem_inc(sink, 1)

                    def normalise(b):
                        dve.tensor_scalar(XHAT[0:S, :], XN[0:S, dsl(b), :], MV[0:S, dsl(b), 0:1].rearrange("p a b -> p (a b)"),
                                          RSTD[0:S, dsl(b)], ALU.subtract, ALU.mult).then_inc(xhat, 1)

                    def low(r, n, put):
                        dve.wait_ge(ring_high, r + 1)
                        put(ring[n % 2]).then_inc(ring_low, 1)

                    def prep(b, p, t, more):
                        qh, ql, scale = (XTH, XTL, 1.0) if clipped else (QH, QL, float(D) ** -0.5)
                        low(at_step(t, 0), 0, lambda r: dve.scalar_tensor_tensor(
                            out=ql[:], in0=r[:, 0:KD * S].rearrange("p (k s) -> p k s", k=KD), scalar=scale, in1=qh[:].bitcast(F32), op0=ALU.mult, op1=ALU.subtract))
                        if more:
                            normalise(b + 1)
                        for n in range(6):
                            k, c0 = n // 3, 512 * (n % 3)
                            low(at_step(t, 1 + n), 1 + n, lambda r, k=k, c0=c0: dve.tensor_tensor(
                                TL[:, k, c0:c0 + 512], r[:, :], TH[:, k, c0:c0 + 512].bitcast(F32), ALU.subtract))
                            if n == 2 and clipped:
                                dve.wait_ge(q_high, b + 1)
                                dve.scalar_tensor_tensor(out=QL[:], in0=QB[:, 0:KD * S].rearrange("p (k s) -> p k s", k=KD), scalar=coef[:, 0:1],
                                                         in1=QH[:].bitcast(F32), op0=ALU.mult, op1=ALU.subtract).then_inc(q_low, 1)

                    def step(t, u):
                        n0 = 0
                        done = [0]

                        def link(ins):
                            done[0] += 1
                            ins.then_inc(chain, 1)
                            held(chain, CH * t + done[0])
                        if not is_last(t):
                            prep(t + 1, 1 - u, t, not (isinstance(t, int) and t == B - 2))
                            n0 = RING_PREP
                        held(scores_copied, t + 1)
                        sm = small[u]
                        if clipped:
                            for r in range(7):
                                src = SC[u] if r == 0 else WORK
                                link(dve.max(top[0:S, 8 * r:8 * r + 8], src[0:S, :]))
                                if r == 0:
                                    dve.tensor_scalar(sm[0:S, 0:1], top[0:S, 0:1], -1.0, None, ALU.mult).then_inc(neg_max, 1)
                                if r < 6:
                                    link(dve.match_replace(WORK[0:S, :], top[0:S, 8 * r:8 * r + 8], src[0:S, :], LOWEST))
                            dve.wait_ge(exps, t + 1)
                            dve.wait_ge(pv_done, t)
                            dve.scalar_tensor_tensor(out=PR[0:S, 0:M], in0=SC[u][0:S, :], scalar=top[0:S, CLIP_K - 1:CLIP_K],
                                                     in1=EXPS[0:S, :], op0=ALU.is_ge, op1=ALU.mult,
                                                     accum_out=sm[0:S, 1:2]).then_inc(probs, 1)
                            dve.wait_ge(probs, t + 1)
                            link(dve.reciprocal(sm[0:S, 2:3], sm[0:S, 1:2]))
                            dve.tensor_scalar(sm[0:S, 4:5], sm[0:S, 2:3], 1.0, None, ALU.mult).then_inc(softmax_read, 1)
                        else:
                            dve.tensor_reduce(sm[0:S, 0:1], SC[u][0:S, :], AX.X, ALU.max, negate=True).then_inc(neg_max, 1)
                            dve.wait_ge(exps, t + 1)
                            link(dve.reciprocal(sm[0:S, 2:3], sm[0:S, 1:2]))
                            dve.tensor_tensor(sm[0:S, 3:4], sm[0:S, 2:3], valid_gain[0:S, dsl(t)], ALU.mult).then_inc(softmax_read, 1)
                        for n in range(3):
                            low(at_step(t, n0 + n), n0 + n, lambda r, n=n: dve.tensor_tensor(
                                PTL[:, 4 * n:4 * n + 4, :], r[:, 0:4 * S].rearrange("p (c s) -> p c s", c=4),
                                PTH[:, 4 * n:4 * n + 4, :].bitcast(F32), ALU.subtract))
                        dve.wait_ge(pv_done, t + 1)
                        if clipped:
                            dve.tensor_scalar(ATT[0:S, :], OB[0:S, 0:D], sm[0:S, 2:3], None, ALU.mult).then_inc(out_read, 1)
                            low(at_step(t, n0 + 3), n0 + 3, lambda r: dve.tensor_tensor(
                                ATL[:], r[:, 0:KD * S].rearrange("p (k s) -> p k s", k=KD), ATH[:].bitcast(F32), ALU.subtract))
                            dve.wait_ge(proj_full, t + 1)
                            dve.scalar_tensor_tensor(out=XNEW[0:S, :], in0=PB[0:S, 0:D], scalar=gains[0:S, 1:2],
                                                     in1=XN[0:S, dsl(t), :].rearrange("p a d -> p (a d)"), op0=ALU.mult, op1=ALU.add).then_inc(updated, 1)
                        else:
                            dve.wait_ge(softmax_read, t + 1)
                            dve.scalar_tensor_tensor(out=XNEW[0:S, :], in0=OB[0:S, 0:D], scalar=sm[0:S, 3:4],
                                                     in1=XN[0:S, dsl(t), :].rearrange("p a d -> p (a d)"), op0=ALU.mult, op1=ALU.add).then_inc(out_read, 1)
                        dve.wait_ge(updated if clipped else out_read, t + 1)
                        link(dve.bn_stats(bn[0:S, 0:6], XNEW[0:S, :]))
                        dve.tensor_scalar(XN[0:S, dsl(t), :].rearrange("p a d -> p (a d)"), XNEW[0:S, :], 1.0, None, ALU.mult)
                        link(dve.bn_aggr(bn[0:S, 6:8], bn[0:S, 0:6]))
                        dve.tensor_scalar(MV[0:S, dsl(t), :].rearrange("p a d -> p (a d)"), bn[0:S, 6:8], 1.0, None, ALU.mult)
                        assert done[0] == CH, done[0]

                    normalise(0)
                    prep(0, 0, -1, True)
                    steps(dve, step)

        def feed_forward(layer):
            L = f"f{layer}_"
            ternary = layer == 1
            EJ = P // E
            EC = EI // EJ
            SCN = -(-SI // P)
            if ternary:
                passes = [[("t", c) for c in range(FI // P)]]
            else:
                every = [("e", c) for c in range(EC)]
                passes = [every[n:n + 6] for n in range(0, EC, 6)] + [[("s", c) for c in range(SCN)]]
            NCM = max(len(p) for p in passes)
            assert all(len(p) % 2 == 0 for p in passes)
            T = B * S
            with ExitStack() as ctx:
                def sb(name, shape, dt=F32):
                    return ctx.enter_context(nc.sbuf_tensor(L + name, shape, dt))

                def bank(name):
                    return ctx.enter_context(nc.psum_tensor(L + name, [P, 512], F32))
                XH, XL = sb("XH", [P, KD, T], F32R), sb("XL", [P, KD, T], F32R)
                if not ternary:
                    YT = sb("YT", [P, KD, T])
                    CW = sb("CW", [P, T])
                WH = sb("WH", [P, NCM, 2 * KD, P], F32R)
                DH = sb("DH", [P, NCM, D], F32R)
                if not ternary:
                    WL, DL = sb("WL", [P, NCM, 2 * KD, P], F32R), sb("DL", [P, NCM, D], F32R)
                RG, RU = sb("RG", [P, NCM, D]), sb("RU", [P, NCM, D])
                RD = sb("RD", [P, KD, NCM * P])
                RDO = None if ternary else sb("RDO", [P, KD, NCM * P])
                GB_, UB_ = [bank("G0"), bank("G1")], [bank("U0"), bank("U1")]
                YB = [[bank(f"Y{u}{k}") for k in range(KD)] for u in range(2)]

                names = ("xhat", "turned", "high", "low", "plain", "logits", "read", "sink", "rstd", "eps", "gw_in", "gw_t",
                         "gw_s", "chain", "exp1", "iota_s", "picked")
                unused = ("plain", "logits", "read", "gw_in", "gw_t", "gw_s", "chain", "exp1", "iota_s", "picked") if ternary else ()
                (xhat, turned, high, low, plain, logits, read, sink, rstd_done, eps_done, gw_in, gw_t, gw_s, chain,
                 exp1, iota_s, picked) = (None if n in unused else sem(L + "n_" + n) for n in names)
                with ExitStack() as rctx:
                    def rb(name, shape, dt=F32):
                        return rctx.enter_context(nc.sbuf_tensor(L + name, shape, dt))
                    XHAT = [rb(f"XHAT{u}", [P, D]) for u in range(2)]
                    if not ternary:
                        NL_ = E + 1
                        XT = [rb(f"XT{u}", [P, KD, S]) for u in range(2)]
                        gw_raw = rb("gw_raw", [NL_, D])
                        gwT = rb("gwT", [P, KD, NL_])
                        LG = rb("LG", [P, B, NL_])
                        top = rb("top", [P, B, 8])
                        idx = rb("idx", [P, B, 8], U32)
                        idxf = rb("idxf", [P, B, 8])
                        iota = rb("iota", [P, B, E])
                        eq, sel = rb("eq", [P, B, E]), rb("sel", [P, B, E])
                        ex, sums = rb("ex", [P, B, E]), rb("sums", [P, B])
                        sig = rb("sig", [P, B])
                    with nc.Block() as blk:
                        @blk.sync
                        def _(sp):
                            if not ternary:
                                sp.dma_start(gw_raw[0:E, :], gate_w).then_inc(gw_in, 16)
                                sp.dma_start(gw_raw[E:E + 1, :], shared_gate_vec).then_inc(gw_in, 16)

                        @blk.gpsimd
                        def _(pool):
                            pool.wait_ge(eps_done, 1)
                            pool.tensor_tensor(RSTD[0:S, :], VEPS[0:S, :], MHALF[0:S, :], ALU.pow).then_inc(rstd_done, 1)
                            if not ternary:
                                pool.iota(iota[:], pattern=[[0, B], [1, E]], base=0, channel_multiplier=0,
                                          allow_small_or_imprecise_dtypes=True).then_inc(iota_s, 1)

                        def pairs(step):
                            def run(eng):
                                step(0, 0)
                                step(1, 1)
                                with eng.Fori(1, B // 2) as j:
                                    step(2 * j, 0)
                                    step(2 * j + 1, 1)
                            return run

                        @blk.tensor
                        def _(pe):
                            if not ternary:
                                pe.wait_ge(gw_in, 32)
                                for k in range(KD):
                                    last = pe.transpose(YB[0][0][:, k * NL_:(k + 1) * NL_], gw_raw[:, k * P:(k + 1) * P], ident[0:NL_, 0:NL_])
                                last.then_inc(gw_t, 1)
                                pe.wait_ge(gw_s, 1)

                            def step(b, u):
                                pe.wait_ge(xhat, b + 1)
                                if not (isinstance(b, int) and b < 2):
                                    pe.wait_ge(low, b - 1)
                                for k in range(KD):
                                    last = pe.transpose(GB_[u][:, k * S:(k + 1) * S], XHAT[u][0:S, k * P:(k + 1) * P], ident[0:S, 0:S])
                                last.then_inc(turned, 1)
                                if not ternary:
                                    pe.wait_ge(plain, b + 1)
                                    if not (isinstance(b, int) and b < 2):
                                        pe.wait_ge(read, b - 1)
                                    for k in range(KD):
                                        last = pe.matmul(UB_[u][0:S, 0:NL_], XT[u][:, k, :], gwT[:, k, :], start=k == 0, stop=k == KD - 1)
                                    last.then_inc(logits, 1)
                            pairs(step)(pe)

                        @blk.scalar
                        def _(act):
                            def step(b, u):
                                r = GB_[u][:, 0:KD * S].rearrange("p (k s) -> p k s", k=KD)
                                act.wait_ge(turned, b + 1)
                                if not ternary:
                                    if not (isinstance(b, int) and b < 2):
                                        act.wait_ge(logits, b - 1)
                                    act.copy(XT[u][:], r).then_inc(plain, 1)
                                act.sem_inc(sink, 1)
                                act.activation(XH[:, :, cols(b, S)], r, ACT.Copy).then_inc(high, 1)
                            pairs(step)(act)
                            if not ternary:
                                act.wait_ge(chain, 1)
                                act.activation(ex[0:S], ex[0:S], ACT.Exp).then_inc(exp1, 1)
                                act.activation(sig[0:S], LG[0:S, :, E], ACT.Exp, scale=-1.0).then_inc(exp1, 1)

                        @blk.vector
                        def _(dve):
                            dve.tensor_scalar(VEPS[0:S, :], MV[0:S, :, 1], LN_EPS, None, ALU.add).then_inc(eps_done, 1)
                            if not ternary:
                                dve.wait_ge(gw_t, 1)
                                dve.tensor_copy(gwT[:], YB[0][0][:, 0:KD * NL_].rearrange("p (k e) -> p k e", k=KD)).then_inc(gw_s, 1)
                            dve.wait_ge(rstd_done, 1)

                            def normalise(b, u):
                                if not (isinstance(b, int) and b < 2):
                                    dve.wait_ge(turned, b - 1)
                                dve.tensor_scalar(XHAT[u][0:S, :], XN[0:S, dsl(b), :], MV[0:S, dsl(b), 0:1].rearrange("p a b -> p (a b)"),
                                                  RSTD[0:S, dsl(b)], ALU.subtract, ALU.mult).then_inc(xhat, 1)

                            def step(b, u, more=True):
                                if more:
                                    normalise(b + 1, 1 - u)
                                dve.wait_ge(high, b + 1)
                                dve.tensor_tensor(XL[:, :, cols(b, S)], GB_[u][:, 0:KD * S].rearrange("p (k s) -> p k s", k=KD),
                                                  XH[:, :, cols(b, S)].bitcast(F32), ALU.subtract).then_inc(low, 1)
                                if not ternary:
                                    dve.wait_ge(logits, b + 1)
                                    dve.tensor_scalar(LG[0:S, dsl(b), :].rearrange("p a e -> p (a e)"), UB_[u][0:S, 0:NL_], 1.0, None, ALU.mult).then_inc(read, 1)
                            normalise(0, 0)
                            step(0, 0)
                            step(1, 1)
                            with dve.Fori(1, B // 2 - 1) as j:
                                step(2 * j, 0)
                                step(2 * j + 1, 1)
                            step(B - 2, 0)
                            step(B - 1, 1, False)
                            if not ternary:
                                n = 0

                                def link(ins):
                                    nonlocal n
                                    n += 1
                                    ins.then_inc(picked, 1)
                                    dve.wait_ge(picked, n)
                                dve.wait_ge(read, B)
                                for b in range(B):
                                    last = dve.max(top[0:S, b, :], LG[0:S, b, 0:E])
                                link(last)
                                for b in range(B):
                                    last = dve.max_index(idx[0:S, b, :], top[0:S, b, :], LG[0:S, b, 0:E])
                                link(last)
                                dve.tensor_tensor(ex[0:S], LG[0:S, :, 0:E], top[0:S, :, 0:1].to_broadcast([S, B, E]),
                                                  ALU.subtract).then_inc(chain, 1)
                                link(dve.tensor_copy(idxf[0:S], idx[0:S]))
                                dve.wait_ge(iota_s, 1)
                                for k in range(TOP_EXPERTS):
                                    dst = sel if k == 0 else eq
                                    link(dve.tensor_tensor(dst[0:S], iota[0:S], idxf[0:S, :, k:k + 1].to_broadcast([S, B, E]), ALU.is_equal))
                                    if k:
                                        link(dve.tensor_tensor(sel[0:S], sel[0:S], eq[0:S], ALU.add))
                                dve.wait_ge(exp1, 2)
                                link(dve.tensor_tensor(sel[0:S], sel[0:S], ex[0:S], ALU.mult))
                                link(dve.tensor_reduce(sums[0:S], sel[0:S], AX.X, ALU.add))
                                link(dve.reciprocal(sums[0:S], sums[0:S]))
                                link(dve.tensor_tensor(CWN[0:S], sel[0:S], sums[0:S, :].rearrange("p (b o) -> p b o", o=1).to_broadcast([S, B, E]), ALU.mult))
                                link(dve.tensor_scalar(sig[0:S], sig[0:S], 1.0, None, ALU.add))
                                dve.reciprocal(SIGN[0:S], sig[0:S])

                names = ("raw_in", "w_full", "w_high", "w_low", "gu_full", "silu", "mid", "hid", "h_high", "h_low",
                         "down", "y_full", "y_read", "y_fin", "y_turned", "x_new", "zeroed", "tern", "sums3", "tot", "scales",
                         "wide", "cwt", "cws", "fsink", "ordered", "links")
                unused = ("w_high", "hid", "zeroed", "wide", "cwt", "cws", "fsink", "ordered") if ternary else \
                    ("tern", "sums3", "tot", "scales", "links")
                (raw_in, w_full, w_high, w_low, gu_full, silu, mid, hid, h_high, h_low, down, y_full, y_read,
                 y_fin, y_turned, x_new, zeroed, tern, sums3, tot, scales, wide, cwt, cws, fsink, ordered, links) = (
                    None if n in unused else sem(L + n) for n in names)
                with ExitStack() as hctx:
                    def hb(name, shape, dt=F32):
                        return hctx.enter_context(nc.sbuf_tensor(L + name, shape, dt))
                    HS = [hb(f"HS{u}", [P, GT]) for u in range(2)]
                    HH, HL = [hb(f"HH{u}", [P, GT], F32R) for u in range(2)], [hb(f"HL{u}", [P, GT], F32R) for u in range(2)]
                    YF = [hb(f"YF{u}", [P, KD, GT]) for u in range(2)] if ternary else [hb("YF", [P, KD, GT])] * 2
                    if ternary:
                        part, half_s = hb("part", [P, 4]), hb("half_s", [P, 16])
                        TM = hb("TM", [P, NCM, D])
                    else:
                        CX = hb("CX", [P, GB, P])
                    blk = hctx.enter_context(nc.Block())
                    before = [sum(len(p) for p in passes[:n]) for n in range(len(passes) + 1)]
                    groups = [0]
                    for p in passes:
                        groups.append(groups[-1] + len(p) + len(p) // 2)
                    raws = [0]
                    NP_ = len(passes)

                    def chunk_no(n, g, c):
                        return before[n] * NG + len(passes[n]) * g + c

                    def used(eng, n, g, c, nch):
                        per = nch - 1
                        base = sum(len(p) - 1 for p in passes[:n]) * NG
                        if c >= 2:
                            eng.wait_ge(down, base + per * g + c - 1)
                        elif not (isinstance(g, int) and g == 0):
                            if c == 0:
                                eng.wait_ge(down, base + per * g)
                            else:
                                eng.wait_ge(y_full, n * NG + g)

                    def over_groups(eng, step):
                        step(0, 0)
                        step(1, 1)
                        with eng.Fori(1, NG // 2) as j:
                            step(2 * j, 0)
                            step(2 * j + 1, 1)

                    @blk.sync
                    def _(sp):
                        total = 0
                        for n, chunks in enumerate(passes):
                            kind, c0, w = chunks[0][0], chunks[0][1], len(chunks)
                            if n:
                                sp.wait_ge(w_full, groups[n])
                            if kind == "s":
                                sp.wait_ge(zeroed, 3)
                            if kind == "e":
                                for e in range(E):
                                    for r, o in ((RG, 0), (RU, EI)):
                                        sp.dma_start(r[e * EJ:(e + 1) * EJ, 0:w, :],
                                                     expert_gate_up[e, o + c0 * EJ:o + (c0 + w) * EJ, :].rearrange("(c j) d -> j c d", j=EJ)).then_inc(raw_in, 16)
                                    for k in range(KD):
                                        sp.dma_start(RD[:, k, e * w * EJ:(e + 1) * w * EJ],
                                                     expert_down[e, k * P:(k + 1) * P, c0 * EJ:(c0 + w) * EJ]).then_inc(raw_in, 16)
                                total += 16 * E * (2 + KD)
                            else:
                                src_g, src_u, src_d, rows = (W_up, W_gate, W_down, FI) if kind == "t" else \
                                    (shared_gate_up[0:SI, :], shared_gate_up[SI:2 * SI, :], shared_down, SI)
                                full, rest = rows // P, rows % P
                                for r, src in ((RG, src_g), (RU, src_u)):
                                    sp.dma_start(r[:, 0:full, :], src[0:full * P, :].rearrange("(c p) d -> p c d", p=P)).then_inc(raw_in, 16)
                                    if rest:
                                        sp.dma_start(r[0:rest, full, :], src[full * P:rows, :]).then_inc(raw_in, 16)
                                sp.dma_start(RD[:, :, 0:rows], src_d.rearrange("(k p) i -> p k i", p=P)).then_inc(raw_in, 16)
                                total += 16 * (3 + 2 * (rest > 0))
                            raws.append(total)

                    @blk.gpsimd
                    def _(pool):
                        for n, chunks in enumerate(passes):
                            if not ternary and n == NP_ - 2:
                                pool.wait_ge(hid, before[n] * NG)
                                pool.wait_ge(w_full, groups[n + 1])
                                pool.memset(RG[SI % P:P, SCN - 1, :], 0.0).then_inc(zeroed, 1)
                                pool.memset(RU[SI % P:P, SCN - 1, :], 0.0).then_inc(zeroed, 1)
                                pool.wait_ge(zeroed, 2)
                                pool.memset(RD[:, :, SI:SCN * P], 0.0).then_inc(zeroed, 1)
                                pool.wait_ge(zeroed, 3)
                            if ternary:
                                continue
                            if n == 0:
                                pool.wait_ge(cws, NG)
                            if chunks[0][0] == "s":
                                pool.wait_ge(cws, 2 * NG)

                            def step(g, u):
                                for c in range(len(chunks)):
                                    pool.wait_ge(mid, chunk_no(n, g, c) + 1)
                                    pool.sem_inc(fsink, 1)
                                    pool.tensor_tensor(HS[c % 2][:], HS[c % 2][:], CW[:, cols(g, GT)], ALU.mult).then_inc(hid, 1)
                            over_groups(pool, step)

                    @blk.tensor
                    def _(pe):
                        ring = [GB_[0], GB_[1]]
                        if ternary:
                            pe.wait_ge(sums3, 3)
                            pe.matmul(YB[0][0][:, 0:3], ones[:], part[:, 0:3], start=True, stop=True).then_inc(tot, 1)
                            pe.wait_ge(tern, 3)

                        def combining(lo):
                            for g in range(NG):
                                pe.wait_ge(wide, lo + g + 1)
                                if g >= 2:
                                    pe.wait_ge(cws, lo + g - 1)
                                for i in range(GB):
                                    last = pe.transpose(UB_[g % 2][:, i * S:(i + 1) * S], CX[0:S, i, :], ident[0:S, 0:S])
                                last.then_inc(cwt, 1)

                        for n, chunks in enumerate(passes):
                            nch = len(chunks)
                            if not ternary and n == 0:
                                combining(0)
                            if not ternary and chunks[0][0] == "s":
                                combining(NG)
                            pe.wait_ge(raw_in, raws[n + 1])
                            if chunks[0][0] == "s":
                                pe.wait_ge(zeroed, 3)
                            if n:
                                pe.wait_ge(mid, before[n] * NG)
                            r = groups[n]
                            for c in range(nch):
                                if r >= 2:
                                    pe.wait_ge(w_low, r - 1)
                                for m, raw in enumerate((RG, RU)):
                                    for k in range(KD):
                                        src = raw[:, c, k * P:(k + 1) * P]
                                        last = pe.transpose(ring[r % 2][:, (m * KD + k) * P:(m * KD + k + 1) * P], src, ident[:])
                                last.then_inc(w_full, 1)
                                r += 1
                            if chunks[0][0] == "e":
                                pe.wait_ge(ordered, n + 1)
                            for c in range(0, nch, 2):
                                pe.wait_ge(w_low, r - 1)
                                for i in range(2):
                                    for k in range(KD):
                                        src = (RDO if chunks[0][0] == "e" else RD)[:, k, (c + i) * P:(c + i + 1) * P]
                                        last = pe.transpose(ring[r % 2][:, (i * KD + k) * P:(i * KD + k + 1) * P], src, ident[:])
                                last.then_inc(w_full, 1)
                                r += 1
                            pe.wait_ge(w_low, r)
                            last_pass = n == NP_ - 1
                            gu_parts = ((WH, XH), (WH, XL)) if ternary else ((WH, XH), (WH, XL), (WL, XH))

                            def hidden(g, c, chunks=chunks, n=n):
                                i = chunk_no(n, g, c)
                                if c >= 2:
                                    pe.wait_ge(mid, i - 1)
                                elif not (isinstance(g, int) and g == 0):
                                    pe.wait_ge(mid, i - 1)
                                for m, bk in enumerate((GB_[c % 2], UB_[c % 2])):
                                    first = True
                                    for k in range(KD):
                                        for w, xx in gu_parts:
                                            last = pe.matmul(bk[:, 0:GT], w[:, c, m * KD + k, :], xx[:, k, cols(g, GT)], start=first,
                                                             stop=k == KD - 1 and (w, xx) == gu_parts[-1])
                                            first = False
                                last.then_inc(gu_full, 1)

                            def project(g, u, c, nch=nch, n=n):
                                i = chunk_no(n, g, c)
                                pe.wait_ge(h_low, i + 1)
                                if c == 0 and not (isinstance(g, int) and g < 2 and n == 0):
                                    if last_pass:
                                        if not (isinstance(g, int) and g < 2):
                                            pe.wait_ge(x_new, GB * (g - 1))
                                        else:
                                            pe.wait_ge(y_read, n * NG)
                                    else:
                                        pe.wait_ge(y_read, n * NG + g - 1)
                                parts = ((DH, HH), (DH, HL)) if ternary else ((DH, HH), (DH, HL), (DL, HH))
                                for k in range(KD):
                                    for w, h in parts:
                                        last = pe.matmul(YB[u][k][:, 0:GT], w[:, c, k * P:(k + 1) * P], h[c % 2][:], start=c == 0 and (w, h) == parts[0],
                                                         stop=c == nch - 1 and (w, h) == parts[-1])
                                last.then_inc(y_full if c == nch - 1 else down, 1)

                            def turn_out(g, u):
                                pe.wait_ge(y_fin, g + 1)
                                for i in range(GB):
                                    for k in range(KD):
                                        o = YB[u][i // 2][0:S, (i % 2) * D + k * P:(i % 2) * D + (k + 1) * P]
                                        last = pe.transpose(o, YF[u][:, k, i * S:(i + 1) * S], ident[:])
                                last.then_inc(y_turned, 1)

                            def step(g, u):
                                first = isinstance(g, int) and g == 0
                                for c in range(nch):
                                    hidden(g, c)
                                    if c >= 2:
                                        project(g, u, c - 2)
                                    elif not first:
                                        project(g - 1, 1 - u, nch - 2 + c)
                                    if last_pass and c == nch - 1 and not first:
                                        turn_out(g - 1, 1 - u)
                            over_groups(pe, step)
                            project(NG - 1, 1, nch - 2)
                            project(NG - 1, 1, nch - 1)
                            if last_pass:
                                turn_out(NG - 1, 1)

                    @blk.scalar
                    def _(act):
                        def combining(lo):
                            for g in range(NG):
                                act.wait_ge(cwt, lo + g + 1)
                                if lo and g == 0:
                                    act.wait_ge(hid, before[NP_ - 1] * NG)
                                act.copy(CW[:, g * GT:(g + 1) * GT], UB_[g % 2][:, 0:GT]).then_inc(cws, 1)

                        for n, chunks in enumerate(passes):
                            nch = len(chunks)
                            if not ternary and n == 0:
                                combining(0)
                            if not ternary and chunks[0][0] == "s":
                                combining(NG)
                            if n:
                                act.wait_ge(y_full, n * NG)
                            r = groups[n]
                            if chunks[0][0] == "e":
                                act.wait_ge(raw_in, raws[n + 1])
                                for k in range(KD):
                                    ins = act.copy(RDO[:, k, 0:nch * P].rearrange("p (c e j) -> p e c j", e=E, j=EJ),
                                                   RD[:, k, 0:nch * P].rearrange("p (e c j) -> p e c j", e=E, j=EJ))
                                ins.then_inc(ordered, 1)
                            for c in range(nch):
                                act.wait_ge(w_full, r + 1)
                                ins = act.copy(WH[:, c, :, :], GB_[r % 2][:, :].rearrange("p (m u) -> p m u", m=2 * KD))
                                ins.then_inc(w_low if ternary else w_high, 1)
                                r += 1
                            for c in range(0, nch, 2):
                                act.wait_ge(w_full, r + 1)
                                ins = act.copy(DH[:, c:c + 2, :], GB_[r % 2][:, :].rearrange("p (c d) -> p c d", c=2))
                                ins.then_inc(w_low if ternary else w_high, 1)
                                r += 1

                            def split_high(g, c, n=n):
                                i = chunk_no(n, g, c)
                                act.wait_ge(mid if ternary else hid, i + 1)
                                used(act, n, g, c, nch)
                                act.copy(HH[c % 2][:], HS[c % 2][:]).then_inc(h_high, 1)

                            def step(g, u, n=n):
                                first = isinstance(g, int) and g == 0
                                for c in range(nch):
                                    i = chunk_no(n, g, c)
                                    act.wait_ge(gu_full, i + 1)
                                    if not (isinstance(i, int) and i < 2):
                                        act.wait_ge(h_low, i - 1)
                                    act.activation(HS[c % 2][:], GB_[c % 2][:, 0:GT], ACT.Silu,
                                                   **({"scale": half_s[:, 3:4]} if ternary else {})).then_inc(silu, 1)
                                    if c:
                                        split_high(g, c - 1)
                                    elif not first:
                                        split_high(g - 1, nch - 1)
                            if ternary:
                                act.wait_ge(scales, 1)
                            over_groups(act, step)
                            split_high(NG - 1, nch - 1)

                    @blk.vector
                    def _(dve):
                        if ternary:
                            dve.wait_ge(raw_in, raws[1])
                            for m, raw in enumerate((RG, RU, RD)):
                                dve.tensor_reduce(part[:, m:m + 1], raw[:], AX.XY, ALU.add, apply_absolute_value=True).then_inc(sums3, 1)
                            dve.wait_ge(tot, 1)
                            n = 0

                            def link(ins):
                                nonlocal n
                                n += 1
                                ins.then_inc(links, 1)
                                dve.wait_ge(links, n)
                            link(dve.tensor_scalar(half_s[:, 3:6], YB[0][0][:, 0:3], 1.0 / (FI * D), TERNARY_EPS, ALU.mult, ALU.add))
                            link(dve.tensor_scalar(half_s[:, 6:9], half_s[:, 3:6], 0.5, None, ALU.mult))
                            link(dve.tensor_scalar(half_s[:, 9:12], half_s[:, 3:6], -0.5, None, ALU.mult))
                            link(dve.tensor_scalar(half_s[:, 0:1], half_s[:, 4:5], half_s[:, 5:6], gains[:, 3:4], ALU.mult, ALU.mult))
                            dve.tensor_scalar(half_s[:, 1:2], half_s[:, 0:1], 1.0, None, ALU.mult).then_inc(scales, 1)
                            for m, raw in enumerate((RG, RU, RD)):
                                flat = TM[:].rearrange("p c d -> p (c d)")
                                rf = raw[:].rearrange("p c d -> p (c d)")
                                link(dve.tensor_scalar(flat, rf, half_s[:, 9 + m:10 + m], None, ALU.is_lt))
                                dve.scalar_tensor_tensor(out=rf, in0=rf, scalar=half_s[:, 6 + m:7 + m], in1=flat,
                                                         op0=ALU.is_gt, op1=ALU.subtract).then_inc(tern, 1)
                                dve.wait_ge(tern, m + 1)
                        gain = half_s[:, 0:1] if ternary else gains[:, 2:3]

                        def combining(src, lo):
                            for g in range(NG):
                                if lo + g:
                                    dve.wait_ge(cwt, lo + g)
                                w = src(g)
                                dve.tensor_copy(CX[0:S, :, :].rearrange("p b (e j) -> p b e j", j=w[1]), w[0]).then_inc(wide, 1)

                        for n, chunks in enumerate(passes):
                            nch = len(chunks)
                            last_pass = n == NP_ - 1
                            if not ternary and n == 0:
                                combining(lambda g: (CWN[0:S, g * GB:(g + 1) * GB, :].rearrange("p b (e o) -> p b e o", o=1).to_broadcast([S, GB, E, EJ]), EJ), 0)
                            if not ternary and chunks[0][0] == "s":
                                combining(lambda g: (SIGN[0:S, g * GB:(g + 1) * GB].rearrange("p (b e o) -> p b e o", e=1, o=1).to_broadcast([S, GB, 1, P]), P), NG)
                            if not ternary:
                                r = groups[n]
                                for c in range(nch):
                                    dve.wait_ge(w_high, r + 1)
                                    dve.tensor_tensor(WL[:, c, :, :], GB_[r % 2][:, :].rearrange("p (m u) -> p m u", m=2 * KD),
                                                      WH[:, c, :, :].bitcast(F32), ALU.subtract).then_inc(w_low, 1)
                                    r += 1
                                for c in range(0, nch, 2):
                                    dve.wait_ge(w_high, r + 1)
                                    dve.tensor_tensor(DL[:, c:c + 2, :], GB_[r % 2][:, :].rearrange("p (c d) -> p c d", c=2),
                                                      DH[:, c:c + 2, :].bitcast(F32), ALU.subtract).then_inc(w_low, 1)
                                    r += 1

                            def split_low(g, c, n=n):
                                dve.wait_ge(h_high, chunk_no(n, g, c) + 1)
                                used(dve, n, g, c, nch)
                                dve.tensor_tensor(HL[c % 2][:], HS[c % 2][:], HH[c % 2][:].bitcast(F32), ALU.subtract).then_inc(h_low, 1)

                            def collect(g, u, n=n):
                                dve.wait_ge(y_full, n * NG + g + 1)
                                if last_pass:
                                    if not (isinstance(g, int) and g < (2 if ternary else 1)):
                                        dve.wait_ge(y_turned, g - 1 if ternary else g)
                                for k in range(KD):
                                    y = YB[u][k][:, 0:GT]
                                    if ternary:
                                        ins = dve.tensor_scalar(YF[u][:, k, :], y, 1.0, None, ALU.mult)
                                    elif n == 0:
                                        ins = dve.tensor_scalar(YT[:, k, cols(g, GT)], y, 1.0, None, ALU.mult)
                                    else:
                                        ins = dve.tensor_tensor(YF[u][:, k, :] if last_pass else YT[:, k, cols(g, GT)], y, YT[:, k, cols(g, GT)], ALU.add)
                                ins.then_inc(y_fin if last_pass else y_read, 1)

                            def update(g, u):
                                dve.wait_ge(y_turned, g + 1)
                                for i in range(GB):
                                    xb = XN[0:S, dsl(GB * g + i), :].rearrange("p a d -> p (a d)")
                                    dve.scalar_tensor_tensor(out=xb, in0=YB[u][i // 2][0:S, (i % 2) * D:(i % 2 + 1) * D], scalar=gain[0:S],
                                                             in1=xb, op0=ALU.mult, op1=ALU.add).then_inc(x_new, 1)

                            def step(g, u, n=n):
                                first = isinstance(g, int) and g == 0
                                for c in range(nch):
                                    dve.wait_ge(silu, chunk_no(n, g, c) + 1)
                                    dve.tensor_tensor(HS[c % 2][:], HS[c % 2][:], UB_[c % 2][:, 0:GT], ALU.mult).then_inc(mid, 1)
                                    if c:
                                        split_low(g, c - 1)
                                    elif not first:
                                        split_low(g - 1, nch - 1)
                                    if c == 2 and not first:
                                        collect(g - 1, 1 - u)
                                if last_pass and not first:
                                    update(g - 1, 1 - u)
                            over_groups(dve, step)
                            split_low(NG - 1, nch - 1)
                            collect(NG - 1, 1)
                            if last_pass:
                                update(NG - 1, 1)

        def token_stats():
            with nc.sbuf_tensor("stats_again", [P, B, 6], F32) as stats:
                stat_done = sem("stat_again_done")
                with nc.Block() as blk:
                    @blk.vector
                    def _(dve):
                        for b in range(B):
                            last = dve.bn_stats(stats[0:S, b, :], XN[0:S, b, :])
                        last.then_inc(stat_done, 1)
                        dve.wait_ge(stat_done, 1)
                        for b in range(B):
                            dve.bn_aggr(MV[0:S, b, :], stats[0:S, b, :])

        def cols(n, width):
            return slice(n * width, (n + 1) * width) if isinstance(n, int) else bass.ds(n * width, width)

        def half(b, p):
            return b // 2 if isinstance(b, int) else halves(b, p)

        def halves(b, p):
            return (b - p) // 2

        def dsl(b):
            return slice(b, b + 1) if isinstance(b, int) else bass.ds(b, 1)

        def dyn(t, b):
            return t[b] if isinstance(b, int) else t[bass.ds(b, 1)].rearrange("a m d -> (a m) d")

        def dynrow(t, b):
            return t[dsl(b), :]

        def store():
            stored = sem("stored")
            with nc.Block() as blk:
                @blk.sync
                def _(sp):
                    sp.dma_start(out.rearrange("b s d -> s b d"), XN[0:S, :, :]).then_inc(stored, 16)
                    sp.wait_ge(stored, 16)


        setup()
        attention(0)
        feed_forward(0); token_stats()
        attention(1)
        feed_forward(1)
        store()


_INS = ['x', 'ctx_2048', 'mask_BxS2_bk0', 'g_xattn', 'g_ffn', 'L0_ffn_gate_w', 'L0_ffn_expert_gate_up',
        'L0_ffn_expert_down', 'L0_ffn_shared_gate_up', 'L0_ffn_shared_down', 'L0_ffn_shared_gate_vec',
        'L1_xattn_W_qkv', 'L1_xattn_W_o', 'L1_xattn_beta_q', 'L1_xattn_beta_k', 'L1_xattn_gate',
        'L1_xattn_log_tau', 'L1_ffn_W_up', 'L1_ffn_W_gate', 'L1_ffn_W_down']


def kernel(**inputs):
    import numpy as _np
    import concourse.bacc as _bacc
    from concourse import mybir as _mybir
    from concourse.bass_utils import run_bass_kernel_spmd as _run

    nc = _bacc.Bacc("TRN2", target_bir_lowering=False, num_devices=1)
    arrays, args = {}, []
    for name in _INS:
        a = _np.ascontiguousarray(inputs[name])
        a = a.reshape(1) if a.ndim == 0 else a
        arrays[f"in_{name}_dram"] = a
        args.append(nc.dram_tensor(f"in_{name}_dram", a.shape, _mybir.dt.from_np(a.dtype), kind="ExternalInput").ap())
    args.append(nc.dram_tensor("out_0_dram", inputs['x'].shape, _mybir.dt.float32, kind="ExternalOutput").ap())
    flamingo_kernel(nc, *args)
    r = _run(nc, [arrays], core_ids=[0])
    return r.results[0]["out_0_dram"]
```

```python
from contextlib import ExitStack

import concourse.bass as bass
from concourse import mybir

ALU = mybir.AluOpType
ACT = mybir.ActivationFunctionType
AX = mybir.AxisListType
F32 = mybir.dt.float32
F32R = mybir.dt.float32r
BF16 = mybir.dt.bfloat16
U8 = mybir.dt.uint8
U32 = mybir.dt.uint32
I32 = mybir.dt.int32

P = 128
NEG = -1.0e30
LOWEST = -3.0e38
LN_EPS = 1e-5
TERNARY_EPS = 1e-8
CLIP_K = 54
TOP_EXPERTS = 4
SLOTS = 4


def flamingo_kernel(nc, x, ctx_mem, mask, g_xattn, g_ffn, gate_w, expert_gate_up, expert_down,
                    shared_gate_up, shared_down, shared_gate_vec, W_qkv, W_o, beta_q, beta_k, gate,
                    log_tau, W_up, W_gate, W_down, out):
    B, S, D = x.shape
    M = ctx_mem.shape[1]
    KD = D // P
    MC = -(-M // P)
    MT = M - (MC - 1) * P
    SB = -(-M // 3)
    SB += SB % 2
    SCOLS = [(0, SB), (SB, SB), (2 * SB, M - 2 * SB)]
    E = gate_w.shape[0]
    EI = expert_down.shape[2]
    SI = shared_down.shape[1]
    FI = W_up.shape[0]
    MF = -(-M // 32) * 32
    GB = 4
    NG = B // GB
    GT = GB * S

    mask_bias_dram = nc.dram_tensor("mask_bias", (B, M), BF16, kind="Internal").ap()

    places_dram = nc.dram_tensor("places_dram", (B, SLOTS), I32, kind="Internal").ap()
    context_rows = ctx_mem.rearrange("b m d -> (b m) d")

    with ExitStack() as whole:
        def sem(name):
            return whole.enter_context(nc.semaphore(name))

        attention_sems = {}

        def attention_sem(name):
            if name not in attention_sems:
                attention_sems[name] = sem("attn_" + name)
            return attention_sems[name]

        def clear_attention_sems():
            with nc.Block() as blk:
                @blk.gpsimd
                def _(pool):
                    for s in attention_sems.values():
                        pool.sem_clear(s)

        def keep(name, shape, dt=F32):
            return whole.enter_context(nc.sbuf_tensor(name, shape, dt))

        XN = keep("XN", [P, B, D])
        MV = keep("MV", [P, B, 2])
        RSTD = keep("RSTD", [P, B])
        VEPS = keep("VEPS", [P, B])
        MHALF = keep("MHALF", [P, B])
        ident = keep("ident", [P, P])
        ones = keep("ones", [P, P])
        gains = keep("gains", [P, 4])
        coef = keep("coef", [P, 1])
        CWN = keep("CWN", [P, B, E])
        SIGN = keep("SIGN", [P, B])
        exact = keep("exact", [P, B])
        redo_gain = keep("redo_gain", [P, B])
        any_redo = keep("any_redo", [P, 1], I32)
        picking = whole.enter_context(ExitStack())

        def pick(name, shape, dt=F32):
            return picking.enter_context(nc.sbuf_tensor(name, shape, dt))

        short_gain, long_gain = pick("short_gain", [P, B]), pick("long_gain", [P, B])
        places = pick("places", [1, B * SLOTS], I32)
        picked_bias = pick("picked_bias", [P, SLOTS * P], BF16)
        pick_row = pick("pick_row", [P, B * S], BF16)
        any_long = pick("any_long", [P, 1], I32)

        def setup():
            with ExitStack() as ctx:
                def sb(name, shape, dt=F32):
                    return ctx.enter_context(nc.sbuf_tensor(name, shape, dt))
                mask_u8 = sb("mask_u8", [B, M], U8)
                mask_bias = sb("mask_bias_sb", [B, M], BF16)
                any_valid = sb("any_valid", [B, 1])
                wide = sb("wide", [B, 2, P])
                chunk_bias = sb("chunk_bias_sb", [B, MC, P], BF16)
                act, iota_c, key = sb("act", [B, MC]), sb("iota_c", [B, MC]), sb("key", [B, MC])
                best, ge, ids = sb("best", [B, 8]), sb("ge", [B, 8]), sb("ids", [B, 8])
                n_act, is_short = sb("n_act", [B, 1]), sb("is_short", [B, 1])
                row_of = sb("row_of", [B, 1])
                place = sb("place", [B, SLOTS], I32)
                here = sb("here", [B, SLOTS, MC])
                start = sb("start", [B, SLOTS])
                vg, shorts, not_short = sb("vg", [P, B]), sb("shorts", [P, B]), sb("not_short", [P, B])
                flags = sb("flags", [P, 1])
                g_raw = sb("g_raw", [P, 4])
                sc = sb("sc", [P, 16])
                stats = sb("stats", [P, B, 6])
                pv = ctx.enter_context(nc.psum_tensor("pv_valid", [P, 2, B], F32))
                x_in, small_in, mask_in = sem("x_in"), sem("small_in"), sem("mask_in")
                consts, v_step, a_step = sem("consts"), sem("setup_v"), sem("setup_a")
                wide_t, bias_out, stat_done = sem("wide_t"), sem("bias_out"), sem("stat_done")
                blk = ctx.enter_context(nc.Block())

                @blk.sync
                def _(sp):
                    sp.dma_start(mask_u8[:], mask).then_inc(mask_in, 16)
                    sp.dma_start(g_raw[:, 0:2], bass_bcast(g_xattn, 2)).then_inc(small_in, 16)
                    sp.dma_start(g_raw[:, 2:4], bass_bcast(g_ffn, 2)).then_inc(small_in, 16)
                    for n, t in enumerate((gate, beta_q, beta_k, log_tau)):
                        sp.dma_start(sc[:, n:n + 1], bass_bcast(t, 1)).then_inc(small_in, 16)
                    for n in range(4):
                        q = B // 4
                        sp.dma_start(XN[0:S, n * q:(n + 1) * q, :],
                                     x[n * q:(n + 1) * q].rearrange("b s d -> s b d")).then_inc(x_in, 16)
                    sp.wait_ge(v_step, 8)
                    sp.dma_start(mask_bias_dram, mask_bias[:]).then_inc(bias_out, 16)
                    sp.dma_start(places_dram, place[:]).then_inc(bias_out, 16)
                    sp.wait_ge(bias_out, 32)
                    sp.dma_start(places[:], places_dram.rearrange("(a b) c -> a (b c)", a=1)).then_inc(bias_out, 16)
                    sp.wait_ge(bias_out, 48)

                @blk.gpsimd
                def _(pool):
                    pool.memset(ident[:], 0.0).then_inc(consts, 1)
                    pool.memset(ones[:], 1.0).then_inc(consts, 1)
                    pool.memset(MHALF[:], -0.5).then_inc(consts, 1)
                    pool.wait_ge(consts, 3)
                    pool.affine_select(out=ident[:], in_=ident[:], compare_op=ALU.not_equal, fill=1.0, base=0,
                                       pattern=[[-1, P]], channel_multiplier=1).then_inc(consts, 1)
                    pool.iota(iota_c[:], pattern=[[1, MC]], base=0, channel_multiplier=0, allow_small_or_imprecise_dtypes=True).then_inc(consts, 1)
                    pool.iota(row_of[:], pattern=[[0, 1]], base=0, channel_multiplier=M, allow_small_or_imprecise_dtypes=True).then_inc(consts, 1)
                    pool.memset(picked_bias[:], 0.0).then_inc(consts, 1)
                    pool.memset(pick_row[:], 0.0).then_inc(consts, 1)
                    pool.wait_ge(consts, 8)
                    pool.affine_select(out=pick_row[:].rearrange("p (b s) -> p b s", s=S), in_=pick_row[:].rearrange("p (b s) -> p b s", s=S),
                                       compare_op=ALU.not_equal, fill=1.0, base=0, pattern=[[-1, B], [0, S]], channel_multiplier=1).then_inc(consts, 1)

                @blk.scalar
                def _(act):
                    act.wait_ge(small_in, 96)
                    act.activation(gains[:], g_raw[:], ACT.Tanh).then_inc(a_step, 1)
                    act.activation(sc[:, 4:5], sc[:, 0:1], ACT.Exp, scale=-1.0).then_inc(a_step, 1)
                    act.activation(sc[:, 5:6], sc[:, 3:4], ACT.Exp).then_inc(a_step, 1)

                @blk.tensor
                def _(pe):
                    pe.wait_ge(consts, 4)
                    pe.wait_ge(v_step, 14 + MC)
                    pe.transpose(pv[:, 0, :], wide[:, 0, :], ident[0:B, 0:B])
                    pe.transpose(pv[:, 1, :], wide[:, 1, :], ident[0:B, 0:B]).then_inc(wide_t, 1)

                @blk.vector
                def _(dve):
                    n = 0

                    def chain(ins):
                        nonlocal n
                        n += 1
                        ins.then_inc(v_step, 1)
                        dve.wait_ge(v_step, n)
                    dve.wait_ge(mask_in, 16)
                    chain(dve.tensor_scalar(mask_bias[:], mask_u8[:], 1.0, -NEG, ALU.subtract, ALU.mult))
                    dve.memset(chunk_bias[:, MC - 1, 0:P - MT], NEG)
                    dve.tensor_copy(chunk_bias[:, MC - 1, P - MT:P], mask_bias[:, (MC - 1) * P:M])
                    dve.tensor_copy(chunk_bias[:, 0:MC - 1, :], mask_bias[:, 0:(MC - 1) * P].rearrange("b (c p) -> b c p", p=P))
                    dve.tensor_reduce(act[:, 0:MC - 1], mask_u8[:, 0:(MC - 1) * P].rearrange("b (c p) -> b c p", p=P), AX.X, ALU.max)
                    chain(dve.tensor_reduce(act[:, MC - 1:MC], mask_u8[:, (MC - 1) * P:M], AX.X, ALU.max))
                    dve.wait_ge(consts, 6)
                    chain(dve.scalar_tensor_tensor(out=key[:], in0=act[:], scalar=32.0, in1=iota_c[:], op0=ALU.mult, op1=ALU.add))
                    chain(dve.max(best[:], key[:]))
                    chain(dve.tensor_scalar(ge[:], best[:], 32.0, None, ALU.is_ge))
                    chain(dve.scalar_tensor_tensor(out=ids[:], in0=ge[:], scalar=-32.0, in1=best[:], op0=ALU.mult, op1=ALU.add))
                    chain(dve.tensor_scalar(start[:], ids[:, 0:SLOTS], float(P), float(M - P), ALU.mult, ALU.min))
                    chain(dve.tensor_scalar(place[:, 0:SLOTS], start[:], row_of[:, 0:1], None, ALU.add))
                    for n_ in range(SLOTS):
                        last = dve.tensor_scalar(here[:, n_, :], iota_c[:], ids[:, n_:n_ + 1], None, ALU.is_equal)
                    dve.wait_ge(consts, 9)
                    chain(last)
                    for c in range(MC):
                        for n_ in range(SLOTS):
                            o = picked_bias[0:B, n_ * P:(n_ + 1) * P]
                            last = dve.scalar_tensor_tensor(out=o, in0=chunk_bias[:, c, :], scalar=here[:, n_, c:c + 1], in1=o,
                                                            op0=ALU.mult, op1=ALU.add)
                        chain(last)
                    chain(dve.tensor_reduce(any_valid[:], act[:], AX.X, ALU.max))
                    chain(dve.tensor_reduce(n_act[:], act[:], AX.X, ALU.add))
                    chain(dve.tensor_scalar(is_short[:], n_act[:], float(SLOTS), None, ALU.is_le))
                    chain(dve.tensor_scalar(wide[:, 0, :], ones[0:B, :], any_valid[:, 0:1], None, ALU.mult))
                    chain(dve.tensor_scalar(wide[:, 1, :], ones[0:B, :], is_short[:, 0:1], None, ALU.mult))
                    dve.wait_ge(a_step, 3)
                    chain(dve.tensor_scalar(sc[:, 6:7], sc[:, 4:5], 1.0, None, ALU.add))
                    chain(dve.reciprocal(sc[:, 7:8], sc[:, 6:7]))
                    chain(dve.tensor_tensor(sc[:, 8:9], sc[:, 7:8], sc[:, 1:2], ALU.mult))
                    chain(dve.tensor_scalar(sc[:, 9:10], sc[:, 7:8], -1.0, 1.0, ALU.mult, ALU.add))
                    chain(dve.tensor_tensor(sc[:, 10:11], sc[:, 9:10], sc[:, 2:3], ALU.mult))
                    chain(dve.tensor_tensor(sc[:, 11:12], sc[:, 8:9], sc[:, 10:11], ALU.add))
                    chain(dve.tensor_scalar(coef[:], sc[:, 11:12], float(D) ** -0.5, sc[:, 5:6], ALU.mult, ALU.mult))
                    dve.wait_ge(wide_t, 1)
                    chain(dve.tensor_scalar(vg[:], pv[:, 0, :], gains[:, 0:1], None, ALU.mult))
                    chain(dve.tensor_copy(shorts[:], pv[:, 1, :]))
                    chain(dve.tensor_scalar(not_short[:], shorts[:], -1.0, 1.0, ALU.mult, ALU.add))
                    dve.tensor_tensor(short_gain[:], vg[:], shorts[:], ALU.mult)
                    dve.tensor_tensor(long_gain[:], vg[:], not_short[:], ALU.mult)
                    chain(dve.tensor_reduce(flags[:], not_short[:], AX.X, ALU.max))
                    dve.tensor_copy(any_long[:], flags[:])
                    for q in range(4):
                        dve.wait_ge(x_in, 64)
                        for b in range(q * B // 4, (q + 1) * B // 4):
                            last = dve.bn_stats(stats[0:S, b, :], XN[0:S, b, :])
                    last.then_inc(stat_done, 1)
                    dve.wait_ge(stat_done, 1)
                    for b in range(B):
                        dve.bn_aggr(MV[0:S, b, :], stats[0:S, b, :])

        def bass_bcast(t, n):
            return t.partition_broadcast(P)

        def attention(layer, picked=False, guard=None):
            L = f"a{layer}{'p' if picked else 'q' if layer and guard is None else ''}_"
            clipped = layer == 1
            quick = clipped and guard is None
            NC = SLOTS if picked else MC
            MW = NC * P if picked else M
            NPAD = NC * P
            TG = NC // 4
            PREP = 1 + KD * TG
            R = PREP + TG + clipped
            NRING = 4 if picked else 2
            COLS = [(0, NPAD)] if picked else SCOLS
            masked_rows = not clipped and not picked
            gain_of = short_gain if picked else long_gain

            def guarded(body):
                def run(eng):
                    if guard is None:
                        body(eng)
                    else:
                        flag = eng.value_load(guard, min_val=0, max_val=1)
                        with eng.If(flag > 0):
                            body(eng)
                return run
            with ExitStack() as ctx:
                def sb(name, shape, dt=F32):
                    return ctx.enter_context(nc.sbuf_tensor(L + name, shape, dt))

                def bank(name):
                    return ctx.enter_context(nc.psum_tensor(L + name, [P, 512], F32))
                CR = [sb(f"CR{p}", [P, NC, D]) for p in range(2)]
                NH = [sb(f"NH{p}", [P, NC, D], F32R) for p in range(2)]
                NL = [sb(f"NL{p}", [P, NC, D], F32R) for p in range(2)]
                TH, TL = sb("TH", [P, KD, NPAD], F32R), sb("TL", [P, KD, NPAD], F32R)
                QH, QL = sb("QH", [P, KD, S], F32R), sb("QL", [P, KD, S], F32R)
                XHAT = sb("XHAT", [P, D])
                SC = [sb(f"SC{p}", [P, MF if quick else MW]) for p in range(2)]
                PR = sb("PR", [P, NPAD])
                PTH, PTL = sb("PTH", [P, NC, S], F32R), sb("PTL", [P, NC, S], F32R)
                small = [sb(f"small{p}", [P, 8]) for p in range(2)]
                bn = sb("bn", [P, 8])
                XNEW = sb("XNEW", [P, D])
                if clipped:
                    top = sb("top", [P, 56])
                    WORK = sb("WORK", [P, MF // 8 if quick else MW])
                    if quick:
                        FOLD = sb("FOLD", [P, MF * 7 // 4])
                        cand, CWORK = sb("cand", [P, 112]), sb("CWORK", [P, 112])
                    EXPS = sb("EXPS", [P, MW])
                    XTH, XTL = sb("XTH", [P, KD, S], F32R), sb("XTL", [P, KD, S], F32R)
                    ATT = sb("ATT", [P, D])
                    ATH, ATL = sb("ATH", [P, KD, S], F32R), sb("ATL", [P, KD, S], F32R)
                    wraw = sb("wraw", [P, 2, KD, D])
                    WH, WL = sb("WH", [P, 2, KD, D], F32R), sb("WL", [P, 2, KD, D], F32R)
                elif masked_rows:
                    BIAS = [sb(f"BIAS{p}", [P, MW], BF16) for p in range(2)]
                    row0 = sb("row0", [P, S], BF16)
                ring = [bank(f"ring{n}") for n in range(NRING)]
                SP = [bank(f"S{n}") for n in range(len(COLS))]
                OB = bank("O")
                QB, PB = (bank("Q"), bank("proj")) if clipped else (None, None)

                ctx_in = [attention_sem("ctx_in0"), attention_sem("ctx_in1")]
                names = ("init", "rstd", "xhat", "ring_full", "ring_high", "ring_low", "scores_full", "scores_copied",
                         "neg_max", "exps", "probs", "softmax_read", "nat_high", "nat_low", "pv_done", "out_read",
                         "chain", "q_full", "q_high", "q_low", "proj_full", "updated", "w_in", "w_full",
                         "w_high", "w_low", "eps_done", "sink")
                unused = () if clipped else ("probs", "q_full", "q_high", "q_low", "proj_full", "updated", "w_in",
                                             "w_full", "w_high", "w_low")
                (init, rstd_done, xhat, ring_full, ring_high, ring_low, scores_full, scores_copied, neg_max, exps,
                 probs, softmax_read, nat_high, nat_low, pv_done, out_read, chain, q_full, q_high, q_low,
                 proj_full, updated, w_in, w_full, w_high, w_low, eps_done, sink) = (
                    None if n in unused else attention_sem(n) for n in names)
                blk = ctx.enter_context(nc.Block())
                LOADS = 16 * SLOTS if picked else 32 if clipped else 48

                def step_at(t):
                    return 2 * PREP + (R * t - 1 if not is_first(t) else 0) - (PREP * max(0, t - (B - 2)) if isinstance(t, int) else 0)

                def probs_at(t):
                    if clipped:
                        return step_at(t) + (PREP if prepares(t) else 0) + (0 if is_first(t) else 1)
                    return 2 * PREP + R * t - (PREP if isinstance(t, int) and t == B - 1 else 0)

                def prep_at(b):
                    return PREP * b if isinstance(b, int) and b < 2 else step_at(b - 2) if clipped else probs_at(b - 2) + TG

                def attended_at(t):
                    return step_at(t + 1) + (PREP if prepares(t + 1) else 0)

                PREP_N, PROBS_N, ATTENDED_N = (0, PREP + 1, PREP) if clipped else (TG, 0, None)

                def steps(eng, step):
                    step(0, 0)
                    step(1, 1)
                    with eng.Fori(1, B // 2 - 2) as j:
                        for u in range(2):
                            step(2 * j + u, u)
                    for t in range(B - 4, B):
                        step(t, t % 2)

                def prepares(t):
                    return not (isinstance(t, int) and t >= B - 2)

                def is_first(t):
                    return isinstance(t, int) and t == 0

                def is_last(t):
                    return isinstance(t, int) and t == B - 1

                @blk.sync
                @guarded
                def _(sp):
                    if clipped:
                        sp.dma_start(wraw[:, 0, :, :], W_qkv[0:D, :].rearrange("(c p) d -> p c d", p=P)).then_inc(w_in, 16)
                        sp.dma_start(wraw[:, 1, :, :], W_o.rearrange("(c p) d -> p c d", p=P)).then_inc(w_in, 16)
                    sp.wait_ge(init, 5 if masked_rows else 2)

                    def load(b, p, reused):
                        if reused:
                            sp.wait_ge(nat_low, b - 1)
                            sp.sem_inc(sink, 1)
                        if picked:
                            rows = [sp.value_load(places[0:1, dcol(b * SLOTS + c)], min_val=0, max_val=B * M - P) for c in range(SLOTS)]
                            for c, row in enumerate(rows):
                                sp.dma_start(CR[p][:, c, :], context_rows[bass.ds(row, P), :]).then_inc(ctx_in[p], 16)
                            return
                        sp.dma_start(CR[p][:, 0:MC - 1, :],
                                     dyn(ctx_mem, b)[0:(MC - 1) * P, :].rearrange("(c p) d -> p c d", p=P)).then_inc(ctx_in[p], 16)
                        sp.dma_start(CR[p][0:MT, MC - 1, :], dyn(ctx_mem, b)[(MC - 1) * P:M, :]).then_inc(ctx_in[p], 16)
                        if not clipped:
                            sp.dma_start(BIAS[p][0:1, :], dynrow(mask_bias_dram, b)).then_inc(ctx_in[p], 16)
                    load(0, 0, False)
                    load(1, 1, False)
                    load(2, 0, True)
                    with sp.Fori(0, (B - 4) // 2) as j:
                        for u in range(2):
                            load(2 * j + 3 + u, (u + 1) % 2, True)
                    load(B - 1, 1, True)

                @blk.gpsimd
                @guarded
                def _(pool):
                    pool.memset(CR[0][:, NC - 1, :], 0.0).then_inc(init, 1)
                    pool.memset(CR[1][:, NC - 1, :], 0.0).then_inc(init, 1)
                    if masked_rows:
                        pool.memset(BIAS[0][:], 0.0).then_inc(init, 1)
                        pool.memset(BIAS[1][:], 0.0).then_inc(init, 1)
                        pool.memset(row0[:], 0.0).then_inc(init, 1)
                        pool.wait_ge(init, 5)
                        pool.memset(row0[0:1, :], 1.0).then_inc(init, 1)
                    pool.memset(PR[:], 0.0).then_inc(init, 1)
                    if quick:
                        pool.memset(SC[0][:, M:MF], LOWEST).then_inc(init, 1)
                        pool.memset(SC[1][:, M:MF], LOWEST).then_inc(init, 1)
                    pool.wait_ge(eps_done, 1)
                    pool.tensor_tensor(RSTD[0:S, :], VEPS[0:S, :], MHALF[0:S, :], ALU.pow).then_inc(rstd_done, 1)

                    def split(b, p, count):
                        pool.wait_ge(ctx_in[p], count)
                        if masked_rows:
                            pool.wait_ge(scores_full, b + 1)
                        pool.wait_ge(nat_high, b + 1)
                        pool.tensor_tensor(NL[p][:], CR[p][:], NH[p][:].bitcast(F32), ALU.subtract).then_inc(nat_low, 1)
                    split(0, 0, LOADS)
                    split(1, 1, LOADS)
                    with pool.Fori(1, B // 2) as j:
                        for u in range(2):
                            split(2 * j + u, u, LOADS * j + LOADS)

                @blk.tensor
                @guarded
                def _(pe):
                    def group(r, n, put, after_same=False):
                        if not (isinstance(r, int) and r == 0):
                            if NRING == 2:
                                pe.wait_ge(ring_low, r if after_same else r - 1)
                            elif not (isinstance(r, int) and r <= 2):
                                pe.wait_ge(ring_low, r if isinstance(r, int) and r >= probs_at(B - 1) else r - 2)
                        put(ring[n % NRING]).then_inc(ring_full, 1)

                    def prep(b, p):
                        pe.wait_ge(xhat, b + 1)

                        def queries(out):
                            for k in range(KD):
                                last = pe.transpose(out[:, k * S:(k + 1) * S], XHAT[0:S, k * P:(k + 1) * P], ident[0:S, 0:S])
                            return last
                        group(prep_at(b), PREP_N, queries, clipped or masked_rows)
                        pe.wait_ge(ctx_in[p], LOADS * half(b, p) + LOADS)
                        for n in range(KD * TG):
                            k, c0 = n // TG, 4 * (n % TG)

                            def context(out, k=k, c0=c0):
                                for c in range(4):
                                    last = pe.transpose(out[:, c * P:(c + 1) * P], CR[p][:, c0 + c, k * P:(k + 1) * P], ident[:])
                                return last
                            group(prep_at(b) + 1 + n, PREP_N + 1 + n, context)
                            if n == 1 and clipped:
                                pe.wait_ge(ring_low, prep_at(b) + 1)
                                for m in range(KD):
                                    first = True
                                    for k2 in range(KD):
                                        for w, xx in ((WH, XTH), (WH, XTL), (WL, XTH)):
                                            last = pe.matmul(QB[:, m * S:(m + 1) * S], w[:, 0, k2, m * P:(m + 1) * P], xx[:, k2, :],
                                                             start=first, stop=k2 == KD - 1 and w is WL)
                                            first = False
                                last.then_inc(q_full, 1)

                    def scores(b):
                        pe.wait_ge(ring_low, prep_at(b) + PREP)
                        if clipped:
                            pe.wait_ge(q_low, b + 1)
                        pe.wait_ge(scores_copied, b)
                        for n, (c0, w) in enumerate(COLS):
                            first = True
                            for k in range(KD):
                                for q, m in ((QH, TH), (QH, TL), (QL, TH)):
                                    last = pe.matmul(SP[n][0:S, 0:w], q[:, k, :], m[:, k, c0:c0 + w], start=first,
                                                     stop=clipped and k == KD - 1 and q is QL)
                                    first = False
                            if picked:
                                last = pe.matmul(SP[n][0:S, 0:w], pick_row[:, cols(b, S)], picked_bias[:, 0:w], start=False, stop=True)
                            elif masked_rows:
                                last = pe.matmul(SP[n][0:S, 0:w], row0[:], BIAS[p_of(b)][:, c0:c0 + w], start=False, stop=True)
                        last.then_inc(scores_full, 1)

                    def p_of(b):
                        return parity[0]

                    def project(t):
                        pe.wait_ge(out_read, t + 1)

                        def attended(out):
                            for k in range(KD):
                                last = pe.transpose(out[:, k * S:(k + 1) * S], ATT[0:S, k * P:(k + 1) * P], ident[0:S, 0:S])
                            return last
                        group(attended_at(t), ATTENDED_N, attended)
                        pe.wait_ge(ring_low, attended_at(t) + 1)
                        pe.wait_ge(updated, t)
                        for k in range(KD):
                            for a, w in ((ATH, WH), (ATH, WL), (ATL, WH)):
                                last = pe.matmul(PB[0:S, 0:D], a[:, k, :], w[:, 1, k, :], start=k == 0 and a is ATH and w is WH,
                                                 stop=k == KD - 1 and a is ATL)
                        last.then_inc(proj_full, 1)

                    parity = [0]

                    def turn_probs(t):
                        pe.wait_ge(probs if clipped else exps, t + 1)
                        for n in range(TG):
                            def turned(out, n=n):
                                for c in range(4):
                                    last = pe.transpose(out[:, c * S:(c + 1) * S], PR[0:S, (4 * n + c) * P:(4 * n + c + 1) * P], ident[0:S, 0:S])
                                return last
                            group(probs_at(t) + n, PROBS_N + n, turned, n == 0 and (is_first(t) or not clipped))

                    def weigh(t, p):
                        pe.wait_ge(ring_low, probs_at(t) + TG)
                        pe.wait_ge(nat_low, t + 1)
                        pe.wait_ge(out_read, t)
                        for c in range(NC):
                            for a, m in ((PTH, NH), (PTH, NL), (PTL, NH)):
                                last = pe.matmul(OB[0:S, 0:D], a[:, c, :], m[p][:, c, :], start=c == 0 and m is NH and a is PTH,
                                                 stop=c == NC - 1 and a is PTL)
                        last.then_inc(pv_done, 1)

                    def step(t, u):
                        if not is_last(t):
                            parity[0] = 1 - u
                            scores(t + 1)
                        if clipped:
                            if not is_first(t):
                                weigh(t - 1, 1 - u)
                            if prepares(t):
                                prep(t + 2, u)
                            if not is_first(t):
                                project(t - 1)
                            turn_probs(t)
                        else:
                            turn_probs(t)
                            if prepares(t):
                                prep(t + 2, u)
                            weigh(t, u)

                    pe.wait_ge(init, 7 if masked_rows else 3)
                    if clipped:
                        pe.wait_ge(w_in, 32)
                        for w in range(2):
                            for k in range(KD):
                                n = 2 * w + k
                                if n >= 1:
                                    pe.wait_ge(w_low, n)
                                for c in range(KD):
                                    last = pe.transpose(QB[:, c * P:(c + 1) * P], wraw[:, w, c, k * P:(k + 1) * P], ident[:])
                                last.then_inc(w_full, 1)
                        pe.wait_ge(w_low, 4)
                    prep(0, 0)
                    scores(0)
                    prep(1, 1)
                    steps(pe, step)
                    if clipped:
                        weigh(B - 1, 1)
                        project(B - 1)

                @blk.scalar
                @guarded
                def _(act):
                    if clipped:
                        for n in range(4):
                            act.wait_ge(w_full, n + 1)
                            act.copy(WH[:, n // 2, n % 2, :], QB[:, 0:D]).then_inc(w_high, 1)

                    def high(r, n, put):
                        act.wait_ge(ring_full, r + 1)
                        put(ring[n % NRING]).then_inc(ring_high, 1)

                    def prep(b, p, between=()):
                        if not is_first(b):
                            act.wait_ge(scores_full, b)
                        qd, scale = (XTH, 1.0) if clipped else (QH, float(D) ** -0.5)
                        high(prep_at(b), PREP_N, lambda r: act.activation(qd[:], r[:, 0:KD * S].rearrange("p (k s) -> p k s", k=KD), ACT.Copy, scale=scale))
                        for n in range(KD * TG):
                            k, c0 = n // TG, 512 * (n % TG)
                            high(prep_at(b) + 1 + n, PREP_N + 1 + n, lambda r, k=k, c0=c0: act.copy(TH[:, k, c0:c0 + 512], r[:, :]))
                            if n < len(between) and between[n]:
                                between[n]()
                            if n == 2 and clipped:
                                act.wait_ge(q_full, b + 1)
                                act.activation(QH[:], QB[:, 0:KD * S].rearrange("p (k s) -> p k s", k=KD), ACT.Copy, scale=coef[:, 0:1]).then_inc(q_high, 1)

                    def split_high(b, p, part=None):
                        act.wait_ge(ctx_in[p], LOADS * half(b, p) + LOADS)
                        act.wait_ge(ring_full, prep_at(b) + PREP)
                        if not (isinstance(b, int) and b < 2):
                            act.wait_ge(pv_done, b - 1)
                        c = slice(0, NC) if part is None else slice(part * NC // 3, (part + 1) * NC // 3)
                        copied = act.copy(NH[p][:, c, :], CR[p][:, c, :])
                        if part in (None, 2):
                            copied.then_inc(nat_high, 1)

                    def copy_scores(b, p):
                        act.wait_ge(scores_full, b + 1)
                        if not (isinstance(b, int) and b < 2):
                            act.wait_ge(softmax_read, b - 1)
                            act.wait_ge(exps, b - 1)
                        for n, (c0, w) in enumerate(COLS):
                            last = act.copy(SC[p][0:S, c0:c0 + w], SP[n][0:S, 0:w])
                        last.then_inc(scores_copied, 1)

                    def high_attended(t):
                        if not is_first(t):
                            act.wait_ge(proj_full, t)
                        high(attended_at(t), ATTENDED_N, lambda r: act.copy(ATH[:], r[:, 0:KD * S].rearrange("p (k s) -> p k s", k=KD)))

                    def step(t, u):
                        act.wait_ge(neg_max, t + 1)
                        if not is_first(t):
                            act.wait_ge(probs if clipped else pv_done, t)
                        act.activation((EXPS if clipped else PR)[0:S, 0:MW], SC[u][0:S, 0:MW], ACT.Exp, bias=small[u][0:S, 0:1],
                                       **({} if clipped else {"accum_out": small[u][0:S, 1:2]})).then_inc(exps, 1)
                        if not is_last(t) and not clipped:
                            split_high(t + 1, 1 - u)
                        if not is_last(t):
                            copy_scores(t + 1, 1 - u)
                        if clipped:
                            if prepares(t):
                                prep(t + 2, u, [None if n % 2 == 0 else lambda n=n: split_high(t + 1, 1 - u, n // 2) for n in range(6)])
                            elif not is_last(t):
                                split_high(t + 1, 1 - u)
                            if not is_first(t):
                                high_attended(t - 1)
                        if not is_first(t):
                            act.wait_ge(pv_done, t)
                        for n in range(TG):
                            high(probs_at(t) + n, PROBS_N + n, lambda r, n=n: act.copy(
                                PTH[:, 4 * n:4 * n + 4, :], r[:, 0:4 * S].rearrange("p (c s) -> p c s", c=4)))
                        if prepares(t) and not clipped:
                            prep(t + 2, u)

                    prep(0, 0)
                    if clipped:
                        copy_scores(0, 0)
                        split_high(0, 0)
                    else:
                        split_high(0, 0)
                        copy_scores(0, 0)
                    prep(1, 1)
                    steps(act, step)
                    if clipped:
                        high_attended(B - 1)

                CH = 34 if quick else 16 if clipped else 3

                @blk.vector
                @guarded
                def _(dve):
                    if clipped:
                        for n in range(4):
                            dve.wait_ge(w_high, n + 1)
                            dve.tensor_tensor(WL[:, n // 2, n % 2, :], QB[:, 0:D], WH[:, n // 2, n % 2, :].bitcast(F32),
                                              ALU.subtract).then_inc(w_low, 1)
                    dve.tensor_scalar(VEPS[0:S, :], MV[0:S, :, 1], LN_EPS, None, ALU.add).then_inc(eps_done, 1)
                    dve.wait_ge(rstd_done, 1)
                    if quick:
                        dve.wait_ge(init, 5)

                    def held(s, value):
                        dve.wait_ge(s, value)
                        if clipped:
                            dve.sem_inc(sink, 1)

                    def normalise(b):
                        dve.tensor_scalar(XHAT[0:S, :], XN[0:S, dsl(b), :], MV[0:S, dsl(b), 0:1].rearrange("p a b -> p (a b)"),
                                          RSTD[0:S, dsl(b)], ALU.subtract, ALU.mult).then_inc(xhat, 1)

                    def low(r, n, put):
                        dve.wait_ge(ring_high, r + 1)
                        put(ring[n % NRING]).then_inc(ring_low, 1)

                    def prep_parts(b):
                        qh, ql, scale = (XTH, XTL, 1.0) if clipped else (QH, QL, float(D) ** -0.5)

                        def queries():
                            low(prep_at(b), PREP_N, lambda r: dve.scalar_tensor_tensor(
                                out=ql[:], in0=r[:, 0:KD * S].rearrange("p (k s) -> p k s", k=KD), scalar=scale, in1=qh[:].bitcast(F32), op0=ALU.mult, op1=ALU.subtract))
                            if not is_last(b):
                                normalise(b + 1)

                        def context(n):
                            k, c0 = n // TG, 512 * (n % TG)
                            low(prep_at(b) + 1 + n, PREP_N + 1 + n, lambda r: dve.tensor_tensor(
                                TL[:, k, c0:c0 + 512], r[:, :], TH[:, k, c0:c0 + 512].bitcast(F32), ALU.subtract))
                            if n == 2 and clipped:
                                dve.wait_ge(q_high, b + 1)
                                dve.scalar_tensor_tensor(out=QL[:], in0=QB[:, 0:KD * S].rearrange("p (k s) -> p k s", k=KD), scalar=coef[:, 0:1],
                                                         in1=QH[:].bitcast(F32), op0=ALU.mult, op1=ALU.subtract).then_inc(q_low, 1)
                        return [queries] + [lambda n=n: context(n) for n in range(KD * TG)]

                    def prep(b):
                        for part in prep_parts(b):
                            part()

                    linked = [0, 0]

                    def link(ins, meanwhile=()):
                        linked[1] += 1
                        ins.then_inc(chain, 1)
                        for f in meanwhile:
                            f()
                        held(chain, linked[0] + linked[1])

                    def update(t, u):
                        if clipped:
                            dve.wait_ge(proj_full, t + 1)
                            f, o = small[u][0:S, 3:4], PB
                        else:
                            dve.wait_ge(softmax_read, t + 1)
                            dve.wait_ge(pv_done, t + 1)
                            f, o = small[u][0:S, 3:4], OB
                        dve.scalar_tensor_tensor(out=XNEW[0:S, :], in0=o[0:S, 0:D], scalar=f, in1=XN[0:S, dsl(t), :].rearrange("p a d -> p (a d)"),
                                                 op0=ALU.mult, op1=ALU.add).then_inc(updated if clipped else out_read, 1)
                        dve.wait_ge(updated if clipped else out_read, t + 1)
                        link(dve.bn_stats(bn[0:S, 0:6], XNEW[0:S, :]))
                        dve.tensor_scalar(XN[0:S, dsl(t), :].rearrange("p a d -> p (a d)"), XNEW[0:S, :], 1.0, None, ALU.mult)
                        link(dve.bn_aggr(bn[0:S, 6:8], bn[0:S, 0:6]))
                        dve.tensor_scalar(MV[0:S, dsl(t), :].rearrange("p a d -> p (a d)"), bn[0:S, 6:8], 1.0, None, ALU.mult)

                    def low_attended(t):
                        low(attended_at(t), ATTENDED_N, lambda r: dve.tensor_tensor(
                            ATL[:], r[:, 0:KD * S].rearrange("p (k s) -> p k s", k=KD), ATH[:].bitcast(F32), ALU.subtract))

                    def attend(t, u):
                        dve.wait_ge(pv_done, t + 1)
                        dve.tensor_scalar(ATT[0:S, :], OB[0:S, 0:D], small[u][0:S, 2:3], None, ALU.mult).then_inc(out_read, 1)

                    def step(t, u):
                        linked[:] = [0 if is_first(t) else CH * t - 2, 0]
                        sm = small[u]
                        if clipped:
                            def top_of(out, src0, work, after):
                                for r in range(7):
                                    src = src0 if r == 0 else work
                                    found = dve.max(out[0:S, 8 * r:8 * r + 8], src)
                                    if r == 0 and out is not top or r == 0 and not quick:
                                        link(found)
                                        maximum()
                                        for f in after.get(r, ()):
                                            f()
                                    else:
                                        link(found, after.get(r, ()))
                                    if r < 6:
                                        link(dve.match_replace(work, out[0:S, 8 * r:8 * r + 8], src, LOWEST))

                            def maximum():
                                dve.tensor_scalar(sm[0:S, 0:1], (cand if quick else top)[0:S, 0:1], -1.0, None, ALU.mult).then_inc(neg_max, 1)

                            def attend_before():
                                if not is_first(t):
                                    attend(t - 1, 1 - u)

                            def low_before():
                                if not is_first(t):
                                    low_attended(t - 1)
                            parts = prep_parts(t + 2) if prepares(t) else []
                            if quick:
                                held(scores_copied, t + 1)
                                src, at = SC[u][0:S, 0:MF], 0
                                segments = []
                                for n in range(3):
                                    w = MF >> (n + 1)
                                    dve.tensor_tensor(FOLD[0:S, at + w:at + 2 * w], src[:, 0:w], src[:, w:2 * w], ALU.min)
                                    link(dve.tensor_tensor(FOLD[0:S, at:at + w], src[:, 0:w], src[:, w:2 * w], ALU.max))
                                    segments += [(at + w + i * (w >> n), w >> n) for i in range(1 << n)]
                                    src, at = FOLD[0:S, at:at + w], at + 2 * w

                                def segment(n):
                                    a0, w = segments[n]
                                    dve.max(cand[0:S, 56 + 8 * n:64 + 8 * n], FOLD[0:S, a0:a0 + w])
                                after = {r: [lambda r=r: segment(r)] for r in range(6)}
                                after[5].append(lambda: segment(6))
                                after[6] = [attend_before]
                                top_of(cand, src, WORK[0:S, :], after)
                                top_of(top, cand[0:S, :], CWORK[0:S, :], {r: [part] for r, part in enumerate(parts)})
                                low_before()
                                link(dve.tensor_reduce(sm[0:S, 5:6], cand[0:S, 56:112].rearrange("p (n k) -> p n k", k=8)[:, :, 7:8],
                                                       AX.XY, ALU.max))
                                link(dve.tensor_scalar(sm[0:S, 6:7], sm[0:S, 5:6], top[0:S, CLIP_K - 1:CLIP_K], None, ALU.is_le))
                                dve.tensor_scalar(sm[0:S, 3:4], sm[0:S, 6:7], gains[0:S, 1:2], None, ALU.mult)
                                dve.tensor_scalar(exact[0:S, dsl(t)], sm[0:S, 6:7], 1.0, None, ALU.mult)
                            else:
                                held(scores_copied, t + 1)
                                top_of(top, SC[u][0:S, :], WORK[0:S, :],
                                       {2: (attend_before,), 3: parts[0:2], 4: parts[2:4], 5: parts[4:6], 6: parts[6:]})
                                low_before()
                                dve.tensor_scalar(sm[0:S, 3:4], redo_gain[0:S, dsl(t)], 1.0, None, ALU.mult)
                            dve.wait_ge(exps, t + 1)
                            if not is_first(t):
                                dve.wait_ge(pv_done, t)
                            dve.scalar_tensor_tensor(out=PR[0:S, 0:MW], in0=SC[u][0:S, 0:MW], scalar=top[0:S, CLIP_K - 1:CLIP_K],
                                                     in1=EXPS[0:S, :], op0=ALU.is_ge, op1=ALU.mult,
                                                     accum_out=sm[0:S, 1:2]).then_inc(probs, 1)
                            if not is_first(t):
                                update(t - 1, 1 - u)
                            dve.wait_ge(probs, t + 1)
                            link(dve.reciprocal(sm[0:S, 2:3], sm[0:S, 1:2]))
                            dve.tensor_scalar(sm[0:S, 4:5], sm[0:S, 2:3], 1.0, None, ALU.mult).then_inc(softmax_read, 1)
                        else:
                            dve.wait_ge(scores_copied, t + 1)
                            dve.tensor_reduce(sm[0:S, 0:1], SC[u][0:S, :], AX.X, ALU.max, negate=True).then_inc(neg_max, 1)
                            if not is_first(t):
                                update(t - 1, 1 - u)
                            dve.wait_ge(exps, t + 1)
                            link(dve.reciprocal(sm[0:S, 2:3], sm[0:S, 1:2]))
                            dve.tensor_tensor(sm[0:S, 3:4], sm[0:S, 2:3], gain_of[0:S, dsl(t)], ALU.mult).then_inc(softmax_read, 1)
                        for n in range(TG):
                            low(probs_at(t) + n, PROBS_N + n, lambda r, n=n: dve.tensor_tensor(
                                PTL[:, 4 * n:4 * n + 4, :], r[:, 0:4 * S].rearrange("p (c s) -> p c s", c=4),
                                PTH[:, 4 * n:4 * n + 4, :].bitcast(F32), ALU.subtract))
                        if prepares(t) and not clipped:
                            prep(t + 2)
                        assert linked[1] == (CH - 2 if is_first(t) else CH), linked

                    normalise(0)
                    prep(0)
                    prep(1)
                    steps(dve, step)
                    linked[:] = [CH * B - 2, 0]
                    if clipped:
                        attend(B - 1, 1)
                        low_attended(B - 1)
                    update(B - 1, 1)

        def find_redo():
            with ExitStack() as ctx:
                left = ctx.enter_context(nc.sbuf_tensor("left", [P, B], F32))
                count = ctx.enter_context(nc.sbuf_tensor("left_count", [P, 2], F32))
                total = ctx.enter_context(nc.psum_tensor("left_total", [P, 1], F32))
                redo_step, total_full = sem("redo_step"), sem("redo_total")
                blk = ctx.enter_context(nc.Block())

                @blk.tensor
                def _(pe):
                    pe.wait_ge(redo_step, 2)
                    pe.matmul(total[:, :], ones[0:S, :], count[0:S, 0:1], start=True, stop=True).then_inc(total_full, 1)

                @blk.vector
                def _(dve):
                    dve.tensor_scalar(left[0:S, :], exact[0:S, :], -1.0, 1.0, ALU.mult, ALU.add).then_inc(redo_step, 1)
                    dve.wait_ge(redo_step, 1)
                    dve.tensor_reduce(count[0:S, 0:1], left[0:S, :], AX.X, ALU.add).then_inc(redo_step, 1)
                    dve.tensor_scalar(redo_gain[0:S, :], left[0:S, :], gains[0:S, 1:2], None, ALU.mult)
                    dve.wait_ge(total_full, 1)
                    dve.tensor_scalar(count[:, 1:2], total[:, :], 0.5, None, ALU.is_ge).then_inc(redo_step, 1)
                    dve.wait_ge(redo_step, 3)
                    dve.tensor_copy(any_redo[:], count[:, 1:2])

        def feed_forward(layer):
            L = f"f{layer}_"
            ternary = layer == 1
            EJ = P // E
            EC = EI // EJ
            SCN = -(-SI // P)
            if ternary:
                passes = [[("t", c) for c in range(FI // P)]]
            else:
                every = [("e", c) for c in range(EC)]
                passes = [every[n:n + 6] for n in range(0, EC, 6)] + [[("s", c) for c in range(SCN)]]
            NCM = max(len(p) for p in passes)
            assert all(len(p) % 2 == 0 for p in passes)
            T = B * S
            with ExitStack() as ctx:
                def sb(name, shape, dt=F32):
                    return ctx.enter_context(nc.sbuf_tensor(L + name, shape, dt))

                def bank(name):
                    return ctx.enter_context(nc.psum_tensor(L + name, [P, 512], F32))
                XH, XL = sb("XH", [P, KD, T], F32R), sb("XL", [P, KD, T], F32R)
                if not ternary:
                    YT = sb("YT", [P, KD, T])
                    CW = sb("CW", [P, T])
                WH = sb("WH", [P, NCM, 2 * KD, P], F32R)
                DH = sb("DH", [P, NCM, D], F32R)
                if not ternary:
                    WL, DL = sb("WL", [P, NCM, 2 * KD, P], F32R), sb("DL", [P, NCM, D], F32R)
                RG, RU = sb("RG", [P, NCM, D]), sb("RU", [P, NCM, D])
                RD = sb("RD", [P, KD, NCM * P])
                RDO = None if ternary else sb("RDO", [P, KD, NCM * P])
                GB_, UB_ = [bank("G0"), bank("G1")], [bank("U0"), bank("U1")]
                YB = [[bank(f"Y{u}{k}") for k in range(KD)] for u in range(2)]

                names = ("xhat", "turned", "high", "low", "plain", "logits", "read", "sink", "rstd", "eps", "gw_in", "gw_t",
                         "gw_s", "chain", "exp1", "iota_s", "picked")
                unused = ("plain", "logits", "read", "gw_in", "gw_t", "gw_s", "chain", "exp1", "iota_s", "picked") if ternary else ()
                (xhat, turned, high, low, plain, logits, read, sink, rstd_done, eps_done, gw_in, gw_t, gw_s, chain,
                 exp1, iota_s, picked) = (None if n in unused else sem(L + "n_" + n) for n in names)
                with ExitStack() as rctx:
                    def rb(name, shape, dt=F32):
                        return rctx.enter_context(nc.sbuf_tensor(L + name, shape, dt))
                    XHAT = [rb(f"XHAT{u}", [P, D]) for u in range(2)]
                    if not ternary:
                        NL_ = E + 1
                        XT = [rb(f"XT{u}", [P, KD, S]) for u in range(2)]
                        gw_raw = rb("gw_raw", [NL_, D])
                        gwT = rb("gwT", [P, KD, NL_])
                        LG = rb("LG", [P, B, NL_])
                        top = rb("top", [P, B, 8])
                        idx = rb("idx", [P, B, 8], U32)
                        idxf = rb("idxf", [P, B, 8])
                        iota = rb("iota", [P, B, E])
                        eq, sel = rb("eq", [P, B, E]), rb("sel", [P, B, E])
                        ex, sums = rb("ex", [P, B, E]), rb("sums", [P, B])
                        sig = rb("sig", [P, B])
                    with nc.Block() as blk:
                        @blk.sync
                        def _(sp):
                            if not ternary:
                                sp.dma_start(gw_raw[0:E, :], gate_w).then_inc(gw_in, 16)
                                sp.dma_start(gw_raw[E:E + 1, :], shared_gate_vec).then_inc(gw_in, 16)

                        @blk.gpsimd
                        def _(pool):
                            pool.wait_ge(eps_done, 1)
                            pool.tensor_tensor(RSTD[0:S, :], VEPS[0:S, :], MHALF[0:S, :], ALU.pow).then_inc(rstd_done, 1)
                            if not ternary:
                                pool.iota(iota[:], pattern=[[0, B], [1, E]], base=0, channel_multiplier=0,
                                          allow_small_or_imprecise_dtypes=True).then_inc(iota_s, 1)

                        def pairs(step):
                            def run(eng):
                                step(0, 0)
                                step(1, 1)
                                with eng.Fori(1, B // 2) as j:
                                    step(2 * j, 0)
                                    step(2 * j + 1, 1)
                            return run

                        @blk.tensor
                        def _(pe):
                            if not ternary:
                                pe.wait_ge(gw_in, 32)
                                for k in range(KD):
                                    last = pe.transpose(YB[0][0][:, k * NL_:(k + 1) * NL_], gw_raw[:, k * P:(k + 1) * P], ident[0:NL_, 0:NL_])
                                last.then_inc(gw_t, 1)
                                pe.wait_ge(gw_s, 1)

                            def step(b, u):
                                pe.wait_ge(xhat, b + 1)
                                if not (isinstance(b, int) and b < 2):
                                    pe.wait_ge(low, b - 1)
                                for k in range(KD):
                                    last = pe.transpose(GB_[u][:, k * S:(k + 1) * S], XHAT[u][0:S, k * P:(k + 1) * P], ident[0:S, 0:S])
                                last.then_inc(turned, 1)
                                if not ternary:
                                    pe.wait_ge(plain, b + 1)
                                    if not (isinstance(b, int) and b < 2):
                                        pe.wait_ge(read, b - 1)
                                    for k in range(KD):
                                        last = pe.matmul(UB_[u][0:S, 0:NL_], XT[u][:, k, :], gwT[:, k, :], start=k == 0, stop=k == KD - 1)
                                    last.then_inc(logits, 1)
                            pairs(step)(pe)

                        @blk.scalar
                        def _(act):
                            def step(b, u):
                                r = GB_[u][:, 0:KD * S].rearrange("p (k s) -> p k s", k=KD)
                                act.wait_ge(turned, b + 1)
                                if not ternary:
                                    if not (isinstance(b, int) and b < 2):
                                        act.wait_ge(logits, b - 1)
                                    act.copy(XT[u][:], r).then_inc(plain, 1)
                                act.sem_inc(sink, 1)
                                act.activation(XH[:, :, cols(b, S)], r, ACT.Copy).then_inc(high, 1)
                            pairs(step)(act)
                            if not ternary:
                                act.wait_ge(chain, 1)
                                act.activation(ex[0:S], ex[0:S], ACT.Exp).then_inc(exp1, 1)
                                act.activation(sig[0:S], LG[0:S, :, E], ACT.Exp, scale=-1.0).then_inc(exp1, 1)

                        @blk.vector
                        def _(dve):
                            dve.tensor_scalar(VEPS[0:S, :], MV[0:S, :, 1], LN_EPS, None, ALU.add).then_inc(eps_done, 1)
                            if not ternary:
                                dve.wait_ge(gw_t, 1)
                                dve.tensor_copy(gwT[:], YB[0][0][:, 0:KD * NL_].rearrange("p (k e) -> p k e", k=KD)).then_inc(gw_s, 1)
                            dve.wait_ge(rstd_done, 1)

                            def normalise(b, u):
                                if not (isinstance(b, int) and b < 2):
                                    dve.wait_ge(turned, b - 1)
                                dve.tensor_scalar(XHAT[u][0:S, :], XN[0:S, dsl(b), :], MV[0:S, dsl(b), 0:1].rearrange("p a b -> p (a b)"),
                                                  RSTD[0:S, dsl(b)], ALU.subtract, ALU.mult).then_inc(xhat, 1)

                            def step(b, u, more=True):
                                if more:
                                    normalise(b + 1, 1 - u)
                                dve.wait_ge(high, b + 1)
                                dve.tensor_tensor(XL[:, :, cols(b, S)], GB_[u][:, 0:KD * S].rearrange("p (k s) -> p k s", k=KD),
                                                  XH[:, :, cols(b, S)].bitcast(F32), ALU.subtract).then_inc(low, 1)
                                if not ternary:
                                    dve.wait_ge(logits, b + 1)
                                    dve.tensor_scalar(LG[0:S, dsl(b), :].rearrange("p a e -> p (a e)"), UB_[u][0:S, 0:NL_], 1.0, None, ALU.mult).then_inc(read, 1)
                            normalise(0, 0)
                            step(0, 0)
                            step(1, 1)
                            with dve.Fori(1, B // 2 - 1) as j:
                                step(2 * j, 0)
                                step(2 * j + 1, 1)
                            step(B - 2, 0)
                            step(B - 1, 1, False)
                            if not ternary:
                                n = 0

                                def link(ins):
                                    nonlocal n
                                    n += 1
                                    ins.then_inc(picked, 1)
                                    dve.wait_ge(picked, n)
                                dve.wait_ge(read, B)
                                for b in range(B):
                                    last = dve.max(top[0:S, b, :], LG[0:S, b, 0:E])
                                link(last)
                                for b in range(B):
                                    last = dve.max_index(idx[0:S, b, :], top[0:S, b, :], LG[0:S, b, 0:E])
                                link(last)
                                dve.tensor_tensor(ex[0:S], LG[0:S, :, 0:E], top[0:S, :, 0:1].to_broadcast([S, B, E]),
                                                  ALU.subtract).then_inc(chain, 1)
                                link(dve.tensor_copy(idxf[0:S], idx[0:S]))
                                dve.wait_ge(iota_s, 1)
                                for k in range(TOP_EXPERTS):
                                    dst = sel if k == 0 else eq
                                    link(dve.tensor_tensor(dst[0:S], iota[0:S], idxf[0:S, :, k:k + 1].to_broadcast([S, B, E]), ALU.is_equal))
                                    if k:
                                        link(dve.tensor_tensor(sel[0:S], sel[0:S], eq[0:S], ALU.add))
                                dve.wait_ge(exp1, 2)
                                link(dve.tensor_tensor(sel[0:S], sel[0:S], ex[0:S], ALU.mult))
                                link(dve.tensor_reduce(sums[0:S], sel[0:S], AX.X, ALU.add))
                                link(dve.reciprocal(sums[0:S], sums[0:S]))
                                link(dve.tensor_tensor(CWN[0:S], sel[0:S], sums[0:S, :].rearrange("p (b o) -> p b o", o=1).to_broadcast([S, B, E]), ALU.mult))
                                link(dve.tensor_scalar(sig[0:S], sig[0:S], 1.0, None, ALU.add))
                                dve.reciprocal(SIGN[0:S], sig[0:S])

                names = ("raw_in", "w_full", "w_high", "w_low", "gu_full", "silu", "mid", "hid", "h_high", "h_low",
                         "down", "y_full", "y_read", "y_fin", "y_turned", "x_new", "zeroed", "tern", "sums3", "tot", "scales",
                         "wide", "cwt", "cws", "fsink", "ordered", "links")
                unused = ("w_high", "hid", "zeroed", "wide", "cwt", "cws", "fsink", "ordered") if ternary else \
                    ("tern", "sums3", "tot", "scales", "links")
                (raw_in, w_full, w_high, w_low, gu_full, silu, mid, hid, h_high, h_low, down, y_full, y_read,
                 y_fin, y_turned, x_new, zeroed, tern, sums3, tot, scales, wide, cwt, cws, fsink, ordered, links) = (
                    None if n in unused else sem(L + n) for n in names)
                with ExitStack() as hctx:
                    def hb(name, shape, dt=F32):
                        return hctx.enter_context(nc.sbuf_tensor(L + name, shape, dt))
                    HS = [hb(f"HS{u}", [P, GT]) for u in range(2)]
                    HH, HL = [hb(f"HH{u}", [P, GT], F32R) for u in range(2)], [hb(f"HL{u}", [P, GT], F32R) for u in range(2)]
                    YF = [hb(f"YF{u}", [P, KD, GT]) for u in range(2)] if ternary else [hb("YF", [P, KD, GT])] * 2
                    if ternary:
                        part, half_s = hb("part", [P, 4]), hb("half_s", [P, 16])
                        TM = hb("TM", [P, NCM, D])
                    else:
                        CX = hb("CX", [P, GB, P])
                    blk = hctx.enter_context(nc.Block())
                    before = [sum(len(p) for p in passes[:n]) for n in range(len(passes) + 1)]
                    groups = [0]
                    for p in passes:
                        groups.append(groups[-1] + len(p) + len(p) // 2)
                    raws = [0]
                    NP_ = len(passes)

                    def chunk_no(n, g, c):
                        return before[n] * NG + len(passes[n]) * g + c

                    def used(eng, n, g, c, nch):
                        per = nch - 1
                        base = sum(len(p) - 1 for p in passes[:n]) * NG
                        if c >= 2:
                            eng.wait_ge(down, base + per * g + c - 1)
                        elif not (isinstance(g, int) and g == 0):
                            if c == 0:
                                eng.wait_ge(down, base + per * g)
                            else:
                                eng.wait_ge(y_full, n * NG + g)

                    def over_groups(eng, step):
                        step(0, 0)
                        step(1, 1)
                        with eng.Fori(1, NG // 2) as j:
                            step(2 * j, 0)
                            step(2 * j + 1, 1)

                    @blk.sync
                    def _(sp):
                        total = 0
                        for n, chunks in enumerate(passes):
                            kind, c0, w = chunks[0][0], chunks[0][1], len(chunks)
                            if n:
                                sp.wait_ge(w_full, groups[n])
                            if kind == "s":
                                sp.wait_ge(zeroed, 3)
                            if kind == "e":
                                for e in range(E):
                                    for r, o in ((RG, 0), (RU, EI)):
                                        sp.dma_start(r[e * EJ:(e + 1) * EJ, 0:w, :],
                                                     expert_gate_up[e, o + c0 * EJ:o + (c0 + w) * EJ, :].rearrange("(c j) d -> j c d", j=EJ)).then_inc(raw_in, 16)
                                    for k in range(KD):
                                        sp.dma_start(RD[:, k, e * w * EJ:(e + 1) * w * EJ],
                                                     expert_down[e, k * P:(k + 1) * P, c0 * EJ:(c0 + w) * EJ]).then_inc(raw_in, 16)
                                total += 16 * E * (2 + KD)
                            else:
                                src_g, src_u, src_d, rows = (W_up, W_gate, W_down, FI) if kind == "t" else \
                                    (shared_gate_up[0:SI, :], shared_gate_up[SI:2 * SI, :], shared_down, SI)
                                full, rest = rows // P, rows % P
                                for r, src in ((RG, src_g), (RU, src_u)):
                                    sp.dma_start(r[:, 0:full, :], src[0:full * P, :].rearrange("(c p) d -> p c d", p=P)).then_inc(raw_in, 16)
                                    if rest:
                                        sp.dma_start(r[0:rest, full, :], src[full * P:rows, :]).then_inc(raw_in, 16)
                                sp.dma_start(RD[:, :, 0:rows], src_d.rearrange("(k p) i -> p k i", p=P)).then_inc(raw_in, 16)
                                total += 16 * (3 + 2 * (rest > 0))
                            raws.append(total)

                    @blk.gpsimd
                    def _(pool):
                        for n, chunks in enumerate(passes):
                            if not ternary and n == NP_ - 2:
                                pool.wait_ge(hid, before[n] * NG)
                                pool.wait_ge(w_full, groups[n + 1])
                                pool.memset(RG[SI % P:P, SCN - 1, :], 0.0).then_inc(zeroed, 1)
                                pool.memset(RU[SI % P:P, SCN - 1, :], 0.0).then_inc(zeroed, 1)
                                pool.wait_ge(zeroed, 2)
                                pool.memset(RD[:, :, SI:SCN * P], 0.0).then_inc(zeroed, 1)
                                pool.wait_ge(zeroed, 3)
                            if ternary:
                                continue
                            if n == 0:
                                pool.wait_ge(cws, NG)
                            if chunks[0][0] == "s":
                                pool.wait_ge(cws, 2 * NG)

                            def step(g, u):
                                for c in range(len(chunks)):
                                    pool.wait_ge(mid, chunk_no(n, g, c) + 1)
                                    pool.sem_inc(fsink, 1)
                                    pool.tensor_tensor(HS[c % 2][:], HS[c % 2][:], CW[:, cols(g, GT)], ALU.mult).then_inc(hid, 1)
                            over_groups(pool, step)

                    @blk.tensor
                    def _(pe):
                        ring = [GB_[0], GB_[1]]
                        if ternary:
                            pe.wait_ge(sums3, 3)
                            pe.matmul(YB[0][0][:, 0:3], ones[:], part[:, 0:3], start=True, stop=True).then_inc(tot, 1)
                            pe.wait_ge(tern, 3)

                        def combining(lo):
                            for g in range(NG):
                                pe.wait_ge(wide, lo + g + 1)
                                if g >= 2:
                                    pe.wait_ge(cws, lo + g - 1)
                                for i in range(GB):
                                    last = pe.transpose(UB_[g % 2][:, i * S:(i + 1) * S], CX[0:S, i, :], ident[0:S, 0:S])
                                last.then_inc(cwt, 1)

                        for n, chunks in enumerate(passes):
                            nch = len(chunks)
                            if not ternary and n == 0:
                                combining(0)
                            if not ternary and chunks[0][0] == "s":
                                combining(NG)
                            pe.wait_ge(raw_in, raws[n + 1])
                            if chunks[0][0] == "s":
                                pe.wait_ge(zeroed, 3)
                            if n:
                                pe.wait_ge(mid, before[n] * NG)
                            r = groups[n]
                            for c in range(nch):
                                if r >= 2:
                                    pe.wait_ge(w_low, r - 1)
                                for m, raw in enumerate((RG, RU)):
                                    for k in range(KD):
                                        src = raw[:, c, k * P:(k + 1) * P]
                                        last = pe.transpose(ring[r % 2][:, (m * KD + k) * P:(m * KD + k + 1) * P], src, ident[:])
                                last.then_inc(w_full, 1)
                                r += 1
                            if chunks[0][0] == "e":
                                pe.wait_ge(ordered, n + 1)
                            for c in range(0, nch, 2):
                                pe.wait_ge(w_low, r - 1)
                                for i in range(2):
                                    for k in range(KD):
                                        src = (RDO if chunks[0][0] == "e" else RD)[:, k, (c + i) * P:(c + i + 1) * P]
                                        last = pe.transpose(ring[r % 2][:, (i * KD + k) * P:(i * KD + k + 1) * P], src, ident[:])
                                last.then_inc(w_full, 1)
                                r += 1
                            pe.wait_ge(w_low, r)
                            last_pass = n == NP_ - 1
                            gu_parts = ((WH, XH), (WH, XL)) if ternary else ((WH, XH), (WH, XL), (WL, XH))

                            def hidden(g, c, chunks=chunks, n=n):
                                i = chunk_no(n, g, c)
                                if c >= 2:
                                    pe.wait_ge(mid, i - 1)
                                elif not (isinstance(g, int) and g == 0):
                                    pe.wait_ge(mid, i - 1)
                                for m, bk in enumerate((GB_[c % 2], UB_[c % 2])):
                                    first = True
                                    for k in range(KD):
                                        for w, xx in gu_parts:
                                            last = pe.matmul(bk[:, 0:GT], w[:, c, m * KD + k, :], xx[:, k, cols(g, GT)], start=first,
                                                             stop=k == KD - 1 and (w, xx) == gu_parts[-1])
                                            first = False
                                last.then_inc(gu_full, 1)

                            def project(g, u, c, nch=nch, n=n):
                                i = chunk_no(n, g, c)
                                pe.wait_ge(h_low, i + 1)
                                if c == 0 and not (isinstance(g, int) and g < 2 and n == 0):
                                    if last_pass:
                                        if not (isinstance(g, int) and g < 2):
                                            pe.wait_ge(x_new, GB * (g - 1))
                                        else:
                                            pe.wait_ge(y_read, n * NG)
                                    else:
                                        pe.wait_ge(y_read, n * NG + g - 1)
                                parts = ((DH, HH), (DH, HL)) if ternary else ((DH, HH), (DH, HL), (DL, HH))
                                for k in range(KD):
                                    for w, h in parts:
                                        last = pe.matmul(YB[u][k][:, 0:GT], w[:, c, k * P:(k + 1) * P], h[c % 2][:], start=c == 0 and (w, h) == parts[0],
                                                         stop=c == nch - 1 and (w, h) == parts[-1])
                                last.then_inc(y_full if c == nch - 1 else down, 1)

                            def turn_out(g, u):
                                pe.wait_ge(y_fin, g + 1)
                                for i in range(GB):
                                    for k in range(KD):
                                        o = YB[u][i // 2][0:S, (i % 2) * D + k * P:(i % 2) * D + (k + 1) * P]
                                        last = pe.transpose(o, YF[u][:, k, i * S:(i + 1) * S], ident[:])
                                last.then_inc(y_turned, 1)

                            def step(g, u):
                                first = isinstance(g, int) and g == 0
                                for c in range(nch):
                                    hidden(g, c)
                                    if c >= 2:
                                        project(g, u, c - 2)
                                    elif not first:
                                        project(g - 1, 1 - u, nch - 2 + c)
                                    if last_pass and c == nch - 1 and not first:
                                        turn_out(g - 1, 1 - u)
                            over_groups(pe, step)
                            project(NG - 1, 1, nch - 2)
                            project(NG - 1, 1, nch - 1)
                            if last_pass:
                                turn_out(NG - 1, 1)

                    @blk.scalar
                    def _(act):
                        def combining(lo):
                            for g in range(NG):
                                act.wait_ge(cwt, lo + g + 1)
                                if lo and g == 0:
                                    act.wait_ge(hid, before[NP_ - 1] * NG)
                                act.copy(CW[:, g * GT:(g + 1) * GT], UB_[g % 2][:, 0:GT]).then_inc(cws, 1)

                        for n, chunks in enumerate(passes):
                            nch = len(chunks)
                            if not ternary and n == 0:
                                combining(0)
                            if not ternary and chunks[0][0] == "s":
                                combining(NG)
                            if n:
                                act.wait_ge(y_full, n * NG)
                            r = groups[n]
                            if chunks[0][0] == "e":
                                act.wait_ge(raw_in, raws[n + 1])
                                for k in range(KD):
                                    ins = act.copy(RDO[:, k, 0:nch * P].rearrange("p (c e j) -> p e c j", e=E, j=EJ),
                                                   RD[:, k, 0:nch * P].rearrange("p (e c j) -> p e c j", e=E, j=EJ))
                                ins.then_inc(ordered, 1)
                            for c in range(nch):
                                act.wait_ge(w_full, r + 1)
                                ins = act.copy(WH[:, c, :, :], GB_[r % 2][:, :].rearrange("p (m u) -> p m u", m=2 * KD))
                                ins.then_inc(w_low if ternary else w_high, 1)
                                r += 1
                            for c in range(0, nch, 2):
                                act.wait_ge(w_full, r + 1)
                                ins = act.copy(DH[:, c:c + 2, :], GB_[r % 2][:, :].rearrange("p (c d) -> p c d", c=2))
                                ins.then_inc(w_low if ternary else w_high, 1)
                                r += 1

                            def split_high(g, c, n=n):
                                i = chunk_no(n, g, c)
                                act.wait_ge(mid if ternary else hid, i + 1)
                                used(act, n, g, c, nch)
                                act.copy(HH[c % 2][:], HS[c % 2][:]).then_inc(h_high, 1)

                            def step(g, u, n=n):
                                first = isinstance(g, int) and g == 0
                                for c in range(nch):
                                    i = chunk_no(n, g, c)
                                    act.wait_ge(gu_full, i + 1)
                                    if not (isinstance(i, int) and i < 2):
                                        act.wait_ge(h_low, i - 1)
                                    act.activation(HS[c % 2][:], GB_[c % 2][:, 0:GT], ACT.Silu,
                                                   **({"scale": half_s[:, 3:4]} if ternary else {})).then_inc(silu, 1)
                                    if c:
                                        split_high(g, c - 1)
                                    elif not first:
                                        split_high(g - 1, nch - 1)
                            if ternary:
                                act.wait_ge(scales, 1)
                            over_groups(act, step)
                            split_high(NG - 1, nch - 1)

                    @blk.vector
                    def _(dve):
                        if ternary:
                            dve.wait_ge(raw_in, raws[1])
                            for m, raw in enumerate((RG, RU, RD)):
                                dve.tensor_reduce(part[:, m:m + 1], raw[:], AX.XY, ALU.add, apply_absolute_value=True).then_inc(sums3, 1)
                            dve.wait_ge(tot, 1)
                            n = 0

                            def link(ins):
                                nonlocal n
                                n += 1
                                ins.then_inc(links, 1)
                                dve.wait_ge(links, n)
                            link(dve.tensor_scalar(half_s[:, 3:6], YB[0][0][:, 0:3], 1.0 / (FI * D), TERNARY_EPS, ALU.mult, ALU.add))
                            link(dve.tensor_scalar(half_s[:, 6:9], half_s[:, 3:6], 0.5, None, ALU.mult))
                            link(dve.tensor_scalar(half_s[:, 9:12], half_s[:, 3:6], -0.5, None, ALU.mult))
                            link(dve.tensor_scalar(half_s[:, 0:1], half_s[:, 4:5], half_s[:, 5:6], gains[:, 3:4], ALU.mult, ALU.mult))
                            dve.tensor_scalar(half_s[:, 1:2], half_s[:, 0:1], 1.0, None, ALU.mult).then_inc(scales, 1)
                            for m, raw in enumerate((RG, RU, RD)):
                                flat = TM[:].rearrange("p c d -> p (c d)")
                                rf = raw[:].rearrange("p c d -> p (c d)")
                                link(dve.tensor_scalar(flat, rf, half_s[:, 9 + m:10 + m], None, ALU.is_lt))
                                dve.scalar_tensor_tensor(out=rf, in0=rf, scalar=half_s[:, 6 + m:7 + m], in1=flat,
                                                         op0=ALU.is_gt, op1=ALU.subtract).then_inc(tern, 1)
                                dve.wait_ge(tern, m + 1)
                        gain = half_s[:, 0:1] if ternary else gains[:, 2:3]

                        def combining(src, lo):
                            for g in range(NG):
                                if lo + g:
                                    dve.wait_ge(cwt, lo + g)
                                w = src(g)
                                dve.tensor_copy(CX[0:S, :, :].rearrange("p b (e j) -> p b e j", j=w[1]), w[0]).then_inc(wide, 1)

                        for n, chunks in enumerate(passes):
                            nch = len(chunks)
                            last_pass = n == NP_ - 1
                            if not ternary and n == 0:
                                combining(lambda g: (CWN[0:S, g * GB:(g + 1) * GB, :].rearrange("p b (e o) -> p b e o", o=1).to_broadcast([S, GB, E, EJ]), EJ), 0)
                            if not ternary and chunks[0][0] == "s":
                                combining(lambda g: (SIGN[0:S, g * GB:(g + 1) * GB].rearrange("p (b e o) -> p b e o", e=1, o=1).to_broadcast([S, GB, 1, P]), P), NG)
                            if not ternary:
                                r = groups[n]
                                for c in range(nch):
                                    dve.wait_ge(w_high, r + 1)
                                    dve.tensor_tensor(WL[:, c, :, :], GB_[r % 2][:, :].rearrange("p (m u) -> p m u", m=2 * KD),
                                                      WH[:, c, :, :].bitcast(F32), ALU.subtract).then_inc(w_low, 1)
                                    r += 1
                                for c in range(0, nch, 2):
                                    dve.wait_ge(w_high, r + 1)
                                    dve.tensor_tensor(DL[:, c:c + 2, :], GB_[r % 2][:, :].rearrange("p (c d) -> p c d", c=2),
                                                      DH[:, c:c + 2, :].bitcast(F32), ALU.subtract).then_inc(w_low, 1)
                                    r += 1

                            def split_low(g, c, n=n):
                                dve.wait_ge(h_high, chunk_no(n, g, c) + 1)
                                used(dve, n, g, c, nch)
                                dve.tensor_tensor(HL[c % 2][:], HS[c % 2][:], HH[c % 2][:].bitcast(F32), ALU.subtract).then_inc(h_low, 1)

                            def collect(g, u, n=n):
                                dve.wait_ge(y_full, n * NG + g + 1)
                                if last_pass:
                                    if not (isinstance(g, int) and g < (2 if ternary else 1)):
                                        dve.wait_ge(y_turned, g - 1 if ternary else g)
                                for k in range(KD):
                                    y = YB[u][k][:, 0:GT]
                                    if ternary:
                                        ins = dve.tensor_scalar(YF[u][:, k, :], y, 1.0, None, ALU.mult)
                                    elif n == 0:
                                        ins = dve.tensor_scalar(YT[:, k, cols(g, GT)], y, 1.0, None, ALU.mult)
                                    else:
                                        ins = dve.tensor_tensor(YF[u][:, k, :] if last_pass else YT[:, k, cols(g, GT)], y, YT[:, k, cols(g, GT)], ALU.add)
                                ins.then_inc(y_fin if last_pass else y_read, 1)

                            def update(g, u):
                                dve.wait_ge(y_turned, g + 1)
                                for i in range(GB):
                                    xb = XN[0:S, dsl(GB * g + i), :].rearrange("p a d -> p (a d)")
                                    dve.scalar_tensor_tensor(out=xb, in0=YB[u][i // 2][0:S, (i % 2) * D:(i % 2 + 1) * D], scalar=gain[0:S],
                                                             in1=xb, op0=ALU.mult, op1=ALU.add).then_inc(x_new, 1)

                            def step(g, u, n=n):
                                first = isinstance(g, int) and g == 0
                                for c in range(nch):
                                    dve.wait_ge(silu, chunk_no(n, g, c) + 1)
                                    dve.tensor_tensor(HS[c % 2][:], HS[c % 2][:], UB_[c % 2][:, 0:GT], ALU.mult).then_inc(mid, 1)
                                    if c:
                                        split_low(g, c - 1)
                                    elif not first:
                                        split_low(g - 1, nch - 1)
                                    if c == 2 and not first:
                                        collect(g - 1, 1 - u)
                                if last_pass and not first:
                                    update(g - 1, 1 - u)
                            over_groups(dve, step)
                            split_low(NG - 1, nch - 1)
                            collect(NG - 1, 1)
                            if last_pass:
                                update(NG - 1, 1)

        def token_stats():
            with nc.sbuf_tensor("stats_again", [P, B, 6], F32) as stats:
                stat_done = sem("stat_again_done")
                with nc.Block() as blk:
                    @blk.vector
                    def _(dve):
                        for b in range(B):
                            last = dve.bn_stats(stats[0:S, b, :], XN[0:S, b, :])
                        last.then_inc(stat_done, 1)
                        dve.wait_ge(stat_done, 1)
                        for b in range(B):
                            dve.bn_aggr(MV[0:S, b, :], stats[0:S, b, :])

        def cols(n, width):
            return slice(n * width, (n + 1) * width) if isinstance(n, int) else bass.ds(n * width, width)

        def half(b, p):
            return b // 2 if isinstance(b, int) else halves(b, p)

        def halves(b, p):
            return (b - p) // 2

        def dcol(n):
            return slice(n, n + 1) if isinstance(n, int) else bass.ds(n, 1)

        def dsl(b):
            return slice(b, b + 1) if isinstance(b, int) else bass.ds(b, 1)

        def dyn(t, b):
            return t[b] if isinstance(b, int) else t[bass.ds(b, 1)].rearrange("a m d -> (a m) d")

        def dynrow(t, b):
            return t[dsl(b), :]

        def store():
            stored = sem("stored")
            with nc.Block() as blk:
                @blk.sync
                def _(sp):
                    sp.dma_start(out.rearrange("b s d -> s b d"), XN[0:S, :, :]).then_inc(stored, 16)
                    sp.wait_ge(stored, 16)


        setup()
        attention(0, picked=True)
        clear_attention_sems()
        attention(0, guard=any_long[0:1, 0:1])
        clear_attention_sems()
        picking.close()
        feed_forward(0)
        token_stats()
        attention(1)
        clear_attention_sems()
        find_redo()
        attention(1, guard=any_redo[0:1, 0:1])
        feed_forward(1)
        store()


_INS = ['x', 'ctx_2048', 'mask_BxS2_bk0', 'g_xattn', 'g_ffn', 'L0_ffn_gate_w', 'L0_ffn_expert_gate_up',
        'L0_ffn_expert_down', 'L0_ffn_shared_gate_up', 'L0_ffn_shared_down', 'L0_ffn_shared_gate_vec',
        'L1_xattn_W_qkv', 'L1_xattn_W_o', 'L1_xattn_beta_q', 'L1_xattn_beta_k', 'L1_xattn_gate',
        'L1_xattn_log_tau', 'L1_ffn_W_up', 'L1_ffn_W_gate', 'L1_ffn_W_down']


def kernel(**inputs):
    import numpy as _np
    import concourse.bacc as _bacc
    from concourse import mybir as _mybir
    from concourse.bass_utils import run_bass_kernel_spmd as _run

    nc = _bacc.Bacc("TRN2", target_bir_lowering=False, num_devices=1)
    arrays, args = {}, []
    for name in _INS:
        a = _np.ascontiguousarray(inputs[name])
        a = a.reshape(1) if a.ndim == 0 else a
        arrays[f"in_{name}_dram"] = a
        args.append(nc.dram_tensor(f"in_{name}_dram", a.shape, _mybir.dt.from_np(a.dtype), kind="ExternalInput").ap())
    args.append(nc.dram_tensor("out_0_dram", inputs['x'].shape, _mybir.dt.float32, kind="ExternalOutput").ap())
    flamingo_kernel(nc, *args)
    r = _run(nc, [arrays], core_ids=[0])
    return r.results[0]["out_0_dram"]
```

```python
from contextlib import ExitStack

import concourse.bass as bass
from concourse import mybir

ALU = mybir.AluOpType
ACT = mybir.ActivationFunctionType
AX = mybir.AxisListType
F32 = mybir.dt.float32
F32R = mybir.dt.float32r
BF16 = mybir.dt.bfloat16
U8 = mybir.dt.uint8
U32 = mybir.dt.uint32
I32 = mybir.dt.int32

P = 128
NEG = -1.0e30
LOWEST = -3.0e38
LN_EPS = 1e-5
TERNARY_EPS = 1e-8
CLIP_K = 54
TOP_EXPERTS = 4
HEAD = 4
SLOTS = 4


def flamingo_kernel(nc, x, ctx_mem, mask, g_xattn, g_ffn, gate_w, expert_gate_up, expert_down,
                    shared_gate_up, shared_down, shared_gate_vec, W_qkv, W_o, beta_q, beta_k, gate,
                    log_tau, W_up, W_gate, W_down, out):
    B, S, D = x.shape
    M = ctx_mem.shape[1]
    KD = D // P
    MC = -(-M // P)
    MT = M - (MC - 1) * P
    SB = -(-M // 3)
    SB += SB % 2
    SCOLS = [(0, SB), (SB, SB), (2 * SB, M - 2 * SB)]
    E = gate_w.shape[0]
    EI = expert_down.shape[2]
    SI = shared_down.shape[1]
    FI = W_up.shape[0]
    MF = -(-M // 32) * 32
    GB = 4
    NG = B // GB
    GT = GB * S

    mask_bias_dram = nc.dram_tensor("mask_bias", (B, M), BF16, kind="Internal").ap()

    places_dram = nc.dram_tensor("places_dram", (B, SLOTS), I32, kind="Internal").ap()
    context_rows = ctx_mem.rearrange("b m d -> (b m) d")

    with ExitStack() as whole:
        def sem(name):
            return whole.enter_context(nc.semaphore(name))

        attention_sems = {}

        def attention_sem(name):
            if name not in attention_sems:
                attention_sems[name] = sem("attn_" + name)
            return attention_sems[name]

        def clear_attention_sems():
            with nc.Block() as blk:
                @blk.gpsimd
                def _(pool):
                    for s in attention_sems.values():
                        pool.sem_clear(s)

        def keep(name, shape, dt=F32):
            return whole.enter_context(nc.sbuf_tensor(name, shape, dt))

        XN = keep("XN", [P, B, D])
        MV = keep("MV", [P, B, 2])
        RSTD = keep("RSTD", [P, B])
        VEPS = keep("VEPS", [P, B])
        MHALF = keep("MHALF", [P, B])
        ident = keep("ident", [P, P])
        ones = keep("ones", [P, P])
        gains = keep("gains", [P, 4])
        coef = keep("coef", [P, 1])
        CWN = keep("CWN", [P, B, E])
        SIGN = keep("SIGN", [P, B])
        exact = keep("exact", [P, B])
        redo_gain = keep("redo_gain", [P, B])
        any_redo = keep("any_redo", [P, 1], I32)
        picking = whole.enter_context(ExitStack())

        def pick(name, shape, dt=F32):
            return picking.enter_context(nc.sbuf_tensor(name, shape, dt))

        short_gain, long_gain = pick("short_gain", [P, B]), pick("long_gain", [P, B])
        places = pick("places", [1, B * SLOTS], I32)
        picked_bias = pick("picked_bias", [P, SLOTS * P], BF16)
        pick_row = pick("pick_row", [P, B * S], BF16)
        any_long = pick("any_long", [P, 1], I32)

        def setup():
            with ExitStack() as ctx:
                def sb(name, shape, dt=F32):
                    return ctx.enter_context(nc.sbuf_tensor(name, shape, dt))
                mask_u8 = sb("mask_u8", [B, M], U8)
                mask_bias = sb("mask_bias_sb", [B, M], BF16)
                any_valid = sb("any_valid", [B, 1])
                wide = sb("wide", [B, 2, P])
                chunk_bias = sb("chunk_bias_sb", [B, MC, P], BF16)
                act, iota_c, key = sb("act", [B, MC]), sb("iota_c", [B, MC]), sb("key", [B, MC])
                best, ge, ids = sb("best", [B, 8]), sb("ge", [B, 8]), sb("ids", [B, 8])
                n_act, is_short = sb("n_act", [B, 1]), sb("is_short", [B, 1])
                row_of = sb("row_of", [B, 1])
                place = sb("place", [B, SLOTS], I32)
                here = sb("here", [B, SLOTS, MC])
                start = sb("start", [B, SLOTS])
                vg, shorts, not_short = sb("vg", [P, B]), sb("shorts", [P, B]), sb("not_short", [P, B])
                flags = sb("flags", [P, 1])
                g_raw = sb("g_raw", [P, 4])
                sc = sb("sc", [P, 16])
                stats = sb("stats", [P, B, 6])
                pv = ctx.enter_context(nc.psum_tensor("pv_valid", [P, 2, B], F32))
                x_in, small_in, mask_in = sem("x_in"), sem("small_in"), sem("mask_in")
                consts, v_step, a_step = sem("consts"), sem("setup_v"), sem("setup_a")
                wide_t, bias_out, stat_done = sem("wide_t"), sem("bias_out"), sem("stat_done")
                blk = ctx.enter_context(nc.Block())

                @blk.sync
                def _(sp):
                    sp.dma_start(mask_u8[:], mask).then_inc(mask_in, 16)
                    sp.dma_start(g_raw[:, 0:2], bass_bcast(g_xattn, 2)).then_inc(small_in, 16)
                    sp.dma_start(g_raw[:, 2:4], bass_bcast(g_ffn, 2)).then_inc(small_in, 16)
                    for n, t in enumerate((gate, beta_q, beta_k, log_tau)):
                        sp.dma_start(sc[:, n:n + 1], bass_bcast(t, 1)).then_inc(small_in, 16)
                    for n in range(4):
                        q = B // 4
                        sp.dma_start(XN[0:S, n * q:(n + 1) * q, :],
                                     x[n * q:(n + 1) * q].rearrange("b s d -> s b d")).then_inc(x_in, 16)
                    sp.wait_ge(v_step, 8)
                    sp.dma_start(mask_bias_dram, mask_bias[:]).then_inc(bias_out, 16)
                    sp.dma_start(places_dram, place[:]).then_inc(bias_out, 16)
                    sp.wait_ge(bias_out, 32)
                    sp.dma_start(places[:], places_dram.rearrange("(a b) c -> a (b c)", a=1)).then_inc(bias_out, 16)
                    sp.wait_ge(bias_out, 48)

                @blk.gpsimd
                def _(pool):
                    pool.memset(ident[:], 0.0).then_inc(consts, 1)
                    pool.memset(ones[:], 1.0).then_inc(consts, 1)
                    pool.memset(MHALF[:], -0.5).then_inc(consts, 1)
                    pool.wait_ge(consts, 3)
                    pool.affine_select(out=ident[:], in_=ident[:], compare_op=ALU.not_equal, fill=1.0, base=0,
                                       pattern=[[-1, P]], channel_multiplier=1).then_inc(consts, 1)
                    pool.iota(iota_c[:], pattern=[[1, MC]], base=0, channel_multiplier=0, allow_small_or_imprecise_dtypes=True).then_inc(consts, 1)
                    pool.iota(row_of[:], pattern=[[0, 1]], base=0, channel_multiplier=M, allow_small_or_imprecise_dtypes=True).then_inc(consts, 1)
                    pool.memset(picked_bias[:], 0.0).then_inc(consts, 1)
                    pool.memset(pick_row[:], 0.0).then_inc(consts, 1)
                    pool.wait_ge(consts, 8)
                    pool.affine_select(out=pick_row[:].rearrange("p (b s) -> p b s", s=S), in_=pick_row[:].rearrange("p (b s) -> p b s", s=S),
                                       compare_op=ALU.not_equal, fill=1.0, base=0, pattern=[[-1, B], [0, S]], channel_multiplier=1).then_inc(consts, 1)

                @blk.scalar
                def _(act):
                    act.wait_ge(small_in, 96)
                    act.activation(gains[:], g_raw[:], ACT.Tanh).then_inc(a_step, 1)
                    act.activation(sc[:, 4:5], sc[:, 0:1], ACT.Exp, scale=-1.0).then_inc(a_step, 1)
                    act.activation(sc[:, 5:6], sc[:, 3:4], ACT.Exp).then_inc(a_step, 1)

                @blk.tensor
                def _(pe):
                    pe.wait_ge(consts, 4)
                    pe.wait_ge(v_step, 14 + MC)
                    pe.transpose(pv[:, 0, :], wide[:, 0, :], ident[0:B, 0:B])
                    pe.transpose(pv[:, 1, :], wide[:, 1, :], ident[0:B, 0:B]).then_inc(wide_t, 1)

                @blk.vector
                def _(dve):
                    n = 0

                    def chain(ins):
                        nonlocal n
                        n += 1
                        ins.then_inc(v_step, 1)
                        dve.wait_ge(v_step, n)
                    dve.wait_ge(mask_in, 16)
                    chain(dve.tensor_scalar(mask_bias[:], mask_u8[:], 1.0, -NEG, ALU.subtract, ALU.mult))
                    dve.memset(chunk_bias[:, MC - 1, 0:P - MT], NEG)
                    dve.tensor_copy(chunk_bias[:, MC - 1, P - MT:P], mask_bias[:, (MC - 1) * P:M])
                    dve.tensor_copy(chunk_bias[:, 0:MC - 1, :], mask_bias[:, 0:(MC - 1) * P].rearrange("b (c p) -> b c p", p=P))
                    dve.tensor_reduce(act[:, 0:MC - 1], mask_u8[:, 0:(MC - 1) * P].rearrange("b (c p) -> b c p", p=P), AX.X, ALU.max)
                    chain(dve.tensor_reduce(act[:, MC - 1:MC], mask_u8[:, (MC - 1) * P:M], AX.X, ALU.max))
                    dve.wait_ge(consts, 6)
                    chain(dve.scalar_tensor_tensor(out=key[:], in0=act[:], scalar=32.0, in1=iota_c[:], op0=ALU.mult, op1=ALU.add))
                    chain(dve.max(best[:], key[:]))
                    chain(dve.tensor_scalar(ge[:], best[:], 32.0, None, ALU.is_ge))
                    chain(dve.scalar_tensor_tensor(out=ids[:], in0=ge[:], scalar=-32.0, in1=best[:], op0=ALU.mult, op1=ALU.add))
                    chain(dve.tensor_scalar(start[:], ids[:, 0:SLOTS], float(P), float(M - P), ALU.mult, ALU.min))
                    chain(dve.tensor_scalar(place[:, 0:SLOTS], start[:], row_of[:, 0:1], None, ALU.add))
                    for n_ in range(SLOTS):
                        last = dve.tensor_scalar(here[:, n_, :], iota_c[:], ids[:, n_:n_ + 1], None, ALU.is_equal)
                    dve.wait_ge(consts, 9)
                    chain(last)
                    for c in range(MC):
                        for n_ in range(SLOTS):
                            o = picked_bias[0:B, n_ * P:(n_ + 1) * P]
                            last = dve.scalar_tensor_tensor(out=o, in0=chunk_bias[:, c, :], scalar=here[:, n_, c:c + 1], in1=o,
                                                            op0=ALU.mult, op1=ALU.add)
                        chain(last)
                    chain(dve.tensor_reduce(any_valid[:], act[:], AX.X, ALU.max))
                    chain(dve.tensor_reduce(n_act[:], act[:], AX.X, ALU.add))
                    chain(dve.tensor_scalar(is_short[:], n_act[:], float(SLOTS), None, ALU.is_le))
                    chain(dve.tensor_scalar(wide[:, 0, :], ones[0:B, :], any_valid[:, 0:1], None, ALU.mult))
                    chain(dve.tensor_scalar(wide[:, 1, :], ones[0:B, :], is_short[:, 0:1], None, ALU.mult))
                    dve.wait_ge(a_step, 3)
                    chain(dve.tensor_scalar(sc[:, 6:7], sc[:, 4:5], 1.0, None, ALU.add))
                    chain(dve.reciprocal(sc[:, 7:8], sc[:, 6:7]))
                    chain(dve.tensor_tensor(sc[:, 8:9], sc[:, 7:8], sc[:, 1:2], ALU.mult))
                    chain(dve.tensor_scalar(sc[:, 9:10], sc[:, 7:8], -1.0, 1.0, ALU.mult, ALU.add))
                    chain(dve.tensor_tensor(sc[:, 10:11], sc[:, 9:10], sc[:, 2:3], ALU.mult))
                    chain(dve.tensor_tensor(sc[:, 11:12], sc[:, 8:9], sc[:, 10:11], ALU.add))
                    chain(dve.tensor_scalar(coef[:], sc[:, 11:12], float(D) ** -0.5, sc[:, 5:6], ALU.mult, ALU.mult))
                    dve.wait_ge(wide_t, 1)
                    chain(dve.tensor_scalar(vg[:], pv[:, 0, :], gains[:, 0:1], None, ALU.mult))
                    chain(dve.tensor_copy(shorts[:], pv[:, 1, :]))
                    chain(dve.tensor_scalar(not_short[:], shorts[:], -1.0, 1.0, ALU.mult, ALU.add))
                    dve.tensor_tensor(short_gain[:], vg[:], shorts[:], ALU.mult)
                    dve.tensor_tensor(long_gain[:], vg[:], not_short[:], ALU.mult)
                    chain(dve.tensor_reduce(flags[:], not_short[:], AX.X, ALU.max))
                    dve.tensor_copy(any_long[:], flags[:])
                    for q in range(4):
                        dve.wait_ge(x_in, 64)
                        for b in range(q * B // 4, (q + 1) * B // 4):
                            last = dve.bn_stats(stats[0:S, b, :], XN[0:S, b, :])
                    last.then_inc(stat_done, 1)
                    dve.wait_ge(stat_done, 1)
                    for b in range(B):
                        dve.bn_aggr(MV[0:S, b, :], stats[0:S, b, :])

        def bass_bcast(t, n):
            return t.partition_broadcast(P)

        def attention(layer, picked=False, guard=None):
            L = f"a{layer}{'p' if picked else 'q' if layer and guard is None else ''}_"
            clipped = layer == 1
            quick = clipped and guard is None
            NC = SLOTS if picked else MC
            MW = NC * P if picked else M
            NPAD = NC * P
            TG = NC // 4
            PREP = 1 + KD * TG
            R = PREP + TG + clipped
            NRING = 4 if picked else 3 if clipped else 2
            COLS = [(0, NPAD)] if picked else SCOLS
            masked_rows = not clipped and not picked
            gain_of = short_gain if picked else long_gain

            def guarded(body):
                def run(eng):
                    if guard is None:
                        body(eng)
                    else:
                        flag = eng.value_load(guard, min_val=0, max_val=1)
                        with eng.If(flag > 0):
                            body(eng)
                return run
            with ExitStack() as ctx:
                def sb(name, shape, dt=F32):
                    return ctx.enter_context(nc.sbuf_tensor(L + name, shape, dt))

                def bank(name):
                    return ctx.enter_context(nc.psum_tensor(L + name, [P, 512], F32))
                CR = [sb(f"CR{p}", [P, NC, D]) for p in range(2)]
                NH = [sb(f"NH{p}", [P, NC, D], F32R) for p in range(2)]
                NL = [sb(f"NL{p}", [P, NC, D], F32R) for p in range(2)]
                TH, TL = sb("TH", [P, KD, NPAD], F32R), sb("TL", [P, KD, NPAD], F32R)
                QH, QL = sb("QH", [P, KD, S], F32R), sb("QL", [P, KD, S], F32R)
                XHAT = sb("XHAT", [P, D])
                SC = [sb(f"SC{p}", [P, MF if quick else MW]) for p in range(2)]
                PR = sb("PR", [P, NPAD])
                PTH, PTL = sb("PTH", [P, NC, S], F32R), sb("PTL", [P, NC, S], F32R)
                small = [sb(f"small{p}", [P, 8]) for p in range(2)]
                bn = sb("bn", [P, 8])
                XNEW = sb("XNEW", [P, D])
                if clipped:
                    top = sb("top", [P, 56])
                    WORK = sb("WORK", [P, MF // 8 if quick else MW])
                    if quick:
                        FOLD = sb("FOLD", [P, MF * 7 // 4])
                        cand, CWORK = sb("cand", [P, 136]), sb("CWORK", [P, 136])
                    EXPS = sb("EXPS", [P, MW])
                    XTH, XTL = sb("XTH", [P, KD, S], F32R), sb("XTL", [P, KD, S], F32R)
                    ATT = sb("ATT", [P, D])
                    ATH, ATL = sb("ATH", [P, KD, S], F32R), sb("ATL", [P, KD, S], F32R)
                    wraw = sb("wraw", [P, 2, KD, D])
                    WH, WL = sb("WH", [P, 2, KD, D], F32R), sb("WL", [P, 2, KD, D], F32R)
                elif masked_rows:
                    BIAS = [sb(f"BIAS{p}", [P, MW], BF16) for p in range(2)]
                    row0 = sb("row0", [P, S], BF16)
                ring = [bank(f"ring{n}") for n in range(NRING)]
                SP = [bank(f"S{n}") for n in range(len(COLS))]
                OB = bank("O")
                both = bank("QP") if clipped else None
                PB, QB = (both[:, 0:D], both[:, D:D + KD * S]) if clipped else (None, None)

                ctx_in = [attention_sem("ctx_in0"), attention_sem("ctx_in1")]
                names = ("init", "rstd", "xhat", "ring_full", "ring_high", "ring_low", "scores_full", "scores_copied",
                         "neg_max", "exps", "probs", "softmax_read", "nat_high", "nat_low", "pv_done", "out_read",
                         "chain", "q_full", "q_high", "q_low", "proj_full", "updated", "w_in", "w_full",
                         "w_high", "w_low", "eps_done", "sink")
                unused = () if clipped else ("probs", "q_full", "q_high", "q_low", "proj_full", "updated", "w_in",
                                             "w_full", "w_high", "w_low")
                (init, rstd_done, xhat, ring_full, ring_high, ring_low, scores_full, scores_copied, neg_max, exps,
                 probs, softmax_read, nat_high, nat_low, pv_done, out_read, chain, q_full, q_high, q_low,
                 proj_full, updated, w_in, w_full, w_high, w_low, eps_done, sink) = (
                    None if n in unused else attention_sem(n) for n in names)
                blk = ctx.enter_context(nc.Block())
                LOADS = 16 * SLOTS if picked else 32 if clipped else 48

                def step_at(t):
                    return 2 * PREP + (R * t - 1 if not is_first(t) else 0) - (PREP * max(0, t - (B - 2)) if isinstance(t, int) else 0)

                def probs_at(t):
                    if clipped:
                        return step_at(t) + (PREP if prepares(t) else 0) + (0 if is_first(t) else 1)
                    return 2 * PREP + R * t - (PREP if isinstance(t, int) and t == B - 1 else 0)

                def prep_at(b):
                    return PREP * b if isinstance(b, int) and b < 2 else step_at(b - 2) if clipped else probs_at(b - 2) + TG

                def attended_at(t):
                    return step_at(t + 1) + (PREP if prepares(t + 1) else 0)

                PREP_N, PROBS_N, ATTENDED_N = (0, PREP + 1, PREP) if clipped else (TG, 0, None)

                def steps(eng, step):
                    step(0, 0)
                    step(1, 1)
                    with eng.Fori(1, B // 2 - 2) as j:
                        for u in range(2):
                            step(2 * j + u, u)
                    for t in range(B - 4, B):
                        step(t, t % 2)

                def prepares(t):
                    return not (isinstance(t, int) and t >= B - 2)

                def is_first(t):
                    return isinstance(t, int) and t == 0

                def is_last(t):
                    return isinstance(t, int) and t == B - 1

                @blk.sync
                @guarded
                def _(sp):
                    if clipped:
                        sp.dma_start(wraw[:, 0, :, :], W_qkv[0:D, :].rearrange("(c p) d -> p c d", p=P)).then_inc(w_in, 16)
                        sp.dma_start(wraw[:, 1, :, :], W_o.rearrange("(c p) d -> p c d", p=P)).then_inc(w_in, 16)
                    sp.wait_ge(init, 5 if masked_rows else 2)

                    def load(b, p, reused):
                        if reused:
                            sp.wait_ge(nat_low, b - 1)
                            sp.sem_inc(sink, 1)
                        if picked:
                            rows = [sp.value_load(places[0:1, dcol(b * SLOTS + c)], min_val=0, max_val=B * M - P) for c in range(SLOTS)]
                            for c, row in enumerate(rows):
                                sp.dma_start(CR[p][:, c, :], context_rows[bass.ds(row, P), :]).then_inc(ctx_in[p], 16)
                            return
                        sp.dma_start(CR[p][:, 0:MC - 1, :],
                                     dyn(ctx_mem, b)[0:(MC - 1) * P, :].rearrange("(c p) d -> p c d", p=P)).then_inc(ctx_in[p], 16)
                        sp.dma_start(CR[p][0:MT, MC - 1, :], dyn(ctx_mem, b)[(MC - 1) * P:M, :]).then_inc(ctx_in[p], 16)
                        if not clipped:
                            sp.dma_start(BIAS[p][0:1, :], dynrow(mask_bias_dram, b)).then_inc(ctx_in[p], 16)
                    load(0, 0, False)
                    load(1, 1, False)
                    load(2, 0, True)
                    with sp.Fori(0, (B - 4) // 2) as j:
                        for u in range(2):
                            load(2 * j + 3 + u, (u + 1) % 2, True)
                    load(B - 1, 1, True)

                @blk.gpsimd
                @guarded
                def _(pool):
                    pool.memset(CR[0][:, NC - 1, :], 0.0).then_inc(init, 1)
                    pool.memset(CR[1][:, NC - 1, :], 0.0).then_inc(init, 1)
                    if masked_rows:
                        pool.memset(BIAS[0][:], 0.0).then_inc(init, 1)
                        pool.memset(BIAS[1][:], 0.0).then_inc(init, 1)
                        pool.memset(row0[:], 0.0).then_inc(init, 1)
                        pool.wait_ge(init, 5)
                        pool.memset(row0[0:1, :], 1.0).then_inc(init, 1)
                    pool.memset(PR[:], 0.0).then_inc(init, 1)
                    if quick:
                        pool.memset(SC[0][:, M:MF], LOWEST).then_inc(init, 1)
                        pool.memset(SC[1][:, M:MF], LOWEST).then_inc(init, 1)
                    pool.wait_ge(eps_done, 1)
                    inverse_deviation(pool, rstd_done)

                    def split(b, p, count):
                        pool.wait_ge(ctx_in[p], count)
                        if masked_rows:
                            pool.wait_ge(scores_full, b + 1)
                        pool.wait_ge(nat_high, b + 1)
                        pool.tensor_tensor(NL[p][:], CR[p][:], NH[p][:].bitcast(F32), ALU.subtract).then_inc(nat_low, 1)
                    split(0, 0, LOADS)
                    split(1, 1, LOADS)
                    with pool.Fori(1, B // 2) as j:
                        for u in range(2):
                            split(2 * j + u, u, LOADS * j + LOADS)

                @blk.tensor
                @guarded
                def _(pe):
                    def group(r, n, put, after_same=False):
                        if not (isinstance(r, int) and r == 0):
                            if NRING == 3:
                                back = 1 if after_same else 2 if n in (0, 1) or (isinstance(r, int) and r < 3 * PREP + TG) else 3
                                if not (isinstance(r, int) and r + 1 - back <= 0):
                                    pe.wait_ge(ring_low, r + 1 - back)
                            elif NRING == 2:
                                pe.wait_ge(ring_low, r if after_same else r - 1)
                            elif not (isinstance(r, int) and r <= 2):
                                pe.wait_ge(ring_low, r if isinstance(r, int) and r >= probs_at(B - 1) else r - 2)
                        put(ring[n % NRING]).then_inc(ring_full, 1)

                    def prep(b, p, between=()):
                        pe.wait_ge(xhat, b + 1)

                        def queries(out):
                            for k in range(KD):
                                last = pe.transpose(out[:, k * S:(k + 1) * S], XHAT[0:S, k * P:(k + 1) * P], ident[0:S, 0:S])
                            return last
                        group(prep_at(b), PREP_N, queries,
                              (isinstance(b, int) and b < 3) if clipped else masked_rows)
                        if between:
                            between[0]()
                        pe.wait_ge(ctx_in[p], LOADS * half(b, p) + LOADS)
                        for n in range(KD * TG):
                            k, c0 = n // TG, 4 * (n % TG)

                            def context(out, k=k, c0=c0):
                                for c in range(4):
                                    last = pe.transpose(out[:, c * P:(c + 1) * P], CR[p][:, c0 + c, k * P:(k + 1) * P], ident[:])
                                return last
                            group(prep_at(b) + 1 + n, PREP_N + 1 + n, context)
                            if 1 + n < len(between):
                                between[1 + n]()
                            if n == 3 and clipped:
                                pe.wait_ge(ring_low, prep_at(b) + 1)
                                if not (isinstance(b, int) and b < 4):
                                    pe.wait_ge(updated, b - 3)
                                for m in range(KD):
                                    first = True
                                    for k2 in range(KD):
                                        for w, xx in ((WH, XTH), (WH, XTL), (WL, XTH)):
                                            last = pe.matmul(QB[:, m * S:(m + 1) * S], w[:, 0, k2, m * P:(m + 1) * P], xx[:, k2, :],
                                                             start=first, stop=k2 == KD - 1 and w is WL)
                                            first = False
                                last.then_inc(q_full, 1)

                    def scores(b):
                        pe.wait_ge(ring_low, prep_at(b) + PREP)
                        if clipped:
                            pe.wait_ge(q_low, b + 1)
                        pe.wait_ge(scores_copied, b)
                        for n, (c0, w) in enumerate(COLS):
                            first = True
                            for k in range(KD):
                                for q, m in ((QH, TH), (QH, TL), (QL, TH)):
                                    last = pe.matmul(SP[n][0:S, 0:w], q[:, k, :], m[:, k, c0:c0 + w], start=first,
                                                     stop=clipped and k == KD - 1 and q is QL)
                                    first = False
                            if picked:
                                last = pe.matmul(SP[n][0:S, 0:w], pick_row[:, cols(b, S)], picked_bias[:, 0:w], start=False, stop=True)
                            elif masked_rows:
                                last = pe.matmul(SP[n][0:S, 0:w], row0[:], BIAS[p_of(b)][:, c0:c0 + w], start=False, stop=True)
                        last.then_inc(scores_full, 1)

                    def p_of(b):
                        return parity[0]

                    def project(t):
                        pe.wait_ge(out_read, t + 1)

                        def attended(out):
                            for k in range(KD):
                                last = pe.transpose(out[:, k * S:(k + 1) * S], ATT[0:S, k * P:(k + 1) * P], ident[0:S, 0:S])
                            return last
                        group(attended_at(t), ATTENDED_N, attended, not prepares(t + 1))
                        pe.wait_ge(ring_low, attended_at(t) + 1)
                        pe.wait_ge(updated, t)
                        pe.wait_ge(q_low, min(t + 4, B) if isinstance(t, int) else t + 4)
                        for k in range(KD):
                            for a, w in ((ATH, WH), (ATH, WL), (ATL, WH)):
                                last = pe.matmul(PB[0:S, 0:D], a[:, k, :], w[:, 1, k, :], start=k == 0 and a is ATH and w is WH,
                                                 stop=k == KD - 1 and a is ATL)
                        last.then_inc(proj_full, 1)

                    parity = [0]

                    def turn_probs(t):
                        pe.wait_ge(probs if clipped else exps, t + 1)
                        for n in range(TG):
                            def turned(out, n=n):
                                for c in range(4):
                                    last = pe.transpose(out[:, c * S:(c + 1) * S], PR[0:S, (4 * n + c) * P:(4 * n + c + 1) * P], ident[0:S, 0:S])
                                return last
                            group(probs_at(t) + n, PROBS_N + n, turned, n == 0 and not clipped)

                    def weigh(t, p, some=range(NC)):
                        if 0 in some:
                            pe.wait_ge(ring_low, probs_at(t) + TG)
                            pe.wait_ge(nat_low, t + 1)
                            pe.wait_ge(out_read, t)
                        for c in some:
                            for a, m in ((PTH, NH), (PTH, NL), (PTL, NH)):
                                last = pe.matmul(OB[0:S, 0:D], a[:, c, :], m[p][:, c, :], start=c == 0 and m is NH and a is PTH,
                                                 stop=c == NC - 1 and a is PTL)
                        if NC - 1 in some:
                            last.then_inc(pv_done, 1)

                    def step(t, u):
                        if not is_last(t):
                            parity[0] = 1 - u
                            scores(t + 1)
                        if clipped:
                            quarter = NC // 4
                            if not prepares(t):
                                weigh(t - 1, 1 - u)
                            elif is_first(t):
                                prep(t + 2, u)
                            else:
                                prep(t + 2, u, [lambda n=n: weigh(t - 1, 1 - u, range(quarter * n, quarter * n + quarter))
                                                for n in range(4)])
                            if not is_first(t):
                                project(t - 1)
                            turn_probs(t)
                        else:
                            turn_probs(t)
                            if prepares(t):
                                prep(t + 2, u)
                            weigh(t, u)

                    pe.wait_ge(init, 7 if masked_rows else 3)
                    if clipped:
                        pe.wait_ge(w_in, 32)
                        for w in range(2):
                            for k in range(KD):
                                n = 2 * w + k
                                if n >= 1:
                                    pe.wait_ge(w_low, n)
                                for c in range(KD):
                                    last = pe.transpose(ring[2][:, c * P:(c + 1) * P], wraw[:, w, c, k * P:(k + 1) * P], ident[:])
                                last.then_inc(w_full, 1)
                        pe.wait_ge(w_low, 4)
                    prep(0, 0)
                    scores(0)
                    prep(1, 1)
                    steps(pe, step)
                    if clipped:
                        weigh(B - 1, 1)
                        project(B - 1)

                @blk.scalar
                @guarded
                def _(act):
                    if clipped:
                        for n in range(4):
                            act.wait_ge(w_full, n + 1)
                            act.copy(WH[:, n // 2, n % 2, :], ring[2][:, 0:D]).then_inc(w_high, 1)

                    def high(r, n, put):
                        act.wait_ge(ring_full, r + 1)
                        put(ring[n % NRING]).then_inc(ring_high, 1)

                    def prep(b, p, between=()):
                        if not is_first(b):
                            act.wait_ge(scores_full, b)
                        qd, scale = (XTH, 1.0) if clipped else (QH, float(D) ** -0.5)
                        high(prep_at(b), PREP_N, lambda r: act.activation(qd[:], r[:, 0:KD * S].rearrange("p (k s) -> p k s", k=KD), ACT.Copy, scale=scale))
                        for n in range(KD * TG):
                            k, c0 = n // TG, 512 * (n % TG)
                            high(prep_at(b) + 1 + n, PREP_N + 1 + n, lambda r, k=k, c0=c0: act.copy(TH[:, k, c0:c0 + 512], r[:, :]))
                            if n < len(between) and between[n]:
                                between[n]()
                            if n == 4 and clipped:
                                act.wait_ge(q_full, b + 1)
                                act.activation(QH[:], QB[:, 0:KD * S].rearrange("p (k s) -> p k s", k=KD), ACT.Copy, scale=coef[:, 0:1]).then_inc(q_high, 1)

                    def split_high(b, p, part=None):
                        act.wait_ge(ctx_in[p], LOADS * half(b, p) + LOADS)
                        act.wait_ge(ring_full, prep_at(b) + PREP)
                        if not (isinstance(b, int) and b < 2):
                            act.wait_ge(pv_done, b - 1)
                        c = slice(0, NC) if part is None else slice(part * NC // 3, (part + 1) * NC // 3)
                        copied = act.copy(NH[p][:, c, :], CR[p][:, c, :])
                        if part in (None, 2):
                            copied.then_inc(nat_high, 1)

                    def copy_scores(b, p):
                        act.wait_ge(scores_full, b + 1)
                        if not (isinstance(b, int) and b < 2):
                            act.wait_ge(softmax_read, b - 1)
                            act.wait_ge(exps, b - 1)
                        for n, (c0, w) in enumerate(COLS):
                            last = act.copy(SC[p][0:S, c0:c0 + w], SP[n][0:S, 0:w])
                        last.then_inc(scores_copied, 1)

                    def attend(t, p):
                        act.wait_ge(softmax_read, t + 1)
                        act.wait_ge(pv_done, t + 1)
                        act.activation(ATT[0:S, :], OB[0:S, 0:D], ACT.Copy, scale=small[p][0:S, 2:3]).then_inc(out_read, 1)

                    def high_attended(t):
                        if not is_first(t):
                            act.wait_ge(proj_full, t)
                        high(attended_at(t), ATTENDED_N, lambda r: act.copy(ATH[:], r[:, 0:KD * S].rearrange("p (k s) -> p k s", k=KD)))

                    def step(t, u):
                        act.wait_ge(neg_max, t + 1)
                        if not is_first(t):
                            act.wait_ge(probs if clipped else pv_done, t)
                        act.activation((EXPS if clipped else PR)[0:S, 0:MW], SC[u][0:S, 0:MW], ACT.Exp, bias=small[u][0:S, 0:1],
                                       **({} if clipped else {"accum_out": small[u][0:S, 1:2]})).then_inc(exps, 1)
                        if not is_last(t) and not clipped:
                            split_high(t + 1, 1 - u)
                        if not is_last(t):
                            copy_scores(t + 1, 1 - u)
                        if clipped:
                            def after_context(n):
                                if n == 0 and not is_first(t):
                                    attend(t - 1, 1 - u)
                                split_high(t + 1, 1 - u, n)
                            if prepares(t):
                                prep(t + 2, u, [None] * 3 + [lambda n=n: after_context(n) for n in range(3)])
                            else:
                                attend(t - 1, 1 - u)
                                if not is_last(t):
                                    split_high(t + 1, 1 - u)
                            if not is_first(t):
                                high_attended(t - 1)
                        if not is_first(t):
                            act.wait_ge(pv_done, t)
                        for n in range(TG):
                            high(probs_at(t) + n, PROBS_N + n, lambda r, n=n: act.copy(
                                PTH[:, 4 * n:4 * n + 4, :], r[:, 0:4 * S].rearrange("p (c s) -> p c s", c=4)))
                        if prepares(t) and not clipped:
                            prep(t + 2, u)

                    prep(0, 0)
                    if clipped:
                        copy_scores(0, 0)
                        split_high(0, 0)
                    else:
                        split_high(0, 0)
                        copy_scores(0, 0)
                    prep(1, 1)
                    steps(act, step)
                    if clipped:
                        attend(B - 1, 1)
                        high_attended(B - 1)

                CH = 38 if quick else 15 if clipped else 3

                @blk.vector
                @guarded
                def _(dve):
                    if clipped:
                        for n in range(4):
                            dve.wait_ge(w_high, n + 1)
                            dve.tensor_tensor(WL[:, n // 2, n % 2, :], ring[2][:, 0:D], WH[:, n // 2, n % 2, :].bitcast(F32),
                                              ALU.subtract).then_inc(w_low, 1)
                    dve.tensor_scalar(VEPS[0:S, :], MV[0:S, :, 1], LN_EPS, None, ALU.add).then_inc(eps_done, 1)
                    dve.wait_ge(rstd_done, 1)
                    if quick:
                        dve.wait_ge(init, 5)

                    def held(s, value):
                        dve.wait_ge(s, value)
                        if clipped:
                            dve.sem_inc(sink, 1)

                    def normalise(b):
                        if isinstance(b, int) and b == HEAD:
                            dve.wait_ge(rstd_done, 2)
                        dve.tensor_scalar(XHAT[0:S, :], XN[0:S, dsl(b), :], MV[0:S, dsl(b), 0:1].rearrange("p a b -> p (a b)"),
                                          RSTD[0:S, dsl(b)], ALU.subtract, ALU.mult).then_inc(xhat, 1)

                    def low(r, n, put):
                        dve.wait_ge(ring_high, r + 1)
                        put(ring[n % NRING]).then_inc(ring_low, 1)

                    def prep_parts(b):
                        qh, ql, scale = (XTH, XTL, 1.0) if clipped else (QH, QL, float(D) ** -0.5)

                        def queries():
                            low(prep_at(b), PREP_N, lambda r: dve.scalar_tensor_tensor(
                                out=ql[:], in0=r[:, 0:KD * S].rearrange("p (k s) -> p k s", k=KD), scalar=scale, in1=qh[:].bitcast(F32), op0=ALU.mult, op1=ALU.subtract))

                        def tokens():
                            if not is_last(b):
                                normalise(b + 1)

                        def context(n):
                            k, c0 = n // TG, 512 * (n % TG)
                            low(prep_at(b) + 1 + n, PREP_N + 1 + n, lambda r: dve.tensor_tensor(
                                TL[:, k, c0:c0 + 512], r[:, :], TH[:, k, c0:c0 + 512].bitcast(F32), ALU.subtract))

                        def projected():
                            dve.wait_ge(q_high, b + 1)
                            dve.scalar_tensor_tensor(out=QL[:], in0=QB[:, 0:KD * S].rearrange("p (k s) -> p k s", k=KD), scalar=coef[:, 0:1],
                                                     in1=QH[:].bitcast(F32), op0=ALU.mult, op1=ALU.subtract).then_inc(q_low, 1)
                        made = [queries, tokens] + [lambda n=n: context(n) for n in range(KD * TG)]
                        return made[:7] + [projected] + made[7:] if clipped else made

                    def prep(b):
                        for part in prep_parts(b):
                            part()

                    linked = [0, 0]

                    def mark(ins):
                        linked[1] += 1
                        ins.then_inc(chain, 1)
                        return linked[0] + linked[1]

                    def link(ins, meanwhile=()):
                        linked[1] += 1
                        ins.then_inc(chain, 1)
                        for f in meanwhile:
                            f()
                        held(chain, linked[0] + linked[1])

                    def added(t, u):
                        if clipped:
                            dve.wait_ge(proj_full, t + 1)
                            f, o = small[u][0:S, 3:4], PB
                        else:
                            dve.wait_ge(softmax_read, t + 1)
                            dve.wait_ge(pv_done, t + 1)
                            f, o = small[u][0:S, 3:4], OB
                        dve.scalar_tensor_tensor(out=XNEW[0:S, :], in0=o[0:S, 0:D], scalar=f, in1=XN[0:S, dsl(t), :].rearrange("p a d -> p (a d)"),
                                                 op0=ALU.mult, op1=ALU.add).then_inc(updated if clipped else out_read, 1)

                    def statistics(t):
                        dve.wait_ge(updated if clipped else out_read, t + 1)
                        taken = mark(dve.bn_stats(bn[0:S, 0:6], XNEW[0:S, :]))
                        dve.tensor_scalar(XN[0:S, dsl(t), :].rearrange("p a d -> p (a d)"), XNEW[0:S, :], 1.0, None, ALU.mult)
                        dve.wait_ge(chain, taken)
                        dve.sem_inc(sink, 1)
                        return mark(dve.bn_aggr(bn[0:S, 6:8], bn[0:S, 0:6]))

                    def new_statistics(t, taken):
                        held(chain, taken)
                        dve.tensor_scalar(MV[0:S, dsl(t), :].rearrange("p a d -> p (a d)"), bn[0:S, 6:8], 1.0, None, ALU.mult)

                    def update(t, u):
                        added(t, u)
                        new_statistics(t, statistics(t))

                    def low_probs(t, some=range(TG)):
                        for n in some:
                            low(probs_at(t) + n, PROBS_N + n, lambda r, n=n: dve.tensor_tensor(
                                PTL[:, 4 * n:4 * n + 4, :], r[:, 0:4 * S].rearrange("p (c s) -> p c s", c=4),
                                PTH[:, 4 * n:4 * n + 4, :].bitcast(F32), ALU.subtract))

                    def low_attended(t):
                        low(attended_at(t), ATTENDED_N, lambda r: dve.tensor_tensor(
                            ATL[:], r[:, 0:KD * S].rearrange("p (k s) -> p k s", k=KD), ATH[:].bitcast(F32), ALU.subtract))

                    def step(t, u):
                        linked[:] = [0 if is_first(t) else CH * t - 2, 0]
                        sm = small[u]
                        if clipped:
                            def top_of(out, src0, work, after):
                                for r in range(7):
                                    src = src0 if r == 0 else work
                                    found = dve.max(out[0:S, 8 * r:8 * r + 8], src)
                                    if r == 0 and not quick:
                                        link(found)
                                        maximum()
                                        for f in after.get(r, ()):
                                            f()
                                    else:
                                        link(found, after.get(r, ()))
                                    if r < 6:
                                        link(dve.match_replace(work, out[0:S, 8 * r:8 * r + 8], src, LOWEST), after.get(r + 0.5, ()))

                            def maximum():
                                dve.tensor_scalar(sm[0:S, 0:1], top[0:S, 0:1], -1.0, None, ALU.mult).then_inc(neg_max, 1)

                            def low_before():
                                if not is_first(t):
                                    low_attended(t - 1)
                            parts = prep_parts(t + 2) if prepares(t) else []
                            if quick:
                                held(scores_copied, t + 1)
                                src, at = SC[u][0:S, 0:MF], 0
                                segments = []
                                for n in range(3):
                                    w = MF >> (n + 1)
                                    folded = mark(dve.tensor_tensor(FOLD[0:S, at:at + w], src[:, 0:w], src[:, w:2 * w], ALU.max))
                                    dve.tensor_tensor(FOLD[0:S, at + w:at + 2 * w], src[:, 0:w], src[:, w:2 * w], ALU.min)
                                    if not is_first(t):
                                        low_probs(t - 1, range(n, n + 1))
                                    held(chain, folded)
                                    segments += [(at + w + i * (w >> n), w >> n) for i in range(1 << n)]
                                    src, at = FOLD[0:S, at:at + w], at + 2 * w

                                def segment(n):
                                    a0, w = segments[n]
                                    dve.max(cand[0:S, 80 + 8 * n:88 + 8 * n], FOLD[0:S, a0:a0 + w])
                                H = MF // 16
                                replaced = [0, 0]
                                for r in range(5):
                                    found = [0, 0]
                                    for h in range(2):
                                        o = 32 * h + 8 * r if r < 4 else 64 + 8 * h
                                        if r:
                                            held(chain, replaced[h])
                                        best_of = src if r == 0 else WORK[0:S, :]
                                        if r == 4 and h == 0:
                                            segment(6)
                                        found[h] = mark(dve.max(cand[0:S, o:o + 8], best_of[:, h * H:(h + 1) * H]))
                                    if r == 0:
                                        segment(0)
                                        held(chain, found[1])
                                        dve.tensor_reduce(sm[0:S, 0:1], cand[0:S, 0:64].rearrange("p (n k) -> p n k", k=32)[:, :, 0:1],
                                                          AX.XY, ALU.max, negate=True).then_inc(neg_max, 1)
                                    elif r < 4:
                                        segment(2 * r - 1)
                                    if r < 4:
                                        for h in range(2):
                                            o = 32 * h + 8 * r
                                            held(chain, found[h])
                                            replaced[h] = mark(dve.match_replace(WORK[0:S, h * H:(h + 1) * H], cand[0:S, o:o + 8],
                                                                                 best_of[:, h * H:(h + 1) * H], LOWEST))
                                        if 0 < r < 3:
                                            segment(2 * r)
                                held(chain, found[1])
                                top_of(top, cand[0:S, :], CWORK[0:S, :],
                                       dict(zip((0, 0.5, 1, 2, 3, 4, 5, 5.5, 6), [[p] for p in parts])))
                                low_before()
                            else:
                                if not is_first(t):
                                    low_probs(t - 1)
                                held(scores_copied, t + 1)
                                top_of(top, SC[u][0:S, :], WORK[0:S, :],
                                       {1: parts[0:2], 2: parts[2:4], 3: parts[4:7], 5: parts[7:]})
                                low_before()
                                dve.tensor_scalar(sm[0:S, 3:4], redo_gain[0:S, dsl(t)], 1.0, None, ALU.mult)
                            dve.wait_ge(exps, t + 1)
                            if not is_first(t):
                                dve.wait_ge(pv_done, t)
                            dve.scalar_tensor_tensor(out=PR[0:S, 0:MW], in0=SC[u][0:S, 0:MW], scalar=top[0:S, CLIP_K - 1:CLIP_K],
                                                     in1=EXPS[0:S, :], op0=ALU.is_ge, op1=ALU.mult,
                                                     accum_out=sm[0:S, 1:2]).then_inc(probs, 1)

                            def greatest_left():
                                return mark(dve.tensor_reduce(sm[0:S, 5:6], cand[0:S, 64:136].rearrange("p (n k) -> p n k", k=8)[:, :, 7:8],
                                                              AX.XY, ALU.max))

                            def proof(found):
                                held(chain, found)
                                return mark(dve.tensor_scalar(sm[0:S, 6:7], sm[0:S, 5:6], top[0:S, CLIP_K - 1:CLIP_K], None, ALU.is_le))

                            def proved(found):
                                held(chain, found)
                                dve.tensor_scalar(sm[0:S, 3:4], sm[0:S, 6:7], gains[0:S, 1:2], None, ALU.mult)
                                dve.tensor_scalar(exact[0:S, dsl(t)], sm[0:S, 6:7], 1.0, None, ALU.mult)
                            if quick:
                                left = greatest_left()
                            if not is_first(t):
                                added(t - 1, 1 - u)
                            if quick:
                                left = proof(left)
                            if not is_first(t):
                                taken = statistics(t - 1)
                            if quick:
                                proved(left)
                            dve.wait_ge(probs, t + 1)
                            dve.reciprocal(sm[0:S, 2:3], sm[0:S, 1:2]).then_inc(softmax_read, 1)
                            if not is_first(t):
                                new_statistics(t - 1, taken)
                        else:
                            dve.wait_ge(scores_copied, t + 1)
                            dve.tensor_reduce(sm[0:S, 0:1], SC[u][0:S, :], AX.X, ALU.max, negate=True).then_inc(neg_max, 1)
                            if not is_first(t):
                                update(t - 1, 1 - u)
                            dve.wait_ge(exps, t + 1)
                            link(dve.reciprocal(sm[0:S, 2:3], sm[0:S, 1:2]))
                            dve.tensor_tensor(sm[0:S, 3:4], sm[0:S, 2:3], gain_of[0:S, dsl(t)], ALU.mult).then_inc(softmax_read, 1)
                        if not clipped:
                            low_probs(t)
                        if prepares(t) and not clipped:
                            prep(t + 2)
                        assert linked[1] == (CH - 2 if is_first(t) else CH), linked

                    normalise(0)
                    prep(0)
                    prep(1)
                    steps(dve, step)
                    linked[:] = [CH * B - 2, 0]
                    if clipped:
                        low_probs(B - 1)
                        low_attended(B - 1)
                    update(B - 1, 1)

        def find_redo():
            with ExitStack() as ctx:
                left = ctx.enter_context(nc.sbuf_tensor("left", [P, B], F32))
                count = ctx.enter_context(nc.sbuf_tensor("left_count", [P, 2], F32))
                total = ctx.enter_context(nc.psum_tensor("left_total", [P, 1], F32))
                redo_step, total_full = sem("redo_step"), sem("redo_total")
                blk = ctx.enter_context(nc.Block())

                @blk.tensor
                def _(pe):
                    pe.wait_ge(redo_step, 2)
                    pe.matmul(total[:, :], ones[0:S, :], count[0:S, 0:1], start=True, stop=True).then_inc(total_full, 1)

                @blk.vector
                def _(dve):
                    dve.tensor_scalar(left[0:S, :], exact[0:S, :], -1.0, 1.0, ALU.mult, ALU.add).then_inc(redo_step, 1)
                    dve.wait_ge(redo_step, 1)
                    dve.tensor_reduce(count[0:S, 0:1], left[0:S, :], AX.X, ALU.add).then_inc(redo_step, 1)
                    dve.tensor_scalar(redo_gain[0:S, :], left[0:S, :], gains[0:S, 1:2], None, ALU.mult)
                    dve.wait_ge(total_full, 1)
                    dve.tensor_scalar(count[:, 1:2], total[:, :], 0.5, None, ALU.is_ge).then_inc(redo_step, 1)
                    dve.wait_ge(redo_step, 3)
                    dve.tensor_copy(any_redo[:], count[:, 1:2])

        def feed_forward(layer):
            L = f"f{layer}_"
            ternary = layer == 1
            EJ = P // E
            EC = EI // EJ
            SCN = -(-SI // P)
            if ternary:
                passes = [[("t", c) for c in range(FI // P)]]
            else:
                every = [("e", c) for c in range(EC)]
                passes = [every[n:n + 6] for n in range(0, EC, 6)] + [[("s", c) for c in range(SCN)]]
            NCM = max(len(p) for p in passes)
            assert all(len(p) % 2 == 0 for p in passes)
            T = B * S
            with ExitStack() as ctx:
                def sb(name, shape, dt=F32):
                    return ctx.enter_context(nc.sbuf_tensor(L + name, shape, dt))

                def bank(name):
                    return ctx.enter_context(nc.psum_tensor(L + name, [P, 512], F32))
                XH, XL = sb("XH", [P, KD, T], F32R), sb("XL", [P, KD, T], F32R)
                if not ternary:
                    YT = sb("YT", [P, KD, T])
                    CW = sb("CW", [P, T])
                WH = sb("WH", [P, NCM, 2 * KD, P], F32R)
                DH = sb("DH", [P, NCM, D], F32R)
                if not ternary:
                    WL, DL = sb("WL", [P, NCM, 2 * KD, P], F32R), sb("DL", [P, NCM, D], F32R)
                RG, RU = sb("RG", [P, NCM, D]), sb("RU", [P, NCM, D])
                RD = sb("RD", [P, KD, NCM * P])
                RDO = None if ternary else sb("RDO", [P, KD, NCM * P])
                GB_, UB_ = [bank("G0"), bank("G1")], [bank("U0"), bank("U1")]
                YB = [[bank(f"Y{u}{k}") for k in range(KD)] for u in range(2)]

                raw_in, w_full, zeroed = sem(L + "raw_in"), sem(L + "w_full"), None if ternary else sem(L + "zeroed")
                groups = [0]
                for p in passes:
                    groups.append(groups[-1] + len(p) + len(p) // 2)
                raws = [0] * (len(passes) + 1)

                def load_weights(sp, n):
                    chunks = passes[n]
                    kind, c0, w = chunks[0][0], chunks[0][1], len(chunks)
                    if n:
                        sp.wait_ge(w_full, groups[n])
                    if kind == "s":
                        sp.wait_ge(zeroed, 3)
                    if kind == "e":
                        for e in range(E):
                            for r, o in ((RG, 0), (RU, EI)):
                                sp.dma_start(r[e * EJ:(e + 1) * EJ, 0:w, :],
                                             expert_gate_up[e, o + c0 * EJ:o + (c0 + w) * EJ, :].rearrange("(c j) d -> j c d", j=EJ)).then_inc(raw_in, 16)
                            for k in range(KD):
                                sp.dma_start(RD[:, k, e * w * EJ:(e + 1) * w * EJ],
                                             expert_down[e, k * P:(k + 1) * P, c0 * EJ:(c0 + w) * EJ]).then_inc(raw_in, 16)
                        raws[n + 1] = raws[n] + 16 * E * (2 + KD)
                    else:
                        src_g, src_u, src_d, rows = (W_up, W_gate, W_down, FI) if kind == "t" else \
                            (shared_gate_up[0:SI, :], shared_gate_up[SI:2 * SI, :], shared_down, SI)
                        full, rest = rows // P, rows % P
                        for r, src in ((RG, src_g), (RU, src_u)):
                            sp.dma_start(r[:, 0:full, :], src[0:full * P, :].rearrange("(c p) d -> p c d", p=P)).then_inc(raw_in, 16)
                            if rest:
                                sp.dma_start(r[0:rest, full, :], src[full * P:rows, :]).then_inc(raw_in, 16)
                        sp.dma_start(RD[:, :, 0:rows], src_d.rearrange("(k p) i -> p k i", p=P)).then_inc(raw_in, 16)
                        raws[n + 1] = raws[n] + 16 * (3 + 2 * (rest > 0))

                names = ("xhat", "turned", "high", "low", "plain", "logits", "read", "sink", "rstd", "eps", "gw_in", "gw_t",
                         "gw_s", "chain", "exp1", "iota_s", "picked")
                unused = ("plain", "logits", "read", "gw_in", "gw_t", "gw_s", "chain", "exp1", "iota_s", "picked") if ternary else ()
                (xhat, turned, high, low, plain, logits, read, sink, rstd_done, eps_done, gw_in, gw_t, gw_s, chain,
                 exp1, iota_s, picked) = (None if n in unused else sem(L + "n_" + n) for n in names)
                with ExitStack() as rctx:
                    def rb(name, shape, dt=F32):
                        return rctx.enter_context(nc.sbuf_tensor(L + name, shape, dt))
                    XHAT = [rb(f"XHAT{u}", [P, 2, D]) for u in range(2)]
                    if not ternary:
                        NL_ = E + 1
                        XT = [rb(f"XT{u}", [P, KD, 2 * S]) for u in range(2)]
                        gw_raw = rb("gw_raw", [NL_, D])
                        gwT = rb("gwT", [P, KD, NL_])
                        LG = rb("LG", [P, B, NL_])
                        top = rb("top", [P, B, 8])
                        idx = rb("idx", [P, B, 8], U32)
                        idxf = rb("idxf", [P, B, 8])
                        iota = rb("iota", [P, B, E])
                        eq, sel = rb("eq", [P, B, E]), rb("sel", [P, B, E])
                        ex, sums = rb("ex", [P, B, E]), rb("sums", [P, B])
                        sig = rb("sig", [P, B])
                    with nc.Block() as blk:
                        @blk.sync
                        def _(sp):
                            if not ternary:
                                sp.dma_start(gw_raw[0:E, :], gate_w).then_inc(gw_in, 16)
                                sp.dma_start(gw_raw[E:E + 1, :], shared_gate_vec).then_inc(gw_in, 16)
                            load_weights(sp, 0)

                        @blk.gpsimd
                        def _(pool):
                            pool.wait_ge(eps_done, 1)
                            inverse_deviation(pool, rstd_done)
                            if not ternary:
                                pool.iota(iota[:], pattern=[[0, B], [1, E]], base=0, channel_multiplier=0,
                                          allow_small_or_imprecise_dtypes=True).then_inc(iota_s, 1)

                        Q = B // 2

                        def by_twos(step):
                            def run(eng):
                                step(0, 0)
                                step(1, 1)
                                with eng.Fori(1, Q // 2 - 1) as j:
                                    step(2 * j, 0)
                                    step(2 * j + 1, 1)
                                step(Q - 2, 0)
                                step(Q - 1, 1)
                            return run

                        def is_final(q):
                            return isinstance(q, int) and q == Q - 1

                        @blk.tensor
                        def _(pe):
                            if not ternary:
                                pe.wait_ge(gw_in, 32)
                                for k in range(KD):
                                    last = pe.transpose(YB[0][0][:, k * NL_:(k + 1) * NL_], gw_raw[:, k * P:(k + 1) * P], ident[0:NL_, 0:NL_])
                                last.then_inc(gw_t, 1)
                                pe.wait_ge(gw_s, 1)

                            def turn(q, u):
                                pe.wait_ge(xhat, q + 1)
                                if not (isinstance(q, int) and q < 2):
                                    pe.wait_ge(low, q - 1)
                                for k in range(KD):
                                    for i in range(2):
                                        last = pe.transpose(GB_[u][:, (2 * k + i) * S:(2 * k + i + 1) * S], XHAT[u][0:S, i, k * P:(k + 1) * P],
                                                            ident[0:S, 0:S])
                                last.then_inc(turned, 1)

                            def step(q, u):
                                if not is_final(q):
                                    turn(q + 1, 1 - u)
                                if not ternary:
                                    pe.wait_ge(plain, q + 1)
                                    if not (isinstance(q, int) and q < 2):
                                        pe.wait_ge(read, q - 1)
                                    for i in range(2):
                                        for k in range(KD):
                                            last = pe.matmul(UB_[u][0:S, i * NL_:(i + 1) * NL_], XT[u][:, k, i * S:(i + 1) * S], gwT[:, k, :],
                                                             start=k == 0, stop=k == KD - 1)
                                    last.then_inc(logits, 1)
                            turn(0, 0)
                            by_twos(step)(pe)

                        @blk.scalar
                        def _(act):
                            def step(q, u):
                                r = GB_[u][:, 0:2 * KD * S].rearrange("p (k s) -> p k s", k=KD)
                                act.wait_ge(turned, q + 1)
                                if not ternary:
                                    if not (isinstance(q, int) and q < 2):
                                        act.wait_ge(logits, q - 1)
                                    act.copy(XT[u][:], r).then_inc(plain, 1)
                                act.sem_inc(sink, 1)
                                act.activation(XH[:, :, cols(q, 2 * S)], r, ACT.Copy).then_inc(high, 1)
                            by_twos(step)(act)
                            if not ternary:
                                act.wait_ge(chain, 1)
                                act.activation(ex[0:S], ex[0:S], ACT.Exp).then_inc(exp1, 1)
                                act.activation(sig[0:S], LG[0:S, :, E], ACT.Exp, scale=-1.0).then_inc(exp1, 1)

                        @blk.vector
                        def _(dve):
                            dve.tensor_scalar(VEPS[0:S, :], MV[0:S, :, 1], LN_EPS, None, ALU.add).then_inc(eps_done, 1)
                            if not ternary:
                                dve.wait_ge(gw_t, 1)
                                dve.tensor_copy(gwT[:], YB[0][0][:, 0:KD * NL_].rearrange("p (k e) -> p k e", k=KD)).then_inc(gw_s, 1)
                            dve.wait_ge(rstd_done, 1)

                            def normalise(q, u):
                                if isinstance(q, int) and 2 * q == HEAD:
                                    dve.wait_ge(rstd_done, 2)
                                if not (isinstance(q, int) and q < 2):
                                    dve.wait_ge(turned, q - 1)
                                for i in range(2):
                                    b = 2 * q + i
                                    last = dve.tensor_scalar(XHAT[u][0:S, i, :], XN[0:S, dsl(b), :], MV[0:S, dsl(b), 0:1].rearrange("p a b -> p (a b)"),
                                                             RSTD[0:S, dsl(b)], ALU.subtract, ALU.mult)
                                last.then_inc(xhat, 1)

                            def read_logits(q, u):
                                dve.wait_ge(logits, q + 1)
                                dve.tensor_scalar(LG[0:S, cols(q, 2), :], UB_[u][0:S, 0:2 * NL_].rearrange("p (i e) -> p i e", i=2),
                                                  1.0, None, ALU.mult).then_inc(read, 1)

                            def step(q, u):
                                dve.wait_ge(high, q + 1)
                                dve.tensor_tensor(XL[:, :, cols(q, 2 * S)], GB_[u][:, 0:2 * KD * S].rearrange("p (k s) -> p k s", k=KD),
                                                  XH[:, :, cols(q, 2 * S)].bitcast(F32), ALU.subtract).then_inc(low, 1)
                                if not (isinstance(q, int) and q >= Q - 2):
                                    normalise(q + 2, u)
                                if not ternary and not (isinstance(q, int) and q == 0):
                                    read_logits(q - 1, 1 - u)
                            normalise(0, 0)
                            normalise(1, 1)
                            by_twos(step)(dve)
                            if not ternary:
                                read_logits(Q - 1, 1)
                            if not ternary:
                                n = 0

                                def link(ins):
                                    nonlocal n
                                    n += 1
                                    ins.then_inc(picked, 1)
                                    dve.wait_ge(picked, n)
                                dve.wait_ge(read, Q)
                                for b in range(B):
                                    last = dve.max(top[0:S, b, :], LG[0:S, b, 0:E])
                                link(last)
                                for b in range(B):
                                    last = dve.max_index(idx[0:S, b, :], top[0:S, b, :], LG[0:S, b, 0:E])
                                link(last)
                                dve.tensor_tensor(ex[0:S], LG[0:S, :, 0:E], top[0:S, :, 0:1].to_broadcast([S, B, E]),
                                                  ALU.subtract).then_inc(chain, 1)
                                link(dve.tensor_copy(idxf[0:S], idx[0:S]))
                                dve.wait_ge(iota_s, 1)
                                for k in range(TOP_EXPERTS):
                                    dst = sel if k == 0 else eq
                                    link(dve.tensor_tensor(dst[0:S], iota[0:S], idxf[0:S, :, k:k + 1].to_broadcast([S, B, E]), ALU.is_equal))
                                    if k:
                                        link(dve.tensor_tensor(sel[0:S], sel[0:S], eq[0:S], ALU.add))
                                dve.wait_ge(exp1, 2)
                                link(dve.tensor_tensor(sel[0:S], sel[0:S], ex[0:S], ALU.mult))
                                link(dve.tensor_reduce(sums[0:S], sel[0:S], AX.X, ALU.add))
                                link(dve.reciprocal(sums[0:S], sums[0:S]))
                                link(dve.tensor_tensor(CWN[0:S], sel[0:S], sums[0:S, :].rearrange("p (b o) -> p b o", o=1).to_broadcast([S, B, E]), ALU.mult))
                                link(dve.tensor_scalar(sig[0:S], sig[0:S], 1.0, None, ALU.add))
                                dve.reciprocal(SIGN[0:S], sig[0:S])

                names = ("w_high", "w_low", "gu_full", "silu", "mid", "hid", "h_high", "h_low",
                         "down", "y_full", "y_read", "y_fin", "y_turned", "x_new", "tern", "sums3", "tot", "scales",
                         "wide", "cwt", "cws", "fsink", "ordered", "links")
                unused = ("w_high", "hid", "wide", "cwt", "cws", "fsink", "ordered") if ternary else \
                    ("tern", "sums3", "tot", "scales", "links")
                (w_high, w_low, gu_full, silu, mid, hid, h_high, h_low, down, y_full, y_read,
                 y_fin, y_turned, x_new, tern, sums3, tot, scales, wide, cwt, cws, fsink, ordered, links) = (
                    None if n in unused else sem(L + n) for n in names)
                with ExitStack() as hctx:
                    def hb(name, shape, dt=F32):
                        return hctx.enter_context(nc.sbuf_tensor(L + name, shape, dt))
                    HS = [hb(f"HS{u}", [P, GT]) for u in range(2)]
                    HH, HL = [hb(f"HH{u}", [P, GT], F32R) for u in range(2)], [hb(f"HL{u}", [P, GT], F32R) for u in range(2)]
                    YF = [hb(f"YF{u}", [P, KD, GT]) for u in range(2)] if ternary else [hb("YF", [P, KD, GT])] * 2
                    if ternary:
                        part, half_s = hb("part", [P, 4]), hb("half_s", [P, 16])
                        TM = hb("TM", [P, NCM, D])
                    else:
                        CX = hb("CX", [P, GB, P])
                    stored = sem("stored") if ternary else None
                    blk = hctx.enter_context(nc.Block())
                    before = [sum(len(p) for p in passes[:n]) for n in range(len(passes) + 1)]
                    NP_ = len(passes)

                    def chunk_no(n, g, c):
                        return before[n] * NG + len(passes[n]) * g + c

                    def used(eng, n, g, c, nch):
                        per = nch - 1
                        base = sum(len(p) - 1 for p in passes[:n]) * NG
                        if c >= 2:
                            eng.wait_ge(down, base + per * g + c - 1)
                        elif not (isinstance(g, int) and g == 0):
                            if c == 0:
                                eng.wait_ge(down, base + per * g)
                            else:
                                eng.wait_ge(y_full, n * NG + g)

                    def over_groups(eng, step):
                        step(0, 0)
                        step(1, 1)
                        with eng.Fori(1, NG // 2) as j:
                            step(2 * j, 0)
                            step(2 * j + 1, 1)

                    @blk.sync
                    def _(sp):
                        for n in range(1, len(passes)):
                            load_weights(sp, n)
                        if ternary:
                            for g in range(NG):
                                sp.wait_ge(x_new, GB * (g + 1))
                                sp.dma_start(out[g * GB:(g + 1) * GB].rearrange("b s d -> s b d"),
                                             XN[0:S, g * GB:(g + 1) * GB, :]).then_inc(stored, 16)
                            sp.wait_ge(stored, 16 * NG)

                    @blk.gpsimd
                    def _(pool):
                        for n, chunks in enumerate(passes):
                            if not ternary and n == NP_ - 2:
                                pool.wait_ge(hid, before[n] * NG)
                                pool.wait_ge(w_full, groups[n + 1])
                                pool.memset(RG[SI % P:P, SCN - 1, :], 0.0).then_inc(zeroed, 1)
                                pool.memset(RU[SI % P:P, SCN - 1, :], 0.0).then_inc(zeroed, 1)
                                pool.wait_ge(zeroed, 2)
                                pool.memset(RD[:, :, SI:SCN * P], 0.0).then_inc(zeroed, 1)
                                pool.wait_ge(zeroed, 3)
                            if ternary:
                                continue
                            if n == 0:
                                pool.wait_ge(cws, NG)
                            if chunks[0][0] == "s":
                                pool.wait_ge(cws, 2 * NG)

                            def step(g, u):
                                for c in range(len(chunks)):
                                    pool.wait_ge(mid, chunk_no(n, g, c) + 1)
                                    pool.sem_inc(fsink, 1)
                                    pool.tensor_tensor(HS[c % 2][:], HS[c % 2][:], CW[:, cols(g, GT)], ALU.mult).then_inc(hid, 1)
                            over_groups(pool, step)

                    @blk.tensor
                    def _(pe):
                        ring = [GB_[0], GB_[1], UB_[0], UB_[1]]
                        if ternary:
                            pe.wait_ge(sums3, 3)
                            pe.matmul(YB[0][0][:, 0:3], ones[:], part[:, 0:3], start=True, stop=True).then_inc(tot, 1)
                            pe.wait_ge(tern, 3)

                        def combining(lo):
                            for g in range(NG):
                                pe.wait_ge(wide, lo + g + 1)
                                if g >= 2:
                                    pe.wait_ge(cws, lo + g - 1)
                                for i in range(GB):
                                    last = pe.transpose(UB_[g % 2][:, i * S:(i + 1) * S], CX[0:S, i, :], ident[0:S, 0:S])
                                last.then_inc(cwt, 1)

                        for n, chunks in enumerate(passes):
                            nch = len(chunks)
                            if not ternary and n == 0:
                                combining(0)
                            if not ternary and chunks[0][0] == "s":
                                combining(NG)
                            pe.wait_ge(raw_in, raws[n + 1])
                            if chunks[0][0] == "s":
                                pe.wait_ge(zeroed, 3)
                            if n:
                                pe.wait_ge(mid, before[n] * NG)
                            if not ternary and (n == 0 or chunks[0][0] == "s"):
                                pe.wait_ge(cws, NG if n == 0 else 2 * NG)
                            r = groups[n]
                            for c in range(nch):
                                if r >= 4:
                                    pe.wait_ge(w_low, r - 3)
                                for m, raw in enumerate((RG, RU)):
                                    for k in range(KD):
                                        src = raw[:, c, k * P:(k + 1) * P]
                                        last = pe.transpose(ring[r % 4][:, (m * KD + k) * P:(m * KD + k + 1) * P], src, ident[:])
                                last.then_inc(w_full, 1)
                                r += 1
                            if chunks[0][0] == "e":
                                pe.wait_ge(ordered, n + 1)
                            for c in range(0, nch, 2):
                                pe.wait_ge(w_low, r - 3)
                                for i in range(2):
                                    for k in range(KD):
                                        src = (RDO if chunks[0][0] == "e" else RD)[:, k, (c + i) * P:(c + i + 1) * P]
                                        last = pe.transpose(ring[r % 4][:, (i * KD + k) * P:(i * KD + k + 1) * P], src, ident[:])
                                last.then_inc(w_full, 1)
                                r += 1
                            pe.wait_ge(w_low, r)
                            last_pass = n == NP_ - 1
                            gu_parts = ((WH, XH), (WH, XL)) if ternary else ((WH, XH), (WH, XL), (WL, XH))

                            def hidden(g, c, chunks=chunks, n=n):
                                i = chunk_no(n, g, c)
                                if c >= 2:
                                    pe.wait_ge(mid, i - 1)
                                elif not (isinstance(g, int) and g == 0):
                                    pe.wait_ge(mid, i - 1)
                                for m, bk in enumerate((GB_[c % 2], UB_[c % 2])):
                                    first = True
                                    for k in range(KD):
                                        for w, xx in gu_parts:
                                            last = pe.matmul(bk[:, 0:GT], w[:, c, m * KD + k, :], xx[:, k, cols(g, GT)], start=first,
                                                             stop=k == KD - 1 and (w, xx) == gu_parts[-1])
                                            first = False
                                last.then_inc(gu_full, 1)

                            def project(g, u, c, nch=nch, n=n):
                                i = chunk_no(n, g, c)
                                pe.wait_ge(h_low, i + 1)
                                if c == 0 and not (isinstance(g, int) and g < 2 and n == 0):
                                    if last_pass:
                                        if not (isinstance(g, int) and g < 2):
                                            pe.wait_ge(x_new, GB * (g - 1))
                                        else:
                                            pe.wait_ge(y_read, n * NG)
                                    else:
                                        pe.wait_ge(y_read, n * NG + g - 1)
                                parts = ((DH, HH), (DH, HL)) if ternary else ((DH, HH), (DH, HL), (DL, HH))
                                for k in range(KD):
                                    for w, h in parts:
                                        last = pe.matmul(YB[u][k][:, 0:GT], w[:, c, k * P:(k + 1) * P], h[c % 2][:], start=c == 0 and (w, h) == parts[0],
                                                         stop=c == nch - 1 and (w, h) == parts[-1])
                                last.then_inc(y_full if c == nch - 1 else down, 1)

                            def turn_out(g, u):
                                pe.wait_ge(y_fin, g + 1)
                                for i in range(GB):
                                    for k in range(KD):
                                        o = YB[u][i // 2][0:S, (i % 2) * D + k * P:(i % 2) * D + (k + 1) * P]
                                        last = pe.transpose(o, YF[u][:, k, i * S:(i + 1) * S], ident[:])
                                last.then_inc(y_turned, 1)

                            def step(g, u):
                                first = isinstance(g, int) and g == 0
                                for c in range(nch):
                                    hidden(g, c)
                                    if c >= 2:
                                        project(g, u, c - 2)
                                    elif not first:
                                        project(g - 1, 1 - u, nch - 2 + c)
                                    if last_pass and c == nch - 1 and not first:
                                        turn_out(g - 1, 1 - u)
                            over_groups(pe, step)
                            project(NG - 1, 1, nch - 2)
                            project(NG - 1, 1, nch - 1)
                            if last_pass:
                                turn_out(NG - 1, 1)

                    @blk.scalar
                    def _(act):
                        def combining(lo):
                            for g in range(NG):
                                act.wait_ge(cwt, lo + g + 1)
                                if lo and g == 0:
                                    act.wait_ge(hid, before[NP_ - 1] * NG)
                                act.copy(CW[:, g * GT:(g + 1) * GT], UB_[g % 2][:, 0:GT]).then_inc(cws, 1)

                        for n, chunks in enumerate(passes):
                            nch = len(chunks)
                            if not ternary and n == 0:
                                combining(0)
                            if not ternary and chunks[0][0] == "s":
                                combining(NG)
                            if n:
                                act.wait_ge(y_full, n * NG)
                            r = groups[n]
                            if chunks[0][0] == "e":
                                act.wait_ge(raw_in, raws[n + 1])
                                for k in range(KD):
                                    ins = act.copy(RDO[:, k, 0:nch * P].rearrange("p (c e j) -> p e c j", e=E, j=EJ),
                                                   RD[:, k, 0:nch * P].rearrange("p (e c j) -> p e c j", e=E, j=EJ))
                                ins.then_inc(ordered, 1)
                            for c in range(nch):
                                act.wait_ge(w_full, r + 1)
                                ins = act.copy(WH[:, c, :, :], (GB_ + UB_)[r % 4][:, :].rearrange("p (m u) -> p m u", m=2 * KD))
                                ins.then_inc(w_low if ternary else w_high, 1)
                                r += 1
                            for c in range(0, nch, 2):
                                act.wait_ge(w_full, r + 1)
                                ins = act.copy(DH[:, c:c + 2, :], (GB_ + UB_)[r % 4][:, :].rearrange("p (c d) -> p c d", c=2))
                                ins.then_inc(w_low if ternary else w_high, 1)
                                r += 1

                            def split_high(g, c, n=n):
                                i = chunk_no(n, g, c)
                                act.wait_ge(mid if ternary else hid, i + 1)
                                used(act, n, g, c, nch)
                                act.copy(HH[c % 2][:], HS[c % 2][:]).then_inc(h_high, 1)

                            def step(g, u, n=n):
                                first = isinstance(g, int) and g == 0
                                for c in range(nch):
                                    i = chunk_no(n, g, c)
                                    act.wait_ge(gu_full, i + 1)
                                    if not (isinstance(i, int) and i < 2):
                                        act.wait_ge(h_low, i - 1)
                                    act.activation(HS[c % 2][:], GB_[c % 2][:, 0:GT], ACT.Silu,
                                                   **({"scale": half_s[:, 3:4]} if ternary else {})).then_inc(silu, 1)
                                    if c:
                                        split_high(g, c - 1)
                                    elif not first:
                                        split_high(g - 1, nch - 1)
                            if ternary:
                                act.wait_ge(scales, 1)
                            over_groups(act, step)
                            split_high(NG - 1, nch - 1)

                    @blk.vector
                    def _(dve):
                        if ternary:
                            dve.wait_ge(raw_in, raws[1])
                            for m, raw in enumerate((RG, RU, RD)):
                                dve.tensor_reduce(part[:, m:m + 1], raw[:], AX.XY, ALU.add, apply_absolute_value=True).then_inc(sums3, 1)
                            dve.wait_ge(tot, 1)
                            n = 0

                            def link(ins):
                                nonlocal n
                                n += 1
                                ins.then_inc(links, 1)
                                dve.wait_ge(links, n)
                            link(dve.tensor_scalar(half_s[:, 3:6], YB[0][0][:, 0:3], 1.0 / (FI * D), TERNARY_EPS, ALU.mult, ALU.add))
                            link(dve.tensor_scalar(half_s[:, 6:9], half_s[:, 3:6], 0.5, None, ALU.mult))
                            link(dve.tensor_scalar(half_s[:, 9:12], half_s[:, 3:6], -0.5, None, ALU.mult))
                            link(dve.tensor_scalar(half_s[:, 0:1], half_s[:, 4:5], half_s[:, 5:6], gains[:, 3:4], ALU.mult, ALU.mult))
                            dve.tensor_scalar(half_s[:, 1:2], half_s[:, 0:1], 1.0, None, ALU.mult).then_inc(scales, 1)
                            for m, raw in enumerate((RG, RU, RD)):
                                flat = TM[:].rearrange("p c d -> p (c d)")
                                rf = raw[:].rearrange("p c d -> p (c d)")
                                link(dve.tensor_scalar(flat, rf, half_s[:, 9 + m:10 + m], None, ALU.is_lt))
                                dve.scalar_tensor_tensor(out=rf, in0=rf, scalar=half_s[:, 6 + m:7 + m], in1=flat,
                                                         op0=ALU.is_gt, op1=ALU.subtract).then_inc(tern, 1)
                                dve.wait_ge(tern, m + 1)
                        gain = half_s[:, 0:1] if ternary else gains[:, 2:3]

                        def combining(src, lo):
                            for g in range(NG):
                                if lo + g:
                                    dve.wait_ge(cwt, lo + g)
                                w = src(g)
                                dve.tensor_copy(CX[0:S, :, :].rearrange("p b (e j) -> p b e j", j=w[1]), w[0]).then_inc(wide, 1)

                        for n, chunks in enumerate(passes):
                            nch = len(chunks)
                            last_pass = n == NP_ - 1
                            if not ternary and n == 0:
                                combining(lambda g: (CWN[0:S, g * GB:(g + 1) * GB, :].rearrange("p b (e o) -> p b e o", o=1).to_broadcast([S, GB, E, EJ]), EJ), 0)
                            if not ternary and chunks[0][0] == "s":
                                combining(lambda g: (SIGN[0:S, g * GB:(g + 1) * GB].rearrange("p (b e o) -> p b e o", e=1, o=1).to_broadcast([S, GB, 1, P]), P), NG)
                            if not ternary:
                                r = groups[n]
                                for c in range(nch):
                                    dve.wait_ge(w_high, r + 1)
                                    dve.tensor_tensor(WL[:, c, :, :], (GB_ + UB_)[r % 4][:, :].rearrange("p (m u) -> p m u", m=2 * KD),
                                                      WH[:, c, :, :].bitcast(F32), ALU.subtract).then_inc(w_low, 1)
                                    r += 1
                                for c in range(0, nch, 2):
                                    dve.wait_ge(w_high, r + 1)
                                    dve.tensor_tensor(DL[:, c:c + 2, :], (GB_ + UB_)[r % 4][:, :].rearrange("p (c d) -> p c d", c=2),
                                                      DH[:, c:c + 2, :].bitcast(F32), ALU.subtract).then_inc(w_low, 1)
                                    r += 1

                            def split_low(g, c, n=n):
                                dve.wait_ge(h_high, chunk_no(n, g, c) + 1)
                                used(dve, n, g, c, nch)
                                dve.tensor_tensor(HL[c % 2][:], HS[c % 2][:], HH[c % 2][:].bitcast(F32), ALU.subtract).then_inc(h_low, 1)

                            def collect(g, u, n=n):
                                dve.wait_ge(y_full, n * NG + g + 1)
                                if last_pass:
                                    if not (isinstance(g, int) and g < (2 if ternary else 1)):
                                        dve.wait_ge(y_turned, g - 1 if ternary else g)
                                for k in range(KD):
                                    y = YB[u][k][:, 0:GT]
                                    if ternary:
                                        ins = dve.tensor_scalar(YF[u][:, k, :], y, 1.0, None, ALU.mult)
                                    elif n == 0:
                                        ins = dve.tensor_scalar(YT[:, k, cols(g, GT)], y, 1.0, None, ALU.mult)
                                    else:
                                        ins = dve.tensor_tensor(YF[u][:, k, :] if last_pass else YT[:, k, cols(g, GT)], y, YT[:, k, cols(g, GT)], ALU.add)
                                ins.then_inc(y_fin if last_pass else y_read, 1)

                            def update(g, u):
                                dve.wait_ge(y_turned, g + 1)
                                for i in range(GB):
                                    xb = XN[0:S, dsl(GB * g + i), :].rearrange("p a d -> p (a d)")
                                    dve.scalar_tensor_tensor(out=xb, in0=YB[u][i // 2][0:S, (i % 2) * D:(i % 2 + 1) * D], scalar=gain[0:S],
                                                             in1=xb, op0=ALU.mult, op1=ALU.add).then_inc(x_new, 1)

                            def step(g, u, n=n):
                                first = isinstance(g, int) and g == 0
                                for c in range(nch):
                                    dve.wait_ge(silu, chunk_no(n, g, c) + 1)
                                    dve.tensor_tensor(HS[c % 2][:], HS[c % 2][:], UB_[c % 2][:, 0:GT], ALU.mult).then_inc(mid, 1)
                                    if c:
                                        split_low(g, c - 1)
                                    elif not first:
                                        split_low(g - 1, nch - 1)
                                    if c == 2 and not first:
                                        collect(g - 1, 1 - u)
                                if last_pass and not first:
                                    update(g - 1, 1 - u)
                            over_groups(dve, step)
                            split_low(NG - 1, nch - 1)
                            collect(NG - 1, 1)
                            if last_pass:
                                update(NG - 1, 1)

        def inverse_deviation(pool, done):
            pool.tensor_tensor(RSTD[0:S, 0:HEAD], VEPS[0:S, 0:HEAD], MHALF[0:S, 0:HEAD], ALU.pow).then_inc(done, 1)
            pool.tensor_tensor(RSTD[0:S, HEAD:B], VEPS[0:S, HEAD:B], MHALF[0:S, HEAD:B], ALU.pow).then_inc(done, 1)

        def token_stats():
            with nc.sbuf_tensor("stats_again", [P, B, 6], F32) as stats:
                stat_done = sem("stat_again_done")
                with nc.Block() as blk:
                    @blk.vector
                    def _(dve):
                        for b in range(B):
                            last = dve.bn_stats(stats[0:S, b, :], XN[0:S, b, :])
                        last.then_inc(stat_done, 1)
                        dve.wait_ge(stat_done, 1)
                        for b in range(B):
                            dve.bn_aggr(MV[0:S, b, :], stats[0:S, b, :])

        def cols(n, width):
            return slice(n * width, (n + 1) * width) if isinstance(n, int) else bass.ds(n * width, width)

        def half(b, p):
            return b // 2 if isinstance(b, int) else halves(b, p)

        def halves(b, p):
            return (b - p) // 2

        def dcol(n):
            return slice(n, n + 1) if isinstance(n, int) else bass.ds(n, 1)

        def dsl(b):
            return slice(b, b + 1) if isinstance(b, int) else bass.ds(b, 1)

        def dyn(t, b):
            return t[b] if isinstance(b, int) else t[bass.ds(b, 1)].rearrange("a m d -> (a m) d")

        def dynrow(t, b):
            return t[dsl(b), :]


        setup()
        attention(0, picked=True)
        clear_attention_sems()
        attention(0, guard=any_long[0:1, 0:1])
        clear_attention_sems()
        picking.close()
        feed_forward(0)
        token_stats()
        attention(1)
        clear_attention_sems()
        find_redo()
        attention(1, guard=any_redo[0:1, 0:1])
        feed_forward(1)


_INS = ['x', 'ctx_2048', 'mask_BxS2_bk0', 'g_xattn', 'g_ffn', 'L0_ffn_gate_w', 'L0_ffn_expert_gate_up',
        'L0_ffn_expert_down', 'L0_ffn_shared_gate_up', 'L0_ffn_shared_down', 'L0_ffn_shared_gate_vec',
        'L1_xattn_W_qkv', 'L1_xattn_W_o', 'L1_xattn_beta_q', 'L1_xattn_beta_k', 'L1_xattn_gate',
        'L1_xattn_log_tau', 'L1_ffn_W_up', 'L1_ffn_W_gate', 'L1_ffn_W_down']


def kernel(**inputs):
    import numpy as _np
    import concourse.bacc as _bacc
    from concourse import mybir as _mybir
    from concourse.bass_utils import run_bass_kernel_spmd as _run

    nc = _bacc.Bacc("TRN2", target_bir_lowering=False, num_devices=1)
    arrays, args = {}, []
    for name in _INS:
        a = _np.ascontiguousarray(inputs[name])
        a = a.reshape(1) if a.ndim == 0 else a
        arrays[f"in_{name}_dram"] = a
        args.append(nc.dram_tensor(f"in_{name}_dram", a.shape, _mybir.dt.from_np(a.dtype), kind="ExternalInput").ap())
    args.append(nc.dram_tensor("out_0_dram", inputs['x'].shape, _mybir.dt.float32, kind="ExternalOutput").ap())
    flamingo_kernel(nc, *args)
    r = _run(nc, [arrays], core_ids=[0])
    return r.results[0]["out_0_dram"]
```
